# Optimizing a Trainium2 kernel written in Bass

```python
import numpy as np
import jax
import jax.numpy as jnp

def _softmax(x, axis=-1):
    return jax.nn.softmax(x, axis=axis)

def _gelu(x):
    return jax.nn.gelu(x, approximate=True)

def _silu(x):
    return jax.nn.silu(x)

def _sigmoid(x):
    return jax.nn.sigmoid(x)

def _layernorm(x, axis=-1, eps=1e-05):
    m = jnp.mean(x, axis=axis, keepdims=True)
    v = jnp.var(x, axis=axis, keepdims=True)
    return (x - m) / jnp.sqrt(v + eps)

def _scatter_add(tgt, idx, src, axis=0):
    return tgt.at[idx].add(src)

def _segment_sum(src, seg, n):
    return jax.ops.segment_sum(src, seg, n)
kernel_name = 'mk_adaln_d1_jaxref_r4_b2f533'

def setup_inputs(seed: int=0):
    np.random.seed(seed)
    _w = jnp.asarray

    def _L0_attn_setup():
        import jax, jax.numpy as jnp
        import numpy as np
        D_MODEL = 256
        NUM_HEADS = 16
        D_K = D_MODEL // NUM_HEADS
        THETA = 10000.0
        NEG_INF = -1000000000.0

        def _rope(x, positions):
            half = D_K // 2
            inv_freq = 1.0 / THETA ** (jnp.arange(0, D_K, 2, dtype=jnp.float32) / D_K)
            angles = positions.astype(jnp.float32)[:, None] * inv_freq
            cos, sin = (jnp.cos(angles), jnp.sin(angles))
            xe = x[..., 0::2]
            xo = x[..., 1::2]
            re = xe * cos - xo * sin
            ro = xe * sin + xo * cos
            return jnp.stack([re, ro], axis=-1).reshape(x.shape).astype(x.dtype)
        key = jax.random.key(seed)
        ks = jax.random.split(key, 5)
        sigma = np.sqrt(2.0 / (D_MODEL + D_MODEL))
        x = jax.random.normal(ks[0], (2, 512, D_MODEL), dtype=jnp.float32)
        mk = lambda k: (sigma * jax.random.normal(k, (D_MODEL, D_MODEL))).astype(jnp.float32)
        return {'x': x, 'Wq': mk(ks[1]), 'bq': jnp.zeros((D_MODEL,), jnp.float32), 'Wk': mk(ks[2]), 'bk': jnp.zeros((D_MODEL,), jnp.float32), 'Wv': mk(ks[3]), 'bv': jnp.zeros((D_MODEL,), jnp.float32), 'Wo': mk(ks[4]), 'bo': jnp.zeros((D_MODEL,), jnp.float32), 'token_positions': jnp.arange(512, dtype=jnp.int64) if jax.config.jax_enable_x64 else jnp.arange(512, dtype=jnp.int32)}
    _L0_attn_in = _L0_attn_setup()

    def _L0_ffn_setup():
        import jax, jax.numpy as jnp
        import numpy as np
        B, S, D = (4, 512, 256)
        E, F = (8, 1024)
        key = jax.random.key(seed)
        ks = jax.random.split(key, 5)
        x = jax.random.normal(ks[0], (B, S, D), dtype=jnp.float32)
        switch_w = jax.random.normal(ks[1], (D, E), dtype=jnp.float32) * D ** (-0.5)
        switch_b = jnp.zeros((E,), dtype=jnp.float32)
        w1 = jax.random.normal(ks[2], (E, D, F), dtype=jnp.float32) * D ** (-0.5)
        b1 = jnp.zeros((E, F), dtype=jnp.float32)
        w2 = jax.random.normal(ks[3], (E, F, D), dtype=jnp.float32) * F ** (-0.5)
        b2 = jnp.zeros((E, D), dtype=jnp.float32)
        return {'x': x, 'switch_w': switch_w, 'switch_b': switch_b, 'w1': w1, 'b1': b1, 'w2': w2, 'b2': b2}
    _L0_ffn_in = _L0_ffn_setup()
    _L0_c = _w((lambda *s: np.random.randn(*s).astype(np.float32) * 0.05)(8, 256))
    _L0_wmod = _w((lambda *s: np.random.randn(*s).astype(np.float32) * 0.05)(256, 6 * 256) * 256 ** (-0.5))
    _d = {'L0_attn_x': _L0_attn_in['x'], 'L0_attn_Wq': _L0_attn_in['Wq'], 'L0_attn_bq': _L0_attn_in['bq'], 'L0_attn_Wk': _L0_attn_in['Wk'], 'L0_attn_bk': _L0_attn_in['bk'], 'L0_attn_Wv': _L0_attn_in['Wv'], 'L0_attn_bv': _L0_attn_in['bv'], 'L0_attn_Wo': _L0_attn_in['Wo'], 'L0_attn_bo': _L0_attn_in['bo'], 'L0_attn_token_positions': _L0_attn_in['token_positions'], 'L0_ffn_switch_w': _L0_ffn_in['switch_w'], 'L0_ffn_switch_b': _L0_ffn_in['switch_b'], 'L0_ffn_w1': _L0_ffn_in['w1'], 'L0_ffn_b1': _L0_ffn_in['b1'], 'L0_ffn_w2': _L0_ffn_in['w2'], 'L0_ffn_b2': _L0_ffn_in['b2'], 'L0_c': _L0_c, 'L0_wmod': _L0_wmod}
    _x0 = _d['L0_attn_x']
    _d['L0_attn_x'] = jax.random.normal(jax.random.fold_in(jax.random.key(seed), 1), (8, 512, 256), dtype=_x0.dtype)
    del _x0
    return _d

def reference(L0_attn_x, L0_attn_Wq, L0_attn_bq, L0_attn_Wk, L0_attn_bk, L0_attn_Wv, L0_attn_bv, L0_attn_Wo, L0_attn_bo, L0_attn_token_positions, L0_ffn_switch_w, L0_ffn_switch_b, L0_ffn_w1, L0_ffn_b1, L0_ffn_w2, L0_ffn_b2, L0_c, L0_wmod):

    def _L0_attn_ref(x, Wq, bq, Wk, bk, Wv, bv, Wo, bo, token_positions):
        import jax, jax.numpy as jnp
        import numpy as np
        D_MODEL = 256
        NUM_HEADS = 16
        D_K = D_MODEL // NUM_HEADS
        THETA = 10000.0
        NEG_INF = -1000000000.0

        def _rope(x, positions):
            half = D_K // 2
            inv_freq = 1.0 / THETA ** (jnp.arange(0, D_K, 2, dtype=jnp.float32) / D_K)
            angles = positions.astype(jnp.float32)[:, None] * inv_freq
            cos, sin = (jnp.cos(angles), jnp.sin(angles))
            xe = x[..., 0::2]
            xo = x[..., 1::2]
            re = xe * cos - xo * sin
            ro = xe * sin + xo * cos
            return jnp.stack([re, ro], axis=-1).reshape(x.shape).astype(x.dtype)
        B, S, D = x.shape
        Q = x @ Wq.T + bq
        K = x @ Wk.T + bk
        V = x @ Wv.T + bv

        def split_heads(t):
            return t.reshape(B, S, NUM_HEADS, D_K).transpose(0, 2, 1, 3)
        Q, K, V = (split_heads(Q), split_heads(K), split_heads(V))
        pos = jnp.arange(S)
        Q = _rope(Q, pos)
        K = _rope(K, pos)
        scale = 1.0 / jnp.sqrt(jnp.float32(D_K))
        scores = jnp.einsum('bhqd,bhkd->bhqk', Q, K) * scale
        causal = jnp.tril(jnp.ones((S, S), dtype=bool))
        scores = jnp.where(causal, scores, NEG_INF)
        weights = jax.nn.softmax(scores, axis=-1)
        attn = jnp.einsum('bhqk,bhkd->bhqd', weights, V)
        concat = attn.transpose(0, 2, 1, 3).reshape(B, S, D)
        return concat @ Wo.T + bo

    def _L0_ffn_ref(x, switch_w, switch_b, w1, b1, w2, b2):
        import jax, jax.numpy as jnp
        import numpy as np
        B, S, D = (4, 512, 256)
        E, F = (8, 1024)
        b, s, d = x.shape
        t = x.reshape(-1, d)
        logits = t @ switch_w + switch_b
        route_prob = jax.nn.softmax(logits, axis=-1)
        route_prob_max = jnp.max(route_prob, axis=-1)
        routes = jnp.argmax(route_prob, axis=-1)
        out = jnp.zeros_like(t)
        n_experts = w1.shape[0]
        for e in range(n_experts):
            h = jax.nn.gelu(t @ w1[e] + b1[e])
            y = h @ w2[e] + b2[e]
            mask = (routes == e)[:, None]
            out = jnp.where(mask, y, out)
        out = out * route_prob_max[:, None]
        return out.reshape(b, s, d)
    x = L0_attn_x
    mod = (_silu(L0_c) @ L0_wmod).reshape(L0_c.shape[0], 6, 1, -1)
    sa, ca, ga, sb, cb, gb = (mod[:, 0], mod[:, 1], mod[:, 2], mod[:, 3], mod[:, 4], mod[:, 5])
    ga = (2 * (ga >= 0) - 1) * jnp.maximum(jnp.abs(ga), 0.25)
    gb = (2 * (gb >= 0) - 1) * jnp.maximum(jnp.abs(gb), 0.25)
    h = _layernorm(x, axis=-1) * (1 + ca) + sa
    x = x + ga * _L0_attn_ref(h, L0_attn_Wq, L0_attn_bq, L0_attn_Wk, L0_attn_bk, L0_attn_Wv, L0_attn_bv, L0_attn_Wo, L0_attn_bo, L0_attn_token_positions)
    h = _layernorm(x, axis=-1) * (1 + cb) + sb
    x = x + gb * _L0_ffn_ref(h, L0_ffn_switch_w, L0_ffn_switch_b, L0_ffn_w1, L0_ffn_b1, L0_ffn_w2, L0_ffn_b2)
    return x

_drawn_inputs = setup_inputs


def setup_inputs(seed=0):
    import zlib

    import numpy as np

    out = dict(_drawn_inputs(seed))
    spreads = {'L0_attn_bq': (0.0, 0.8),
     'L0_attn_bk': (0.0, 2.0),
     'L0_attn_bv': (0.0, 0.314),
     'L0_attn_bo': (0.0, 0.313),
     'L0_ffn_switch_b': (0.0, 0.426),
     'L0_ffn_b1': (0.0, 0.8),
     'L0_ffn_b2': (0.0, 0.8)}
    factors = {}
    for name, (base, spread) in spreads.items():
        noise = np.random.default_rng([zlib.crc32(name.encode()), seed]).standard_normal(out[name].shape)
        drawn = base * np.exp(spread * noise) if base else spread * noise
        out[name] = jnp.asarray(drawn.astype(out[name].dtype))
    for name, factor in factors.items():
        out[name] = (out[name] * factor).astype(out[name].dtype)
    return out
```

```python
import concourse.bass as bass
from concourse import mybir
from contextlib import ExitStack
from math import prod

F32 = mybir.dt.float32
F16 = mybir.dt.float16
BF16 = mybir.dt.bfloat16
I32 = mybir.dt.int32
ALU = mybir.AluOpType
ACT = mybir.ActivationFunctionType
AX = mybir.AxisListType

B, S, D = 8, 512, 256
H = 16
DK = D // H
P = 128
QT = S // P
NT = B * QT
KC = D // P
E, F = 8, 1024
NSLOT_T = NT + E
W_SCALE = 64.0
HG = 4
G = H // HG
NU = B * G
HW = 64
NEG = -1.0e30
SCALE = 1.0 / DK ** 0.5
LN_EPS = 1e-5
ADA_MIN = 0.25
LEAD = 5

def shots(length):
    out = []
    for blk in range(QT):
        n = min(2, S // length(blk)) if length(blk) * 2 <= S else 1
        for first in range(0, 2, n):
            for j in range(2):
                out.append((blk, first, n, j))
    return out


MAX_SHOTS = shots(lambda qt: P * (qt + 1))
EXP_SHOTS = shots(lambda kb: S - P * kb)
NSHOT = len(MAX_SHOTS)
EXP_UPTO = [1 + max(i for i, s in enumerate(EXP_SHOTS) if s[0] == kb) for kb in range(QT)]
P_AT = [HG * sum(S - P * k for k in range(kb)) for kb in range(QT + 1)]


def ge(eng, sem, count):
    if isinstance(count, int) and count <= 0:
        return
    eng.wait_ge(sem, count)


def build(nc, x, wq, bq, wk, bk, wv, bv, wo, bo, switch_w, switch_b, w1, b1, w2, b2, c, wmod,
          rope_cos, rope_sin, out):
    with ExitStack() as whole:
        sems = {}

        def sem(name):
            if name not in sems:
                sems[name] = whole.enter_context(nc.semaphore(name))
            return sems[name]

        x1_dram = nc.dram_tensor("x1_dram", [B * S, D], F32, kind="Internal").ap()
        xs_dram = nc.dram_tensor("xs_dram", [NSLOT_T * P, 2 * D], F16, kind="Internal").ap()
        ys_dram = nc.dram_tensor("ys_dram", [(NSLOT_T - 1) * P, D], F32, kind="Internal").ap()

        def sb(name, shape, dt=F32):
            return whole.enter_context(nc.sbuf_tensor(name, shape, dt))

        logits = sb("logits", [P, NT, E])
        mod_t = sb("mod_t", [P, 6 * KC, B])
        gate_b = sb("gate_b", [P, B, D])
        ident = sb("ident", [P, P])
        ident16 = sb("ident16", [P, P], F16)
        attention_part(nc, sem, x, wq, bq, wk, bk, wv, bv, wo, bo, c, wmod, rope_cos, rope_sin,
                       x1_dram, mod_t, gate_b, ident, ident16)
        w1_hi, w1_lo = (sb(n, [P, E, KC, F], F16) for n in ("w1_hi", "w1_lo"))
        w2_hi, w2_lo = (sb(n, [P, E, F // P, D], F16) for n in ("w2_hi", "w2_lo"))
        b1_t = sb("b1_t", [P, E, F // P])
        b2_parts = sb("b2_parts", [3, E * D], BF16)
        slot = sb("slot", [P, NT], I32)
        gate_p = sb("gate_p", [P, NT])
        tile_e = sb("tile_e", [P, NSLOT_T], I32)
        route_part(nc, sem, x1_dram, xs_dram, w1, b1, w2, b2, switch_w, switch_b, logits, mod_t, ident,
                   w1_hi, w1_lo, w2_hi, w2_lo, b1_t, b2_parts, slot, gate_p, tile_e)
        expert_part(nc, sem, x1_dram, xs_dram, ys_dram, gate_b, ident16, w1_hi, w1_lo, w2_hi, w2_lo, b1_t,
                    b2_parts, slot, gate_p, tile_e, out)


def attention_part(nc, sem, x, wq, bq, wk, bk, wv, bv, wo, bo, c, wmod, rope_cos, rope_sin,
                   x1_dram, mod_t, gate_b, ident, ident16):
    with ExitStack() as ctx:
        def sb(name, shape, dt=F32):
            return ctx.enter_context(nc.sbuf_tensor(name, shape, dt))

        def bank(name):
            return ctx.enter_context(nc.psum_tensor(name, [P, 512], F32))

        xs = sb("xs", [P, 2, QT, D])
        xr = sb("xr", [P, 2, QT, D])
        bn = sb("bn", [P, 2, 6])
        mean_var = sb("mean_var", [P, 2, 2])
        rstd = sb("rstd", [P, 2, 1])
        var_eps = sb("var_eps", [P, 1])
        neg_half = sb("neg_half", [P, 1])
        xhat = sb("xhat", [P, D])
        h_t = sb("h_t", [P, KC, P])
        rot_a = sb("rot_a", [P, 2 * D])
        rot_b = sb("rot_b", [P, 2 * D])
        rot = sb("rot", [P, 2 * D])
        q_aug = sb("q_aug", [P, 2, QT, H * HW], F16)
        k_aug = sb("k_aug", [P, H * HW], F16)
        q_t = sb("q_t", [P, 2, H // 2, S], F16)
        k_t = sb("k_t", [P, 2, H // 2, S], F16)
        v_sb = sb("v_sb", [P, 2, QT, H, 32])
        prob = sb("prob", [P, 2, P_AT[QT]])
        row_max = sb("row_max", [P, 2, QT, HG])
        u_sb = sb("u_sb", [P, 2, S])
        recip = sb("recip", [P, S])
        att_t = sb("att_t", [P, 2, G, S])
        gated = sb("gated", [P, 2, D])
        w_qkv = sb("w_qkv", [P, KC, 3 * D])
        w_o = sb("w_o", [P, G, D])
        gate_a = sb("gate_a", [P, B, D])
        cos_t = sb("cos_t", [P, QT, DK])
        sin_t = sb("sin_t", [P, QT, DK])
        bias3 = sb("bias3", [3, 3 * D], BF16)
        ones3 = sb("ones3", [3, P], BF16)
        ident_b = sb("ident_b", [P, P], BF16)
        causal = sb("causal", [P, 2, P], BF16)
        denom_sel = sb("denom_sel", [P, P])
        ps_a, ps_b = bank("ps_a"), bank("ps_b")
        ps_max = [bank("ps_max0"), bank("ps_max1")]
        ps_sc = [bank("ps_sc0"), bank("ps_sc1")]
        ps_pv, ps_nd = bank("ps_pv"), bank("ps_nd")

        nat = prob[:, 0, 0:3 * KC * D].rearrange("p (w c i) -> p w c i", w=3, c=KC)
        nat_o = prob[:, 1, 0:KC * H * 32].rearrange("p (c h d) -> p c h d", c=KC, h=H)
        wmod_sb = prob[:, 0, 1536:1536 + KC * 6 * D].rearrange("p (c n) -> p c n", c=KC)
        c_sb = prob[0:B, 1, 1024:1024 + D]
        c_exp = prob[0:B, 1, 1280:1280 + D]
        c_silu = prob[0:B, 1, 1536:1536 + D]
        c_t = prob[:, 1, 1792:1792 + KC * B].rearrange("p (c b) -> p c b", c=KC)
        mod_r = prob[0:B, 1, 2048:2048 + 2 * D].rearrange("p (g d) -> p g d", g=2)
        mod_s = prob[0:B, 1, 2560:2560 + 2 * D].rearrange("p (g d) -> p g d", g=2)
        mod_m = prob[0:B, 1, 3072:3072 + 2 * D].rearrange("p (g d) -> p g d", g=2)
        row_sel = prob[0:B, 1, 3584:3584 + B * P].rearrange("p (b m) -> p b m", b=B)
        bias_f = u_sb[0:1, :, :].rearrange("p a s -> p (a s)")[:, 0:3 * D]
        bias_r = rot_a[0:1, :], rot_b[0:1, :]
        bias_parts = att_t[0:1, 1, :, :].rearrange("p g s -> p (g s)")[:, 0:9 * D // 2].bitcast(BF16)

        x_v = x.rearrange("b (t p) d -> b p t d", p=P)
        x1_v = x1_dram.rearrange("(b t p) d -> b p t d", t=QT, p=P)

        xs_loaded = [sem("xs_loaded0"), sem("xs_loaded1")]
        xr_loaded = [sem("xr_loaded0"), sem("xr_loaded1")]
        x1_stored = [sem("x1_stored0"), sem("x1_stored1")]
        w_loaded, mod_loaded, small_loaded = sem("w_loaded"), sem("mod_loaded"), sem("small_loaded")
        bias_spread = sem("bias_spread")
        masks_done, zeros_done = sem("masks_done"), sem("zeros_done")
        setup_ps, setup_ev, setup_act, setup_dve, setup_ev2 = (sem("setup_ps"), sem("setup_ev"), sem("setup_act"),
                                                    sem("setup_dve"), sem("setup_ev2"))
        stats_done, rstd_done, xhat_done = sem("stats_done"), sem("rstd_done"), sem("xhat_done")
        mv_done, var_done = sem("mv_done"), sem("var_done")
        xt_ps, ht_done, qkv_ps = sem("xt_ps"), sem("ht_done"), sem("qkv_ps")
        rope_done, rot_done, hi_done, lo_done = (sem("rope_done"), sem("rot_done"), sem("hi_done"),
                                                 sem("lo_done"))
        v_kept, aug_ps, qt_kept, kt_kept = sem("v_kept"), sem("aug_ps"), sem("qt_kept"), sem("kt_kept")
        max_ps, max_done, negmax_done = sem("max_ps"), sem("max_done"), sem("negmax_done")
        shift_ps, shift_kept = sem("shift_ps"), sem("shift_kept")
        sc_ps, exp_done, masked = sem("sc_ps"), sem("exp_done"), sem("masked")
        pv_ps, u_kept, den_ps = sem("pv_ps"), sem("u_kept"), sem("den_ps")
        recip_done, att_done = sem("recip_done"), sem("att_done")
        dve_turns, pool_turns = sem("dve_turns"), sem("pool_turns")
        o_ps, gated_done, x1_done = sem("o_ps"), sem("gated_done"), sem("x1_done")

        block = ctx.enter_context(nc.Block())

        PAIR = 2 * G

        def all_units(eng, unit):
            with eng.Fori(0, B // 2 - 1) as i:
                for u in range(PAIR):
                    unit(i, u)
            for u in range(PAIR):
                unit(B // 2 - 1, u)

        def batch_of(i, n):
            return 2 * i + n // 4, (n // 4) % 2, n % 4

        def in_range(i, n):
            return not isinstance(i, int) or PAIR * i + n < NU

        @block.sync
        def _(sp):
            for n, w in enumerate((wq, wk, wv)):
                sp.dma_start(nat[:, n, :, :], w.rearrange("(c p) i -> p c i", p=P)).then_inc(w_loaded, 16)
            sp.dma_start(c_sb, c).then_inc(mod_loaded, 16)
            sp.dma_start(wmod_sb, wmod.rearrange("(c p) n -> p c n", p=P)).then_inc(mod_loaded, 16)
            for n, b_ in enumerate((bq, bk, bv)):
                sp.dma_start(bias_f[:, n * D:(n + 1) * D], b_.rearrange("(a n) -> a n", a=1)).then_inc(small_loaded, 16)
            sp.dma_start(cos_t[:, :, :], rope_cos.rearrange("(t p) d -> p t d", p=P)).then_inc(small_loaded, 16)
            sp.dma_start(sin_t[:, :, :], rope_sin.rearrange("(t p) d -> p t d", p=P)).then_inc(small_loaded, 16)
            sp.wait_ge(zeros_done, 1)
            for cc in range(KC):
                sp.dma_start(nat_o[:, cc, :, 0:DK], wo[cc * P:(cc + 1) * P, :].rearrange("p (h d) -> p h d", h=H)).then_inc(w_loaded, 16)
                sp.dma_start(nat_o[:, cc, 0, DK:DK + 1], bo[cc * P:(cc + 1) * P].rearrange("(p a) -> p a", a=1)).then_inc(w_loaded, 16)
            for b in range(2):
                sp.dma_start(xs[:, b, :, :], x_v[b]).then_inc(xs_loaded[b], 16)
                sp.dma_start(xr[:, b, :, :], x_v[b]).then_inc(xr_loaded[b], 16)
            sp.wait_ge(setup_dve, 5)
            for n in range(3):
                sp.dma_start(bias3[n:n + 1, :], bias_parts[:, n * 3 * D:(n + 1) * 3 * D]).then_inc(bias_spread, 16)
            with sp.Fori(1, B // 2) as k:
                for half in range(2):
                    b = 2 * k + half
                    sp.wait_ge(xhat_done, 4 * (b - 1))
                    sp.dma_start(xs[:, half, :, :], x_v[b]).then_inc(xs_loaded[half], 16)
                    sp.wait_ge(x1_done, 2 * (b - 1))
                    sp.dma_start(x1_v[b - 2], xr[:, half, :, :]).then_inc(x1_stored[half], 16)
                    sp.wait_ge(x1_stored[half], 16 * k)
                    sp.dma_start(xr[:, half, :, :], x_v[b]).then_inc(xr_loaded[half], 16)
            for half in range(2):
                b = B - 2 + half
                sp.wait_ge(x1_done, 2 * (b + 1))
                sp.dma_start(x1_v[b], xr[:, half, :, :]).then_inc(x1_stored[half], 16)
            for half in range(2):
                sp.wait_ge(x1_stored[half], 16 * (B // 2))

        @block.gpsimd
        def _(pool):
            nc.gpsimd.memset(nat_o, 0.0).then_inc(zeros_done, 1)
            nc.gpsimd.memset(ident[:, :], 0.0).then_inc(masks_done, 1)
            nc.gpsimd.memset(ident16[:, :], 0.0).then_inc(masks_done, 1)
            nc.gpsimd.memset(ident_b[:, :], 0.0).then_inc(masks_done, 1)
            nc.gpsimd.memset(causal[:, :, :], 0.0).then_inc(masks_done, 1)
            nc.gpsimd.memset(denom_sel[:, :], 0.0).then_inc(masks_done, 1)
            nc.gpsimd.memset(ones3[:, :], 1.0).then_inc(masks_done, 1)
            nc.gpsimd.memset(neg_half[:, :], -0.5).then_inc(masks_done, 1)
            nc.gpsimd.memset(q_aug[:, :, :, :], 0.0).then_inc(masks_done, 1)
            nc.gpsimd.memset(k_aug[:, :], 0.0).then_inc(masks_done, 1)
            nc.gpsimd.memset(v_sb[:, :, :, :, :], 0.0).then_inc(masks_done, 1)
            pool.wait_ge(masks_done, 10)
            for m in (ident, ident16, ident_b):
                nc.gpsimd.affine_select(out=m[:, :], in_=m[:, :], compare_op=ALU.not_equal, fill=1.0, base=0,
                                        pattern=[[-1, P]], channel_multiplier=1).then_inc(masks_done, 1)
            nc.gpsimd.affine_select(out=causal[:, :, :], in_=causal[:, :, :], compare_op=ALU.is_ge, fill=NEG, base=0,
                                    pattern=[[0, 2], [-1, P]], channel_multiplier=1).then_inc(masks_done, 1)
            nc.gpsimd.affine_select(out=denom_sel[:, :].rearrange("p (q m) -> p q m", m=32),
                                    in_=denom_sel[:, :].rearrange("p (q m) -> p q m", m=32),
                                    compare_op=ALU.not_equal, fill=1.0, base=-DK,
                                    pattern=[[-32, P // 32], [0, 32]], channel_multiplier=1).then_inc(masks_done, 1)
            nc.gpsimd.memset(k_aug[:, :].rearrange("p (h w) -> p h w", w=HW)[:, :, 3 * DK:3 * DK + 1], 1.0).then_inc(masks_done, 1)
            nc.gpsimd.memset(v_sb[:, :, :, :, DK:DK + 1].rearrange("p a t h o -> p (a t) h o"), 1.0).then_inc(masks_done, 1)

            def rstd_of(T):
                pool.wait_ge(var_done, T + 1)
                nc.gpsimd.tensor_tensor(rstd[:, 0, :], var_eps[:, :], neg_half[:, :], ALU.pow).then_inc(rstd_done, 1)

            def rotate(T):
                pool.wait_ge(rope_done, 3 * T + 3)
                ge(pool, hi_done, 2 * T)
                ge(pool, lo_done, 2 * T)
                nc.gpsimd.tensor_tensor(rot[:, :], rot_a[:, :], rot_b[:, :], ALU.add).then_inc(rot_done, 1)

            for T in range(LEAD):
                rstd_of(T)
                rotate(T)

            def unit(i, u):
                U, T = PAIR * i + u, PAIR * i + u + LEAD
                half = u % 2
                if in_range(i, u + LEAD):
                    rstd_of(T)
                for kb in range(QT):
                    if kb == QT - 1 and in_range(i, u + LEAD):
                        rotate(T)
                    pool.wait_ge(exp_done, NSHOT * U + EXP_UPTO[kb])
                    pool.sem_inc(pool_turns, 1)
                    diag = prob[:, half, P_AT[kb]:P_AT[kb + 1]].rearrange("p (h q) -> p h q", h=HG)[:, :, 0:P]
                    nc.gpsimd.affine_select(out=diag, in_=diag, compare_op=ALU.is_ge, fill=0.0, base=0,
                                            pattern=[[0, HG], [1, P]], channel_multiplier=-1).then_inc(masked, 1)

            all_units(pool, unit)

        @block.tensor
        def _(pe):
            mm = nc.tensor.matmul
            pe.wait_ge(masks_done, 17)
            pe.wait_ge(w_loaded, 16 * (3 + 2 * KC))
            step = [0]

            def evacuated():
                step[0] += 1
                ge(pe, setup_ev, step[0] - 1)

            for w in range(3):
                evacuated()
                for ic in range(KC):
                    for oc in range(KC):
                        last = nc.tensor.transpose(ps_a[:, (ic * KC + oc) * P:(ic * KC + oc + 1) * P],
                                                   nat[:, w, oc, ic * P:(ic + 1) * P], ident[:, :])
                last.then_inc(setup_ps, 1)
            for g0 in range(0, G, 2):
                evacuated()
                for g in range(g0, g0 + 2):
                    for oc in range(KC):
                        last = nc.tensor.transpose(ps_a[:, ((g - g0) * KC + oc) * P:((g - g0) * KC + oc + 1) * P],
                                                   nat_o[:, oc, HG * g:HG * (g + 1), :].rearrange("p h d -> p (h d)"),
                                                   ident[:, :])
                last.then_inc(setup_ps, 1)
            pe.wait_ge(setup_dve, 2)
            evacuated()
            for k in range(KC):
                last = nc.tensor.transpose(ps_a[:, k * B:(k + 1) * B], c_silu[:, k * P:(k + 1) * P], ident[0:B, 0:B])
            last.then_inc(setup_ps, 1)
            evacuated()
            for n in range(6 * KC):
                for k in range(KC):
                    last = mm(ps_a[:, n * B:(n + 1) * B], wmod_sb[:, k, n * P:(n + 1) * P], c_t[:, k, :],
                              start=(n == 0 and k == 0), stop=(k == KC - 1), skip_group_check=True)
            last.then_inc(setup_ps, 1)
            evacuated()
            for n, part in enumerate((2, 5)):
                for k in range(KC):
                    last = mm(ps_a[0:B, n * D:(n + 1) * D], c_t[:, k, :], wmod_sb[:, k, part * D:(part + 1) * D],
                              start=(n == 0 and k == 0), stop=(k == KC - 1), skip_group_check=True)
            last.then_inc(setup_ps, 1)
            pe.wait_ge(setup_dve, 9)
            for b in range(B):
                evacuated()
                last = mm(ps_a[:, :], row_sel[:, b, :], mod_r.rearrange("p g d -> p (g d)"), start=True, stop=True)
                last.then_inc(setup_ps, 1)
            pe.wait_ge(setup_ev, step[0])
            pe.wait_ge(bias_spread, 48)

            def x_transposes(T):
                pe.wait_ge(xhat_done, T + 1)
                ge(pe, kt_kept, T)
                for k in range(KC):
                    last = nc.tensor.transpose(ps_a[:, k * P:(k + 1) * P], xhat[:, k * P:(k + 1) * P], ident[:, :])
                last.then_inc(xt_ps, 1)

            def qkv(T):
                pe.wait_ge(ht_done, KC * T + KC)
                ge(pe, qt_kept, T)
                for bank_, a, n in ((ps_b, 0, 2 * D), (ps_a, 2 * D, D)):
                    mm(bank_[:, 0:n], ones3[:, :], bias3[:, a:a + n], start=True, stop=False)
                    for k in range(KC):
                        last = mm(bank_[:, 0:n], h_t[:, k, :], w_qkv[:, k, a:a + n], start=False, stop=(k == KC - 1))
                last.then_inc(qkv_ps, 1)

            def aug_transposes(T, par, t):
                pe.wait_ge(hi_done, 2 * T + 2)
                pe.wait_ge(lo_done, 2 * T + 2)
                for m in range(H // 2):
                    last = nc.tensor.transpose(ps_b[:, :].bitcast(F16)[:, m * P:(m + 1) * P],
                                               q_aug[:, par, t, m * P:(m + 1) * P], ident16[:, :])
                last.then_inc(aug_ps, 1)
                pe.wait_ge(v_kept, T + 1)
                for m in range(H // 2):
                    last = nc.tensor.transpose(ps_a[:, :].bitcast(F16)[:, m * P:(m + 1) * P],
                                               k_aug[:, m * P:(m + 1) * P], ident16[:, :])
                last.then_inc(aug_ps, 1)

            def max_scores(V, par, g, s):
                qt, first, n, j = MAX_SHOTS[s]
                L = P * (qt + 1)
                lo = HW * j
                if s == 0:
                    if g == 0:
                        pe.wait_ge(qt_kept, V + 4)
                        pe.wait_ge(kt_kept, V + 4)
                    ge(pe, shift_kept, V)
                ge(pe, max_done, NSHOT * V + s - 1)
                for m in range(n):
                    mm(ps_max[j][:, m * L:(m + 1) * L], q_t[lo:lo + 3 * DK, par, 2 * g + first + m, qt * P:(qt + 1) * P],
                       k_t[lo:lo + 3 * DK, par, 2 * g + first + m, 0:L], start=(m == 0), stop=False,
                       skip_group_check=True)
                o = ps_max[j][:, 0:n * L].rearrange("p (m l) -> p m l", m=n)[:, :, L - P:L]
                mm(o, ident_b[:, :], causal[:, 0:n, :], start=False, stop=True,
                   skip_group_check=True).then_inc(max_ps, 1)

            def shift_rows(V, par, g):
                pe.wait_ge(negmax_done, V + 1)
                for m in range(2):
                    for qt in range(QT):
                        at = (m * QT + qt) * P
                        last = nc.tensor.transpose(ps_max[0][:, :].bitcast(F16)[:, at:at + P],
                                                   q_aug[:, par, qt, (2 * g + m) * P:(2 * g + m + 1) * P],
                                                   ident16[:, :])
                last.then_inc(shift_ps, 1)

            def scores(U, par, g, s):
                kb, first, n, j = EXP_SHOTS[s]
                L = S - P * kb
                lo = HW * j
                if s == 0:
                    pe.wait_ge(shift_kept, U + 1)
                if s >= 2:
                    pe.wait_ge(exp_done, NSHOT * U + s - 1)
                for m in range(n):
                    last = mm(ps_sc[j][:, m * L:(m + 1) * L], k_t[lo:lo + 3 * DK + 1, par, 2 * g + first + m, kb * P:(kb + 1) * P],
                              q_t[lo:lo + 3 * DK + 1, par, 2 * g + first + m, kb * P:S], start=(m == 0), stop=(m == n - 1),
                              skip_group_check=True)
                last.then_inc(sc_ps, 1)

            def weigh(U, half, par, g, kb):
                pe.wait_ge(masked, QT * U + kb + 1)
                L = S - P * kb
                p_kb = prob[:, half, P_AT[kb]:P_AT[kb + 1]].rearrange("p (j m q) -> p j m q", j=2, m=2)
                for m in range(2):
                    for j in range(2):
                        col = 2 * m + j
                        last = mm(ps_pv[32 * col:32 * col + 32, kb * P:S], v_sb[:, par, kb, HG * g + col, :],
                                  p_kb[:, j, m, :], start=(kb == 0), stop=(kb == QT - 1), skip_group_check=True)
                if kb == QT - 1:
                    last.then_inc(pv_ps, 1)

            def denominators(U, half, wait_at):
                pe.wait_ge(u_kept, U + 1)
                if wait_at:
                    pe.wait_ge(recip_done, U)
                mm(ps_nd[:, :], denom_sel[:, :], u_sb[:, half, :], start=True, stop=True).then_inc(den_ps, 1)

            def project_out(b, par):
                pe.wait_ge(att_done, G * b + G)
                for two in range(2):
                    if two:
                        pe.wait_ge(gated_done, 2 * b + 1)
                    for t in range(2):
                        for g in range(G):
                            at = (2 * two + t) * P
                            last = mm(ps_nd[:, t * D:(t + 1) * D], att_t[:, par, g, at:at + P], w_o[:, g, :],
                                      start=(t == 0 and g == 0), stop=(g == G - 1), skip_group_check=True)
                    last.then_inc(o_ps, 1)

            for T in range(LEAD):
                x_transposes(T)
                qkv(T)
                aug_transposes(T, (T // 4) % 2, T % 4)
            for s in range(NSHOT):
                max_scores(0, 0, 0, s)
            shift_rows(0, 0, 0)

            def unit(i, u):
                U = PAIR * i + u
                b, par, g = batch_of(i, u)
                _, par_t, t = batch_of(i, u + LEAD)
                _, par_v, g_v = batch_of(i, u + 1)
                has_t, has_v = in_range(i, u + LEAD), in_range(i, u + 1)
                T, V = U + LEAD, U + 1
                if has_t:
                    x_transposes(T)
                for s in range(NSHOT):
                    scores(U, par, g, s)
                    if has_v:
                        max_scores(V, par_v, g_v, s)
                    if s == 7:
                        weigh(U, u % 2, par, g, 0)
                    if s == 9:
                        weigh(U, u % 2, par, g, 1)
                        if has_t:
                            qkv(T)
                weigh(U, u % 2, par, g, 2)
                weigh(U, u % 2, par, g, 3)
                if has_v:
                    shift_rows(V, par_v, g_v)
                if has_t:
                    aug_transposes(T, par_t, t)
                denominators(U, u % 2, not has_v)
                if g == G - 1:
                    project_out(b, par)

            all_units(pe, unit)

        @block.scalar
        def _(act):
            act.wait_ge(mod_loaded, 32)
            nc.scalar.activation(c_exp, c_sb, ACT.Exp, scale=-1.0).then_inc(setup_act, 1)

            def keep_v(T, par, t, after_unit):
                act.wait_ge(qkv_ps, T + 1)
                if after_unit is not None:
                    act.wait_ge(pv_ps, after_unit + 1)
                nc.scalar.activation(v_sb[:, par, t, :, 0:DK], ps_a[:, 0:D].rearrange("p (h d) -> p h d", h=H),
                                     ACT.Copy).then_inc(v_kept, 1)

            def hi_parts(T, par, t):
                act.wait_ge(rot_done, T + 1)
                r = rot[:, :].rearrange("p (w h d) -> p w h d", w=2, h=H)
                q_v = q_aug[:, par, t, :].rearrange("p (h w) -> p h w", w=HW)[:, :, 0:4 * DK]
                q_v = q_v.rearrange("p h (a d) -> p h a d", d=2 * DK)[:, :, :, 0:DK]
                k_v = k_aug[:, :].rearrange("p (h w) -> p h w", w=HW)[:, :, 0:2 * DK].rearrange("p h (a d) -> p h a d", a=2)
                for w, v in ((0, q_v), (1, k_v)):
                    nc.scalar.activation(v, r[:, w, :, None, :].to_broadcast([P, H, 2, DK]), ACT.Copy).then_inc(hi_done, 1)

            def keep_kt(T, par, t):
                act.wait_ge(aug_ps, 2 * T + 2)
                nc.scalar.activation(k_t[:, par, :, t * P:(t + 1) * P],
                                     ps_a[:, :].bitcast(F16).rearrange("p (m q) -> p m q", q=P), ACT.Copy).then_inc(kt_kept, 1)

            def keep_shift(V, par, g):
                act.wait_ge(shift_ps, V + 1)
                nc.scalar.activation(q_t[:, par, 2 * g:2 * g + 2, :],
                                     ps_max[0][:, :].bitcast(F16).rearrange("p (m q) -> p m q", m=2), ACT.Copy).then_inc(shift_kept, 1)

            def exps(U, half, s):
                kb, first, n, j = EXP_SHOTS[s]
                L = S - P * kb
                act.wait_ge(sc_ps, NSHOT * U + s + 1)
                a = P_AT[kb] + (2 * j + first) * L
                nc.scalar.activation(prob[:, half, a:a + n * L], ps_sc[j][:, 0:n * L], ACT.Exp,
                                     scale=SCALE).then_inc(exp_done, 1)

            def keep_u(U, half):
                act.wait_ge(pv_ps, U + 1)
                nc.scalar.activation(u_sb[:, half, :], ps_pv[:, :], ACT.Copy).then_inc(u_kept, 1)

            for T in range(LEAD):
                keep_v(T, (T // 4) % 2, T % 4, None)
                hi_parts(T, (T // 4) % 2, T % 4)
                keep_kt(T, (T // 4) % 2, T % 4)
            keep_shift(0, 0, 0)

            def unit(i, u):
                U = PAIR * i + u
                b, par, g = batch_of(i, u)
                _, par_t, t = batch_of(i, u + LEAD)
                _, par_v, g_v = batch_of(i, u + 1)
                has_t, has_v = in_range(i, u + LEAD), in_range(i, u + 1)
                for s in range(NSHOT):
                    exps(U, u % 2, s)
                if has_t and g != G - 1:
                    keep_v(U + LEAD, par_t, t, None)
                if has_t:
                    hi_parts(U + LEAD, par_t, t)
                keep_u(U, u % 2)
                if has_v:
                    keep_shift(U + 1, par_v, g_v)
                if has_t:
                    if g == G - 1:
                        keep_v(U + LEAD, par_t, t, U)
                    keep_kt(U + LEAD, par_t, t)

            all_units(act, unit)

        @block.vector
        def _(dve):
            dve.wait_ge(small_loaded, 80)
            bias_hi, bias_mid, bias_lo = (bias_parts[:, n * 3 * D:(n + 1) * 3 * D] for n in range(3))

            rest1 = att_t[0:1, 0, 0:2, :].rearrange("p g s -> p (g s)")[:, 0:3 * D]
            rest2 = att_t[0:1, 0, 2:4, :].rearrange("p g s -> p (g s)")[:, 0:3 * D]
            done = [0]

            def link(ins):
                done[0] += 1
                ins.then_inc(setup_dve, 1)
                dve.wait_ge(setup_dve, done[0])

            dve.wait_ge(setup_act, 1)
            one_plus = mod_s[:, 0, :]
            link(nc.vector.tensor_scalar(c_exp, c_exp, 1.0, None, ALU.add))
            nc.vector.reciprocal(one_plus, c_exp).then_inc(setup_ev2, 1)
            dve.wait_ge(setup_ev2, 1)
            link(nc.vector.tensor_tensor(c_silu, c_sb, one_plus, ALU.mult))
            link(nc.vector.tensor_copy(bias_hi, bias_f))
            link(nc.vector.tensor_tensor(rest1, bias_f, bias_hi, ALU.subtract))
            nc.vector.tensor_copy(bias_mid, rest1).then_inc(setup_ev2, 1)
            dve.wait_ge(setup_ev2, 2)
            nc.vector.tensor_tensor(rest2, rest1, bias_mid, ALU.subtract).then_inc(setup_ev2, 1)
            dve.wait_ge(setup_ev2, 3)
            link(nc.vector.tensor_copy(bias_lo, rest2))

            kept = [0]

            def keep(dst, src):
                nc.vector.tensor_copy(dst, src).then_inc(setup_ev, 1)

            for w in range(3):
                kept[0] += 1
                dve.wait_ge(setup_ps, kept[0])
                keep(w_qkv[:, :, w * D:(w + 1) * D], ps_a[:, :].rearrange("p (i o) -> p i o", i=KC))
            for g0 in range(0, G, 2):
                kept[0] += 1
                dve.wait_ge(setup_ps, kept[0])
                keep(w_o[:, g0:g0 + 2, :], ps_a[:, :].rearrange("p (g o) -> p g o", g=2))
            kept[0] += 1
            dve.wait_ge(setup_ps, kept[0])
            keep(c_t, ps_a[:, 0:KC * B].rearrange("p (c b) -> p c b", c=KC))
            kept[0] += 1
            dve.wait_ge(setup_ps, kept[0])
            keep(mod_t[:, :, :], ps_a[:, 0:6 * KC * B].rearrange("p (n b) -> p n b", b=B))
            dve.wait_ge(setup_ev, kept[0])
            for part in (1, 4):
                sl = mod_t[:, part * KC:(part + 1) * KC, :]
                link(nc.vector.tensor_scalar(sl, sl, 1.0, None, ALU.add))
            kept[0] += 1
            dve.wait_ge(setup_ps, kept[0])
            keep(mod_r, ps_a[0:B, :].rearrange("p (g d) -> p g d", g=2))
            dve.wait_ge(setup_ev, kept[0])
            nc.vector.tensor_scalar(mod_s, mod_r, 0.0, 2.0, ALU.is_ge, ALU.mult).then_inc(setup_ev2, 1)
            nc.vector.tensor_scalar(mod_m, mod_r, -1.0, None, ALU.mult).then_inc(setup_ev2, 1)
            dve.wait_ge(setup_ev2, 5)
            nc.vector.tensor_tensor(mod_m, mod_m, mod_r, ALU.max).then_inc(setup_ev2, 1)
            dve.wait_ge(setup_ev2, 6)
            nc.vector.tensor_scalar(mod_m, mod_m, ADA_MIN, None, ALU.max).then_inc(setup_ev2, 1)
            dve.wait_ge(setup_ev2, 7)
            link(nc.vector.scalar_tensor_tensor(out=mod_r, in0=mod_s, scalar=-1.0, in1=mod_m, op0=ALU.add, op1=ALU.mult))
            dve.wait_ge(masks_done, 17)
            link(nc.vector.tensor_copy(row_sel, ident[0:B, 0:B, None].to_broadcast([B, B, P])))
            for b in range(B):
                kept[0] += 1
                dve.wait_ge(setup_ps, kept[0])
                nc.vector.tensor_copy(gate_a[:, b, :], ps_a[:, 0:D]).then_inc(setup_ev2, 1)
                keep(gate_b[:, b, :], ps_a[:, D:2 * D])

            def layer_norm(T, par, t, load_count):
                if t == 0:
                    dve.wait_ge(xs_loaded[par], load_count)
                nc.vector.bn_stats(bn[:, 0, :], xs[:, par, t, :]).then_inc(stats_done, 1)
                dve.wait_ge(stats_done, T + 1)
                dve.sem_inc(dve_turns, 1)
                nc.vector.bn_aggr(mean_var[:, 0, :], bn[:, 0, :]).then_inc(mv_done, 1)
                dve.wait_ge(mv_done, T + 1)
                nc.vector.tensor_scalar(var_eps[:, :], mean_var[:, 0, 1:2], LN_EPS, None, ALU.add).then_inc(var_done, 1)
                dve.wait_ge(rstd_done, T + 1)
                nc.vector.tensor_scalar(xhat[:, :], xs[:, par, t, :], mean_var[:, 0, 0:1], rstd[:, 0, :],
                                        ALU.subtract, ALU.mult).then_inc(xhat_done, 1)

            def modulate(T, b):
                dve.wait_ge(xt_ps, T + 1)
                for k in range(KC):
                    nc.vector.tensor_scalar(h_t[:, k, :], ps_a[:, k * P:(k + 1) * P],
                                            mod_t[:, KC + k, b], mod_t[:, k, b],
                                            ALU.mult, ALU.add).then_inc(ht_done, 1)

            def rope(T, t):
                dve.wait_ge(qkv_ps, T + 1)
                qk = ps_b[:, :].rearrange("p (h d) -> p h d", d=DK)
                nc.vector.tensor_tensor(rot_a[:, :].rearrange("p (h d) -> p h d", d=DK), qk,
                                        cos_t[:, t, None, :].to_broadcast([P, 2 * H, DK]), ALU.mult).then_inc(rope_done, 1)
                qk2 = ps_b[:, :].rearrange("p (h d two) -> p h d two", two=2, d=DK // 2)
                b2 = rot_b[:, :].rearrange("p (h d two) -> p h d two", two=2, d=DK // 2)
                s2 = sin_t[:, t, :].rearrange("p (d two) -> p d two", two=2)
                for e in range(2):
                    nc.vector.tensor_tensor(b2[:, :, :, e], qk2[:, :, :, 1 - e],
                                            s2[:, None, :, e].to_broadcast([P, 2 * H, DK // 2]), ALU.mult).then_inc(rope_done, 1)

            def lo_parts(T, par, t):
                dve.wait_ge(hi_done, 2 * T + 2)
                r = rot[:, :].rearrange("p (w h d) -> p w h d", w=2, h=H)
                q_v = q_aug[:, par, t, :].rearrange("p (h w) -> p h w", w=HW)
                k_v = k_aug[:, :].rearrange("p (h w) -> p h w", w=HW)
                nc.vector.tensor_tensor(q_v[:, :, DK:2 * DK], r[:, 0], q_v[:, :, 0:DK], ALU.subtract).then_inc(lo_done, 1)
                nc.vector.tensor_tensor(k_v[:, :, 2 * DK:3 * DK], r[:, 1], k_v[:, :, 0:DK], ALU.subtract).then_inc(lo_done, 1)

            def keep_qt(T, par, t):
                dve.wait_ge(aug_ps, 2 * T + 1)
                nc.vector.tensor_copy(q_t[:, par, :, t * P:(t + 1) * P],
                                      ps_b[:, :].bitcast(F16).rearrange("p (m q) -> p m q", q=P)).then_inc(qt_kept, 1)

            def maxima(V, half, s):
                qt, first, n, j = MAX_SHOTS[s]
                L = P * (qt + 1)
                dve.wait_ge(max_ps, NSHOT * V + s + 1)
                dst = row_max[:, half, qt, :].rearrange("p (m j) -> p m j", j=2)[:, first:first + n, j]
                nc.vector.tensor_reduce(dst, ps_max[j][:, 0:n * L].rearrange("p (m l) -> p m l", m=n),
                                        AX.X, ALU.max).then_inc(max_done, 1)

            def negated(V, half, par, g):
                dve.wait_ge(max_done, NSHOT * V + NSHOT)
                q_v = q_aug[:, par, :, :].rearrange("p t (h w) -> p t h w", w=HW)
                nc.vector.tensor_scalar(q_v[:, :, HG * g:HG * (g + 1), 3 * DK], row_max[:, half, :, :],
                                        -1.0, None, ALU.mult).then_inc(negmax_done, 1)

            def divide(U, half, par, g, wait_at):
                dve.wait_ge(den_ps, U + 1)
                if wait_at:
                    dve.wait_ge(att_done, U)
                nc.vector.reciprocal(recip[:, :], ps_nd[:, :]).then_inc(recip_done, 1)
                dve.wait_ge(recip_done, U + 1)
                nc.vector.tensor_tensor(att_t[:, par, g, :], u_sb[:, half, :], recip[:, :], ALU.mult).then_inc(att_done, 1)

            def residual(b, par, load_count):
                dve.wait_ge(xr_loaded[par], load_count)
                for two in range(2):
                    dve.wait_ge(o_ps, 2 * b + two + 1)
                    if two:
                        dve.wait_ge(x1_done, 2 * b + 1)
                    nc.vector.tensor_tensor(gated[:, :, :], ps_nd[:, :].rearrange("p (t d) -> p t d", t=2),
                                            gate_a[:, bass.ds(b, 1), :].to_broadcast([P, 2, D]), ALU.mult).then_inc(gated_done, 1)
                    dve.wait_ge(gated_done, 2 * b + two + 1)
                    xv = xr[:, par, 2 * two:2 * two + 2, :]
                    nc.vector.tensor_tensor(xv, xv, gated[:, :, :], ALU.add).then_inc(x1_done, 1)

            for T in range(LEAD):
                layer_norm(T, (T // 4) % 2, T % 4, 16)
                modulate(T, slice(T // 4, T // 4 + 1))
                rope(T, T % 4)
                lo_parts(T, (T // 4) % 2, T % 4)
                keep_qt(T, (T // 4) % 2, T % 4)
            for s in range(NSHOT):
                maxima(0, 0, s)
            negated(0, 0, 0, 0)

            def unit(i, u):
                U = PAIR * i + u
                b, par, g = batch_of(i, u)
                b_t, par_t, t = batch_of(i, u + LEAD)
                _, par_v, g_v = batch_of(i, u + 1)
                has_t, has_v = in_range(i, u + LEAD), in_range(i, u + 1)
                if has_t:
                    layer_norm(U + LEAD, par_t, t, 16 * (i + (u + LEAD) // PAIR + 1))
                    modulate(U + LEAD, bass.ds(b_t, 1))
                for s in range(NSHOT):
                    if has_v:
                        maxima(U + 1, (u + 1) % 2, s)
                    if s == 9 and has_t:
                        rope(U + LEAD, t)
                if has_v:
                    negated(U + 1, (u + 1) % 2, par_v, g_v)
                if has_t:
                    lo_parts(U + LEAD, par_t, t)
                    keep_qt(U + LEAD, par_t, t)
                divide(U, u % 2, par, g, not has_v)
                if g == G - 1:
                    residual(b, par, 16 * (i + 1))

            all_units(dve, unit)


def route_part(nc, sem, x1_dram, xs_dram, w1, b1, w2, b2, switch_w, switch_b, logits, mod_t, ident,
               w1_hi, w1_lo, w2_hi, w2_lo, b1_t, b2_parts, slot, gate_p, tile_e):
    with ExitStack() as ctx:
        def sb(name, shape, dt=F32):
            return ctx.enter_context(nc.sbuf_tensor(name, shape, dt))

        def bank(name):
            return ctx.enter_context(nc.psum_tensor(name, [P, 512], F32))

        rows = sb("rows", [P, NT, 2 * D], F16)
        x1 = sb("x1", [P, 2, QT, D])
        raw1 = sb("raw1", [P, KC, F])
        raw2 = sb("raw2", [P, F // P, D])
        zero = sb("zero", [P, 2 * D], F16)
        bn = sb("bn2", [P, 6])
        mean_var = sb("mean_var2", [P, 2])
        var_eps = sb("var_eps2", [P, 1])
        neg_half = sb("neg_half2", [P, 1])
        rstd = sb("rstd2", [P, 1])
        xhat = sb("xhat2", [P, D])
        h_t = sb("h_t2", [P, 2, KC, P])
        sw = sb("sw", [P, KC, E])
        sw_b = sb("sw_b", [P, E])
        b1_nat = sb("b1_nat", [E * F // P, P])
        ps_xt, ps_row, ps_logit = bank("ps_xt"), [bank("ps_row0"), bank("ps_row1")], bank("ps_logit")
        ps_rank = bank("ps_rank")
        scr = [raw1[:, k, n * NT * E:(n + 1) * NT * E].rearrange("p (t e) -> p t e", e=E)
               for k in range(KC) for n in range(4)]
        onehot, tmp, cum_a, cum_b, within, iota_e, shifted, _ = scr
        jcmp = raw2[:, 0, 0:E * NT].rearrange("p (e j) -> p e j", e=E)
        iota_j = raw2[:, 1, 0:NT]
        iota_i = raw2[:, 2, 0:NSLOT_T]
        ecmp = raw2[:, 3:5, :].rearrange("p a b -> p (a b)")[:, 0:NSLOT_T * E].rearrange("p (j e) -> p j e", e=E)
        before = raw2[:, 5, 0:P]
        ones = raw2[:, 5, P:2 * P]
        small = raw2[:, 6, :]
        top, denom, prob_max, first = (small[:, n * NT:(n + 1) * NT] for n in range(4))
        tiles_of, tiles_a, tiles_b, start_of = (small[:, 128 + n * E:128 + (n + 1) * E] for n in range(4))
        slot_f = small[:, 160:160 + NT]
        expert_f = small[:, 192:192 + NSLOT_T]

        lead = rows[0:1, :, :].rearrange("p t d -> p (t d)")
        b2_f = lead[:, 0:2 * E * D].bitcast(F32)
        b2_rest = lead[:, 2 * E * D:4 * E * D].bitcast(F32)
        b2_s = lead[:, 4 * E * D:7 * E * D].bitcast(BF16)

        x1_v = x1_dram.rearrange("(b t p) d -> b p t d", t=QT, p=P)
        w1_v = w1.rearrange("e (c p) f -> e p c f", p=P)
        w2_v = w2.rearrange("e (f p) d -> e p f d", p=P)

        x1_loaded = [sem("c_x1_loaded0"), sem("c_x1_loaded1")]
        zero_done, cleared = sem("c_zero_done"), sem("c_cleared")
        raw1_loaded, raw2_loaded = sem("raw1_loaded"), sem("raw2_loaded")
        w_hi_done, w_lo_done = sem("w_hi_done"), sem("w_lo_done")
        small_in, b2_spread = sem("c_small_in"), sem("b2_spread")
        turns = sem("c_turns")
        b1_ps, b1_kept = sem("b1_ps"), sem("b1_kept")
        b2_mid, b2_split, b2_split_in = sem("b2_mid"), sem("b2_split"), sem("b2_split_in")
        stats, mv, var, rs, xh = sem("c_stats"), sem("c_mv"), sem("c_var"), sem("c_rstd"), sem("c_xhat")
        xt_ps, ht_done, row_ps, logit_ps = sem("c_xt_ps"), sem("c_ht_done"), sem("c_row_ps"), sem("c_logit_ps")
        hi_done, lo_done, logit_kept = sem("c_hi_done"), sem("c_lo_done"), sem("c_logit_kept")
        iotas, chain, shifted_done, exp_done, rank_ps = (sem("c_iotas"), sem("c_chain"), sem("c_shifted"),
                                                         sem("c_exp"), sem("c_rank_ps"))
        onehot_done, slots_done, scattered = sem("c_onehot"), sem("c_slots"), sem("c_scattered")

        block = ctx.enter_context(nc.Block())

        @block.sync
        def _(sp):
            sp.dma_start(sw[:, :, :], switch_w.rearrange("(c p) e -> p c e", p=P)).then_inc(small_in, 16)
            sp.dma_start(sw_b[:, :], switch_b.partition_broadcast(P)).then_inc(small_in, 16)
            sp.dma_start(b1_nat[:, :], b1.rearrange("e (f p) -> (e f) p", p=P)).then_inc(small_in, 16)
            sp.dma_start(b2_f, b2.rearrange("(a e) d -> a (e d)", a=1)).then_inc(b2_split_in, 16)
            for b in range(2):
                sp.dma_start(x1[:, b, :, :], x1_v[b]).then_inc(x1_loaded[b], 16)
            sp.dma_start(raw1[:, :, :], w1_v[0]).then_inc(raw1_loaded, 16)
            sp.dma_start(raw2[:, :, :], w2_v[0]).then_inc(raw2_loaded, 16)
            sp.wait_ge(zero_done, 2)
            sp.dma_start(xs_dram.rearrange("(n p) d -> p n d", p=P),
                         zero[:, None, :].to_broadcast([P, NSLOT_T, 2 * D])).then_inc(cleared, 16)
            sp.wait_ge(b2_split, 3)
            for n in range(3):
                sp.dma_start(b2_parts[n:n + 1, :], b2_s[:, n * E * D:(n + 1) * E * D]).then_inc(b2_spread, 16)

            def load_expert(e):
                sp.wait_ge(w_hi_done, 2 * e - 1)
                sp.wait_ge(w_lo_done, 2 * e - 1)
                sp.dma_start(raw1[:, :, :], w1_v[e]).then_inc(raw1_loaded, 16)
                sp.wait_ge(w_hi_done, 2 * e)
                sp.wait_ge(w_lo_done, 2 * e)
                sp.dma_start(raw2[:, :, :], w2_v[e]).then_inc(raw2_loaded, 16)

            load_expert(1)
            with sp.Fori(1, B // 2) as k:
                for half in range(2):
                    b = 2 * k + half
                    sp.wait_ge(xh, QT * (b - 1))
                    sp.dma_start(x1[:, half, :, :], x1_v[b]).then_inc(x1_loaded[half], 16)
                    load_expert(b)
            sp.wait_ge(cleared, 16)

        @block.gpsimd
        def _(pool):
            nc.gpsimd.memset(zero[:, :], 0.0).then_inc(zero_done, 1)
            nc.gpsimd.memset(neg_half[:, :], -0.5).then_inc(zero_done, 1)
            pool.wait_ge(zero_done, 2)
            with pool.Fori(0, B) as b:
                for t in range(QT):
                    pool.wait_ge(var, QT * b + t + 1)
                    nc.gpsimd.tensor_tensor(rstd[:, :], var_eps[:, :], neg_half[:, :], ALU.pow).then_inc(rs, 1)
            pool.wait_ge(w_hi_done, 2 * E)
            pool.wait_ge(w_lo_done, 2 * E)
            nc.gpsimd.iota(iota_e, pattern=[[0, NT], [1, E]], base=-E, channel_multiplier=0,
                           allow_small_or_imprecise_dtypes=True).then_inc(iotas, 1)
            nc.gpsimd.iota(iota_j, pattern=[[P, NT]], base=0, channel_multiplier=0,
                           allow_small_or_imprecise_dtypes=True).then_inc(iotas, 1)
            nc.gpsimd.iota(iota_i, pattern=[[1, NSLOT_T]], base=0, channel_multiplier=0,
                           allow_small_or_imprecise_dtypes=True).then_inc(iotas, 1)
            nc.gpsimd.memset(ones, 1.0).then_inc(iotas, 1)
            nc.gpsimd.memset(before, 1.0).then_inc(iotas, 1)
            pool.wait_ge(iotas, 5)
            nc.gpsimd.affine_select(out=before, in_=before, compare_op=ALU.is_gt, fill=0.0, base=0,
                                    pattern=[[1, P]], channel_multiplier=-1).then_inc(iotas, 1)
            pool.wait_ge(slots_done, 1)
            pool.wait_ge(cleared, 16)
            pool.wait_ge(hi_done, NT)
            pool.wait_ge(lo_done, NT)
            for T in range(NT):
                nc.gpsimd.indirect_dma_start(xs_dram, bass.IndirectOffsetOnAxis(ap=slot[:, T:T + 1], axis=0),
                                             rows[:, T, :], None).then_inc(scattered, 16)
            pool.wait_ge(scattered, 16 * NT)

        @block.tensor
        def _(pe):
            mm = nc.tensor.matmul
            pe.wait_ge(small_in, 48)
            nc.tensor.transpose(ps_rank[:, 0:E * F // P], b1_nat[:, :], ident[0:E * F // P, 0:E * F // P]).then_inc(b1_ps, 1)
            with pe.Fori(0, B) as b:
                for t in range(QT):
                    T = QT * b + t
                    pe.wait_ge(xh, T + 1)
                    for k in range(KC):
                        last = nc.tensor.transpose(ps_xt[:, k * P:(k + 1) * P], xhat[:, k * P:(k + 1) * P], ident[:, :])
                    last.then_inc(xt_ps, 1)
                    pe.wait_ge(ht_done, KC * T + KC)
                    if t >= 2:
                        pe.wait_ge(lo_done, T - 1)
                        pe.wait_ge(hi_done, T - 1)
                    for k in range(KC):
                        last = nc.tensor.transpose(ps_row[t % 2][:, k * P:(k + 1) * P], h_t[:, t % 2, k, :], ident[:, :])
                    last.then_inc(row_ps, 1)
                    if t:
                        pe.wait_ge(logit_kept, T)
                    for k in range(KC):
                        last = mm(ps_logit[:, 0:E], h_t[:, t % 2, k, :], sw[:, k, :], start=(k == 0), stop=(k == KC - 1))
                    last.then_inc(logit_ps, 1)
                pe.wait_ge(logit_kept, QT * b + QT)
                pe.wait_ge(lo_done, QT * b + QT)
            pe.wait_ge(iotas, 6)
            pe.wait_ge(onehot_done, 1)
            pe.wait_ge(b1_kept, 1)
            flat = onehot.rearrange("p t e -> p (t e)")
            mm(ps_rank[:, 0:NT * E], before, flat, start=True, stop=True)
            mm(ps_rank[:, NT * E:2 * NT * E], ones, flat, start=False, stop=True, skip_group_check=True).then_inc(rank_ps, 1)

        @block.scalar
        def _(act):
            act.wait_ge(b1_ps, 1)
            nc.scalar.activation(b1_t[:, :, :].rearrange("p e f -> p (e f)"), ps_rank[:, 0:E * F // P], ACT.Copy).then_inc(b1_kept, 1)
            act.wait_ge(b2_spread, 48)
            with act.Fori(0, B) as b:
                act.wait_ge(raw1_loaded, 16 * b + 16)
                nc.scalar.activation(w1_hi[:, bass.ds(b, 1), :, :].rearrange("p e c f -> p (e c) f"), raw1[:, :, :],
                                     ACT.Copy, scale=W_SCALE).then_inc(w_hi_done, 1)
                act.wait_ge(raw2_loaded, 16 * b + 16)
                nc.scalar.activation(w2_hi[:, bass.ds(b, 1), :, :].rearrange("p e c f -> p (e c) f"), raw2[:, :, :],
                                     ACT.Copy, scale=W_SCALE).then_inc(w_hi_done, 1)
                for t in range(QT):
                    T = QT * b + t
                    act.wait_ge(row_ps, T + 1)
                    nc.scalar.activation(rows[:, bass.ds(T, 1), 0:D].rearrange("p t d -> p (t d)"), ps_row[t % 2][:, 0:D], ACT.Copy).then_inc(hi_done, 1)
                    act.wait_ge(logit_ps, T + 1)
                    nc.scalar.activation(logits[:, bass.ds(T, 1), :].rearrange("p t d -> p (t d)"), ps_logit[:, 0:E], ACT.Copy).then_inc(logit_kept, 1)
            act.wait_ge(shifted_done, 1)
            nc.scalar.activation(tmp, shifted, ACT.Exp).then_inc(exp_done, 1)

        @block.vector
        def _(dve):
            dve.wait_ge(b2_split_in, 16)
            part = [b2_s[:, n * E * D:(n + 1) * E * D] for n in range(3)]
            nc.vector.tensor_copy(part[0], b2_f).then_inc(b2_split, 1)
            dve.wait_ge(b2_split, 1)
            nc.vector.tensor_tensor(b2_rest, b2_f, part[0], ALU.subtract).then_inc(b2_mid, 1)
            dve.wait_ge(b2_mid, 1)
            nc.vector.tensor_copy(part[1], b2_rest).then_inc(b2_split, 1)
            dve.wait_ge(b2_split, 2)
            nc.vector.tensor_tensor(b2_f, b2_rest, part[1], ALU.subtract).then_inc(b2_mid, 1)
            dve.wait_ge(b2_mid, 2)
            nc.vector.tensor_copy(part[2], b2_f).then_inc(b2_split, 1)
            with dve.Fori(0, B // 2) as i:
                for u in range(2 * QT):
                    T = 2 * QT * i + u
                    par, t = u // QT, u % QT
                    if t == 0:
                        dve.wait_ge(x1_loaded[par], 16 * i + 16)
                    if t % 2 == 1:
                        e = 2 * i + par
                        raw, hi, lo, loaded = ((raw1, w1_hi, w1_lo, raw1_loaded) if t == 1 else
                                               (raw2, w2_hi, w2_lo, raw2_loaded))
                        dve.wait_ge(w_hi_done, 2 * e + (1 if t == 1 else 2))
                        nc.vector.scalar_tensor_tensor(out=lo[:, bass.ds(e, 1), :, :].rearrange("p e c f -> p (e c) f"),
                                                       in0=raw[:, :, :], scalar=W_SCALE,
                                                       in1=hi[:, bass.ds(e, 1), :, :].rearrange("p e c f -> p (e c) f"),
                                                       op0=ALU.mult, op1=ALU.subtract).then_inc(w_lo_done, 1)
                    nc.vector.bn_stats(bn[:, :], x1[:, par, t, :]).then_inc(stats, 1)
                    dve.wait_ge(stats, T + 1)
                    dve.sem_inc(turns, 1)
                    nc.vector.bn_aggr(mean_var[:, :], bn[:, :]).then_inc(mv, 1)
                    dve.wait_ge(mv, T + 1)
                    nc.vector.tensor_scalar(var_eps[:, :], mean_var[:, 1:2], LN_EPS, None, ALU.add).then_inc(var, 1)
                    dve.wait_ge(rs, T + 1)
                    nc.vector.tensor_scalar(xhat[:, :], x1[:, par, t, :], mean_var[:, 0:1], rstd[:, :],
                                            ALU.subtract, ALU.mult).then_inc(xh, 1)
                    dve.wait_ge(xt_ps, T + 1)
                    b_ = 2 * i + par
                    for k in range(KC):
                        nc.vector.tensor_scalar(h_t[:, t % 2, k, :], ps_xt[:, k * P:(k + 1) * P],
                                                mod_t[:, 4 * KC + k, bass.ds(b_, 1)], mod_t[:, 3 * KC + k, bass.ds(b_, 1)],
                                                ALU.mult, ALU.add).then_inc(ht_done, 1)
                    dve.wait_ge(hi_done, T + 1)
                    nc.vector.tensor_tensor(rows[:, bass.ds(T, 1), D:2 * D].rearrange("p t d -> p (t d)"), ps_row[t % 2][:, 0:D],
                                            rows[:, bass.ds(T, 1), 0:D].rearrange("p t d -> p (t d)"), ALU.subtract).then_inc(lo_done, 1)

            done = [0]

            def link(ins):
                done[0] += 1
                ins.then_inc(chain, 1)
                dve.wait_ge(chain, done[0])

            tt, ts, red = nc.vector.tensor_tensor, nc.vector.tensor_scalar, nc.vector.tensor_reduce
            dve.wait_ge(logit_kept, NT)
            dve.wait_ge(iotas, 6)
            link(tt(logits[:, :, :], logits[:, :, :], sw_b[:, None, :].to_broadcast([P, NT, E]), ALU.add))
            link(red(top, logits[:, :, :], AX.X, ALU.max))
            top_b = top[:, :, None].to_broadcast([P, NT, E])
            tt(shifted, logits[:, :, :], top_b, ALU.subtract).then_inc(shifted_done, 1)
            link(tt(onehot, logits[:, :, :], top_b, ALU.is_equal))
            link(tt(cum_a, onehot, iota_e, ALU.mult))
            link(red(first, cum_a, AX.X, ALU.min))
            ins = tt(onehot, iota_e, first[:, :, None].to_broadcast([P, NT, E]), ALU.is_equal)
            ins.then_inc(onehot_done, 1)
            dve.wait_ge(exp_done, 1)
            link(red(denom, tmp, AX.X, ALU.add))
            link(nc.vector.reciprocal(prob_max, denom))
            link(ts(gate_p[:, :], prob_max, 1.0 / W_SCALE, None, ALU.mult))
            dve.wait_ge(rank_ps, 1)
            link(nc.vector.tensor_copy(cum_a, ps_rank[:, NT * E:2 * NT * E].rearrange("p (t e) -> p t e", e=E)))
            link(nc.vector.tensor_copy(within, ps_rank[:, 0:NT * E].rearrange("p (t e) -> p t e", e=E)))
            link(tt(within, within, cum_a, ALU.subtract))
            a, b2_ = cum_a, cum_b
            step = 1
            while step < NT:
                nc.vector.tensor_copy(b2_[:, 0:step, :], a[:, 0:step, :]).then_inc(chain, 1)
                done[0] += 1
                link(tt(b2_[:, step:NT, :], a[:, step:NT, :], a[:, 0:NT - step, :], ALU.add))
                a, b2_ = b2_, a
                step *= 2
            link(tt(jcmp, iota_j[:, None, :].to_broadcast([P, E, NT]),
                    a[:, NT - 1, :, None].to_broadcast([P, E, NT]), ALU.is_lt))
            link(red(tiles_of, jcmp, AX.X, ALU.add))
            ta, tb = tiles_of, tiles_a
            step = 1
            while step < E:
                nc.vector.tensor_copy(tb[:, 0:step], ta[:, 0:step]).then_inc(chain, 1)
                done[0] += 1
                link(tt(tb[:, step:E], ta[:, step:E], ta[:, 0:E - step], ALU.add))
                ta, tb = tb, (tiles_b if ta is tiles_of else ta)
                step *= 2
            link(tt(start_of, ta, tiles_of, ALU.subtract))
            link(ts(start_of, start_of, float(P), None, ALU.mult))
            link(tt(ecmp, iota_i[:, :, None].to_broadcast([P, NSLOT_T, E]), ta[:, None, :].to_broadcast([P, NSLOT_T, E]), ALU.is_ge))
            link(red(expert_f, ecmp, AX.X, ALU.add))
            link(ts(tile_e[:, :], expert_f, float(E - 1), None, ALU.min))
            link(tt(within, within, a, ALU.add))
            link(tt(within, within, start_of[:, None, :].to_broadcast([P, NT, E]), ALU.add))
            link(tt(within, within, onehot, ALU.mult))
            link(red(slot_f, within, AX.X, ALU.add))
            nc.vector.tensor_copy(slot[:, :], slot_f).then_inc(slots_done, 1)


def expert_part(nc, sem, x1_dram, xs_dram, ys_dram, gate_b, ident16, w1_hi, w1_lo, w2_hi, w2_lo, b1_t,
                b2_parts, slot, gate_p, tile_e, out):
    with ExitStack() as ctx:
        def sb(name, shape, dt=F32):
            return ctx.enter_context(nc.sbuf_tensor(name, shape, dt))

        def bank(name):
            return ctx.enter_context(nc.psum_tensor(name, [P, 512], F32))

        FC = F // P
        rows = sb("x_rows", [P, 2, 2 * D], F16)
        tok_t = sb("tok_t", [P, 2, 2, KC, P], F16)
        hid = sb("hid", [P, 2, FC, P])
        hid_hi = sb("hid_hi", [P, 2, FC, P], F16)
        hid_lo = sb("hid_lo", [P, 2, FC, P], F16)
        y = sb("y", [P, 2, D])
        scale3 = sb("scale3", [3, P], BF16)
        x1 = sb("x1_last", [P, 2, QT, D])
        back = sb("back", [P, 2, QT, D])
        ps_x = bank("ps_x")
        ps_h = [[bank(f"ps_h{a}{b}") for b in range(2)] for a in range(2)]
        ps_y = [bank("ps_y0"), bank("ps_y1")]

        rows_loaded = [sem("rows_loaded0"), sem("rows_loaded1")]
        scale_done = sem("scale_done")
        x_ps, x_kept, h_ps, gelu_done = sem("f_x_ps"), sem("f_x_kept"), sem("f_h_ps"), sem("f_gelu")
        hi_done, lo_done, y_ps, y_kept = sem("f_hi"), sem("f_lo"), sem("f_y_ps"), sem("f_y_kept")
        y_stored = [sem("y_stored0"), sem("y_stored1")]
        x1_loaded = [sem("l_x1_loaded0"), sem("l_x1_loaded1")]
        gathered = [sem("gathered0"), sem("gathered1")]
        gated, summed = sem("l_gated"), sem("l_summed")
        out_stored = [sem("out_stored0"), sem("out_stored1")]

        xs_v = xs_dram.rearrange("(n p) d -> n p d", p=P)
        ys_v = ys_dram.rearrange("(n p) d -> n p d", p=P)
        x1_v = x1_dram.rearrange("(b t p) d -> b p t d", t=QT, p=P)
        out_v = out.rearrange("b (t p) d -> b p t d", p=P)
        NJ = NSLOT_T - 1

        block = ctx.enter_context(nc.Block())

        def steps(eng, step):
            step(0, 0, first=True)
            with eng.Fori(0, (NJ - 1) // 2) as i:
                for u in range(2):
                    step(2 * i + u + 1, (u + 1) % 2)

        @block.sync
        def _(sp):
            for j in range(2):
                sp.dma_start(rows[:, j, :], xs_v[j]).then_inc(rows_loaded[j], 16)
            for b in range(2):
                sp.dma_start(x1[:, b, :, :], x1_v[b]).then_inc(x1_loaded[b], 16)
            with sp.Fori(1, NSLOT_T // 2) as k:
                for half in range(2):
                    j = 2 * k + half
                    sp.wait_ge(x_ps, j - 1)
                    sp.dma_start(rows[:, half, :], xs_v[j]).then_inc(rows_loaded[half], 16)
                    sp.wait_ge(y_kept, j - 1)
                    sp.dma_start(ys_v[j - 2], y[:, half, :]).then_inc(y_stored[half], 16)
            sp.wait_ge(y_kept, NJ)
            sp.dma_start(ys_v[NJ - 1], y[:, (NJ - 1) % 2, :]).then_inc(y_stored[0], 16)
            for b in range(2):
                sp.wait_ge(summed, QT * (b + 1))
                sp.dma_start(out_v[b], x1[:, b, :, :]).then_inc(out_stored[b], 16)
            with sp.Fori(1, B // 2) as k:
                for half in range(2):
                    b = 2 * k + half
                    sp.wait_ge(out_stored[half], 16 * k)
                    sp.dma_start(x1[:, half, :, :], x1_v[b]).then_inc(x1_loaded[half], 16)
                    sp.wait_ge(summed, QT * (b + 1))
                    sp.dma_start(out_v[b], x1[:, half, :, :]).then_inc(out_stored[half], 16)
            for half in range(2):
                sp.wait_ge(out_stored[half], 16 * (B // 2))

        @block.gpsimd
        def _(pool):
            nc.gpsimd.memset(scale3[:, :], W_SCALE).then_inc(scale_done, 1)
            pool.wait_ge(y_stored[0], 16 * ((NJ + 1) // 2))
            pool.wait_ge(y_stored[1], 16 * (NJ // 2))
            for b in range(B):
                if b >= 2:
                    pool.wait_ge(summed, QT * (b - 1))
                for t in range(QT):
                    T = QT * b + t
                    nc.gpsimd.indirect_dma_start(back[:, b % 2, t, :], None, ys_dram,
                                                 bass.IndirectOffsetOnAxis(ap=slot[:, T:T + 1], axis=0)).then_inc(gathered[b % 2], 16)

        @block.tensor
        def _(pe):
            mm = nc.tensor.matmul

            def transposes(j, half, load_count):
                pe.wait_ge(rows_loaded[half], load_count)
                ge(pe, x_kept, j)
                for n in range(2 * KC):
                    last = nc.tensor.transpose(ps_x[:, :].bitcast(F16)[:, n * P:(n + 1) * P],
                                               rows[:, half, n * P:(n + 1) * P], ident16[:, :])
                last.then_inc(x_ps, 1)

            def product1(j, half, e):
                pe.wait_ge(x_kept, j + 1)
                for q in range(2):
                    for f in range(q * FC // 2, (q + 1) * FC // 2):
                        o = ps_h[half][q][:, (f % (FC // 2)) * P:(f % (FC // 2) + 1) * P]
                        n = 0
                        for k in range(KC):
                            for w, parts in ((w1_hi, (0, 1)), (w1_lo, (0,))):
                                for part in parts:
                                    last = mm(o, w[:, bass.ds(e, 1), k, f * P:(f + 1) * P].rearrange("p e f -> p (e f)"), tok_t[:, half, part, k, :],
                                              start=(n == 0 and f % (FC // 2) == 0), stop=(n == 3 * KC - 1),
                                              skip_group_check=True)
                                    n += 1
                    last.then_inc(h_ps, 1)

            def product2(j, half, e):
                pe.wait_ge(hi_done, 2 * j + 2)
                pe.wait_ge(lo_done, 2 * j + 2)
                mm(ps_y[half][:, 0:D], scale3[:, :], b2_parts[:, bass.ds(e * D, D)], start=True, stop=False)
                for f in range(FC):
                    for a, w in ((hid_hi, w2_hi), (hid_lo, w2_hi), (hid_hi, w2_lo)):
                        last = mm(ps_y[half][:, 0:D], a[:, half, f, :], w[:, bass.ds(e, 1), f, :].rearrange("p e d -> p (e d)"),
                                  start=False, stop=(f == FC - 1 and w is w2_lo))
                last.then_inc(y_ps, 1)

            pe.wait_ge(scale_done, 1)
            transposes(0, 0, 16)
            e0 = pe.value_load(tile_e[0:1, 0:1], min_val=0, max_val=E - 1)
            product1(0, 0, e0)
            transposes(1, 1, 16)
            with pe.Fori(0, (NJ - 1) // 2) as i:
                for u in range(2):
                    j = 2 * i + u + 1
                    e = pe.value_load(tile_e[0:1, bass.ds(j, 1)], min_val=0, max_val=E - 1)
                    product1(j, (u + 1) % 2, e)
                    transposes(j + 1, u, 16 * (i + 2))
                    e_last = pe.value_load(tile_e[0:1, bass.ds(j - 1, 1)], min_val=0, max_val=E - 1)
                    product2(j - 1, u, e_last)
            e = pe.value_load(tile_e[0:1, NJ - 1:NJ], min_val=0, max_val=E - 1)
            product2(NJ - 1, 0, e)

        @block.scalar
        def _(act):
            def keep_x(j, half):
                act.wait_ge(x_ps, j + 1)
                nc.scalar.activation(tok_t[:, half, :, :, :].rearrange("p a k m -> p (a k m)"),
                                     ps_x[:, :].bitcast(F16)[:, 0:2 * KC * P], ACT.Copy).then_inc(x_kept, 1)

            def gelu(j, half, e):
                for f in range(FC):
                    q = f // (FC // 2)
                    if f % (FC // 2) == 0:
                        act.wait_ge(h_ps, 2 * j + q + 1)
                    ins = nc.scalar.activation(hid[:, half, f, :], ps_h[half][q][:, (f % (FC // 2)) * P:(f % (FC // 2) + 1) * P],
                                               ACT.Gelu_apprx_tanh, bias=b1_t[:, bass.ds(e, 1), f], scale=1.0 / W_SCALE)
                    if f % (FC // 2) == FC // 2 - 1:
                        ins.then_inc(gelu_done, 1)

            keep_x(0, 0)
            e0 = act.value_load(tile_e[0:1, 0:1], min_val=0, max_val=E - 1)
            keep_x(1, 1)
            gelu(0, 0, e0)
            with act.Fori(0, (NJ - 1) // 2) as i:
                for u in range(2):
                    j = 2 * i + u + 1
                    e = act.value_load(tile_e[0:1, bass.ds(j, 1)], min_val=0, max_val=E - 1)
                    keep_x(j + 1, u)
                    gelu(j, (u + 1) % 2, e)

        @block.vector
        def _(dve):
            def halves(j, half):
                for q in range(2):
                    dve.wait_ge(gelu_done, 2 * j + q + 1)
                    sl = slice(q * FC // 2, (q + 1) * FC // 2)
                    nc.vector.tensor_copy(hid_hi[:, half, sl, :], hid[:, half, sl, :]).then_inc(hi_done, 1)
                    dve.wait_ge(hi_done, 2 * j + q + 1)
                    nc.vector.tensor_tensor(hid_lo[:, half, sl, :], hid[:, half, sl, :], hid_hi[:, half, sl, :],
                                            ALU.subtract).then_inc(lo_done, 1)

            def keep_y(j, half):
                dve.wait_ge(y_ps, j + 1)
                nc.vector.tensor_copy(y[:, half, :], ps_y[half][:, 0:D]).then_inc(y_kept, 1)

            halves(0, 0)
            halves(1, 1)
            keep_y(0, 0)
            halves(2, 0)
            keep_y(1, 1)
            with dve.Fori(1, (NJ - 1) // 2) as i:
                for u in range(2):
                    j = 2 * i + u + 1
                    halves(j, (u + 1) % 2)
                    dve.wait_ge(y_stored[u], 16 * i)
                    keep_y(j - 1, u)
            dve.wait_ge(y_stored[0], 16 * ((NJ - 1) // 2))
            keep_y(NJ - 1, 0)
            with dve.Fori(0, B // 2) as i:
                for u in range(2 * QT):
                    par, t = u // QT, u % QT
                    b, T = 2 * i + par, 2 * QT * i + u
                    if t == 0:
                        dve.wait_ge(x1_loaded[par], 16 * i + 16)
                        dve.wait_ge(gathered[par], 16 * QT * (i + 1))
                    nc.vector.scalar_tensor_tensor(out=back[:, par, t, :], in0=back[:, par, t, :],
                                                   scalar=gate_p[:, bass.ds(T, 1)],
                                                   in1=gate_b[:, bass.ds(b, 1), :].rearrange("p b d -> p (b d)"),
                                                   op0=ALU.mult, op1=ALU.mult).then_inc(gated, 1)
                    dve.wait_ge(gated, T + 1)
                    nc.vector.tensor_tensor(x1[:, par, t, :], x1[:, par, t, :], back[:, par, t, :], ALU.add).then_inc(summed, 1)


_INS = {"x": "L0_attn_x", "wq": "L0_attn_Wq", "bq": "L0_attn_bq", "wk": "L0_attn_Wk", "bk": "L0_attn_bk",
        "wv": "L0_attn_Wv", "bv": "L0_attn_bv", "wo": "L0_attn_Wo", "bo": "L0_attn_bo",
        "switch_w": "L0_ffn_switch_w", "switch_b": "L0_ffn_switch_b", "w1": "L0_ffn_w1", "b1": "L0_ffn_b1",
        "w2": "L0_ffn_w2", "b2": "L0_ffn_b2", "c": "L0_c", "wmod": "L0_wmod"}


def rope_tables():
    import numpy as np

    inv_freq = np.float32(1.0) / np.float32(10000.0) ** (np.arange(0, DK, 2, dtype=np.float32) / np.float32(DK))
    angles = (np.arange(S, dtype=np.float32)[:, None] * inv_freq.astype(np.float32)).astype(np.float64)
    sign = np.where(np.arange(DK) % 2 == 0, -1.0, 1.0)
    return (np.repeat(np.cos(angles), 2, axis=1).astype(np.float32),
            (np.repeat(np.sin(angles), 2, axis=1) * sign).astype(np.float32))


def kernel(**inputs):
    import numpy as np
    import concourse.bacc as bacc
    from concourse.bass_utils import run_bass_kernel_spmd

    nc = bacc.Bacc("TRN2", target_bir_lowering=False, num_devices=1)
    arrays = {name: np.ascontiguousarray(inputs[given]) for name, given in _INS.items()}
    arrays["rope_cos"], arrays["rope_sin"] = rope_tables()
    args = [nc.dram_tensor(name, a.shape, mybir.dt.from_np(a.dtype), kind="ExternalInput").ap()
            for name, a in arrays.items()]
    out = nc.dram_tensor("out", (B, S, D), F32, kind="ExternalOutput").ap()
    build(nc, *args, out)
    r = run_bass_kernel_spmd(nc, [arrays], core_ids=[0])
    return r.results[0]["out"]
```

```python
import concourse.bass as bass
from concourse import mybir
from contextlib import ExitStack, nullcontext
from math import prod

F32 = mybir.dt.float32
F16 = mybir.dt.float16
BF16 = mybir.dt.bfloat16
I32 = mybir.dt.int32
ALU = mybir.AluOpType
ACT = mybir.ActivationFunctionType
AX = mybir.AxisListType

B, S, D = 8, 512, 256
H = 16
DK = D // H
P = 128
QT = S // P
NT = B * QT
KC = D // P
E, F = 8, 1024
NSLOT_T = NT + E
W_SCALE = 64.0
HG = 4
G = H // HG
NU = B * G
HW = 64
NEG = -1.0e30
SCALE = 1.0 / DK ** 0.5
LN_EPS = 1e-5
ADA_MIN = 0.25
LEAD = 5

def shots(length):
    out = []
    for blk in range(QT):
        n = min(2, S // length(blk)) if length(blk) * 2 <= S else 1
        for first in range(0, 2, n):
            for j in range(2):
                out.append((blk, first, n, j))
    return out


MAX_SHOTS = shots(lambda qt: P * (qt + 1))
EXP_SHOTS = shots(lambda kb: S - P * kb)
NSHOT = len(MAX_SHOTS)
EXP_UPTO = [1 + max(i for i, s in enumerate(EXP_SHOTS) if s[0] == kb) for kb in range(QT)]
P_AT = [HG * sum(S - P * k for k in range(kb)) for kb in range(QT + 1)]


def ge(eng, sem, count):
    if isinstance(count, int) and count <= 0:
        return
    eng.wait_ge(sem, count)


def build(nc, x, wq, bq, wk, bk, wv, bv, wo, bo, switch_w, switch_b, w1, b1, w2, b2, c, wmod,
          rope_cos, rope_sin, out):
    with ExitStack() as whole:
        sems = {}

        def sem(name):
            if name not in sems:
                sems[name] = whole.enter_context(nc.semaphore(name))
            return sems[name]

        x1_dram = nc.dram_tensor("x1_dram", [B * S, D], F32, kind="Internal").ap()
        xs_dram = nc.dram_tensor("xs_dram", [NSLOT_T * P, 2 * D], F16, kind="Internal").ap()
        ys_dram = nc.dram_tensor("ys_dram", [(NSLOT_T - 1) * P, D], F32, kind="Internal").ap()

        def sb(name, shape, dt=F32):
            return whole.enter_context(nc.sbuf_tensor(name, shape, dt))

        logits = sb("logits", [P, NT, E])
        mod_t = sb("mod_t", [P, 6 * KC, B])
        gate_b = sb("gate_b", [P, B, D])
        ident = sb("ident", [P, P])
        ident16 = sb("ident16", [P, P], F16)
        attention_part(nc, sem, x, wq, bq, wk, bk, wv, bv, wo, bo, c, wmod, rope_cos, rope_sin,
                       x1_dram, mod_t, gate_b, ident, ident16)
        w1_hi, w1_lo = (sb(n, [P, E, KC, F], F16) for n in ("w1_hi", "w1_lo"))
        w2_hi, w2_lo = (sb(n, [P, E, F // P, D], F16) for n in ("w2_hi", "w2_lo"))
        b1_t = sb("b1_t", [P, E, F // P])
        b2_parts = sb("b2_parts", [3, E * D], BF16)
        slot = sb("slot", [P, NT], I32)
        gate_p = sb("gate_p", [P, NT])
        tile_e = sb("tile_e", [P, NSLOT_T], I32)
        route_part(nc, sem, x1_dram, xs_dram, w1, b1, w2, b2, switch_w, switch_b, logits, mod_t, ident,
                   w1_hi, w1_lo, w2_hi, w2_lo, b1_t, b2_parts, slot, gate_p, tile_e)
        expert_part(nc, sem, x1_dram, xs_dram, ys_dram, gate_b, ident16, w1_hi, w1_lo, w2_hi, w2_lo, b1_t,
                    b2_parts, slot, gate_p, tile_e, out)


def attention_part(nc, sem, x, wq, bq, wk, bk, wv, bv, wo, bo, c, wmod, rope_cos, rope_sin,
                   x1_dram, mod_t, gate_b, ident, ident16):
    with ExitStack() as ctx:
        def sb(name, shape, dt=F32):
            return ctx.enter_context(nc.sbuf_tensor(name, shape, dt))

        def bank(name):
            return ctx.enter_context(nc.psum_tensor(name, [P, 512], F32))

        xs = sb("xs", [P, 2, QT, D])
        xr = sb("xr", [P, 2, QT, D])
        bn = sb("bn", [P, 2, 6])
        mean_var = sb("mean_var", [P, 2, 2])
        rstd = sb("rstd", [P, 2, 1])
        var_eps = sb("var_eps", [P, 1])
        neg_half = sb("neg_half", [P, 1])
        xhat = sb("xhat", [P, D])
        h_t = sb("h_t", [P, KC, P])
        rot_a = sb("rot_a", [P, 2 * D])
        rot_b = sb("rot_b", [P, 2 * D])
        rot = sb("rot", [P, 2 * D])
        q_aug = sb("q_aug", [P, 2, QT, H * HW], F16)
        k_aug = sb("k_aug", [P, H * HW], F16)
        q_t = sb("q_t", [P, 2, H // 2, S], F16)
        k_t = sb("k_t", [P, 2, 2, H // 2, S], F16)
        v_sb = sb("v_sb", [P, 2, QT, H, 32])
        prob = sb("prob", [P, 2, P_AT[QT]])
        row_max = sb("row_max", [P, 2, QT, HG])
        u_sb = sb("u_sb", [P, 2, S])
        recip = sb("recip", [P, QT, HG])
        att = sb("att", [P, 2, QT, D])
        att_t = sb("att_t", [P, KC, P])
        gated = sb("gated", [P, D])
        w_qkv = sb("w_qkv", [P, KC, 3 * D])
        w_o = sb("w_o", [P, KC, D])
        gate_a = sb("gate_a", [P, B, D])
        cos_t = sb("cos_t", [P, QT, DK])
        sin_t = sb("sin_t", [P, QT, DK])
        bias3 = sb("bias3", [3, 4 * D], BF16)
        ones3 = sb("ones3", [3, P], BF16)
        ident_b = sb("ident_b", [P, P], BF16)
        causal = sb("causal", [P, 2, P], BF16)
        ps_a, ps_b = bank("ps_a"), bank("ps_b")
        ps_max = [bank("ps_max0"), bank("ps_max1")]
        ps_sc = [bank("ps_sc0"), bank("ps_sc1")]
        ps_pv, ps_nd = bank("ps_pv"), bank("ps_nd")

        nat = prob[:, 0, 0:3 * KC * D].rearrange("p (w c i) -> p w c i", w=3, c=KC)
        nat_o = prob[:, 1, 0:KC * D].rearrange("p (c i) -> p c i", c=KC)
        wmod_sb = prob[:, 0, 1536:1536 + KC * 6 * D].rearrange("p (c n) -> p c n", c=KC)
        c_sb = prob[0:B, 1, 512:512 + D]
        c_exp = prob[0:B, 1, 768:768 + D]
        c_silu = prob[0:B, 1, 1024:1024 + D]
        c_t = prob[:, 1, 1280:1280 + KC * B].rearrange("p (c b) -> p c b", c=KC)
        mod_r = prob[0:B, 1, 1536:1536 + 2 * D].rearrange("p (g d) -> p g d", g=2)
        mod_s = prob[0:B, 1, 2048:2048 + 2 * D].rearrange("p (g d) -> p g d", g=2)
        mod_m = prob[0:B, 1, 2560:2560 + 2 * D].rearrange("p (g d) -> p g d", g=2)
        row_sel = prob[0:B, 1, 3072:3072 + B * P].rearrange("p (b m) -> p b m", b=B)
        bias_rest = prob[0:1, 1, 4096:4096 + 4 * D]
        bias_f = u_sb[0:1, :, :].rearrange("p a s -> p (a s)")[:, 0:4 * D]
        bias_parts = att[0:1, :, :, :].rearrange("p a t d -> p (a t d)")[:, 0:12 * D // 2].bitcast(BF16)

        x_v = x.rearrange("b (t p) d -> b p t d", p=P)
        x1_v = x1_dram.rearrange("(b t p) d -> b p t d", t=QT, p=P)

        xs_loaded = [sem("xs_loaded0"), sem("xs_loaded1")]
        xr_loaded = [sem("xr_loaded0"), sem("xr_loaded1")]
        x1_stored = [sem("x1_stored0"), sem("x1_stored1")]
        w_loaded, mod_loaded, small_loaded = sem("w_loaded"), sem("mod_loaded"), sem("small_loaded")
        bias_spread = sem("bias_spread")
        masks_done = sem("masks_done")
        setup_ps, setup_ev, setup_act, setup_dve, setup_ev2 = (sem("setup_ps"), sem("setup_ev"), sem("setup_act"),
                                                    sem("setup_dve"), sem("setup_ev2"))
        stats_done, rstd_done, xhat_done = sem("stats_done"), sem("rstd_done"), sem("xhat_done")
        mv_done, var_done = sem("mv_done"), sem("var_done")
        xt_ps, ht_done, qk_ps, v_ps = sem("xt_ps"), sem("ht_done"), sem("qk_ps"), sem("v_ps")
        rope_done, rot_done, hi_done, lo_done = (sem("rope_done"), sem("rot_done"), sem("hi_done"),
                                                 sem("lo_done"))
        row_cleared, kt_zeroed, pv0_ps = sem("row_cleared"), sem("kt_zeroed"), sem("pv0_ps")
        kt2_kept = sem("kt2_kept")
        att_tp, att_kept = sem("att_tp"), sem("att_kept")
        v_kept, aug_ps, qt_kept, kt_kept = sem("v_kept"), sem("aug_ps"), sem("qt_kept"), sem("kt_kept")
        max_ps, max_done, negmax_done = sem("max_ps"), sem("max_done"), sem("negmax_done")
        shift_ps, shift_kept = sem("shift_ps"), sem("shift_kept")
        sc_ps, exp_done, masked = sem("sc_ps"), sem("exp_done"), sem("masked")
        pv_ps, u_kept, den_ps = sem("pv_ps"), sem("u_kept"), sem("den_ps")
        recip_done, att_done = sem("recip_done"), sem("att_done")
        dve_turns, pool_turns = sem("dve_turns"), sem("pool_turns")
        o_ps, gated_done, x1_done = sem("o_ps"), sem("gated_done"), sem("x1_done")

        block = ctx.enter_context(nc.Block())

        PAIR = 2 * G
        LOOPS = B // 2 - 1

        def all_units(eng, unit):
            for n in range(G):
                unit(0, n)
            with eng.Fori(0, LOOPS) as i:
                for n in range(G, G + PAIR):
                    unit(i, n)
            for n in range(G, PAIR):
                unit(LOOPS, n)

        def place(n):
            return (n // 4) % 2, n % 4

        def has(i, n):
            return not isinstance(i, int) or PAIR * i + n < NU

        def when(eng, i, n):
            if not isinstance(i, int) and PAIR * (LOOPS - 1) + n >= NU:
                return eng.If(i < LOOPS - 1)
            return nullcontext()

        @block.sync
        def _(sp):
            for n, w in enumerate((wq, wk, wv)):
                sp.dma_start(nat[:, n, :, :], w.rearrange("(c p) i -> p c i", p=P)).then_inc(w_loaded, 16)
            sp.dma_start(c_sb, c).then_inc(mod_loaded, 16)
            sp.dma_start(wmod_sb, wmod.rearrange("(c p) n -> p c n", p=P)).then_inc(mod_loaded, 16)
            for n, b_ in enumerate((bq, bk, bv, bo)):
                sp.dma_start(bias_f[:, n * D:(n + 1) * D], b_.rearrange("(a n) -> a n", a=1)).then_inc(small_loaded, 16)
            sp.dma_start(cos_t[:, :, :], rope_cos.rearrange("(t p) d -> p t d", p=P)).then_inc(small_loaded, 16)
            sp.dma_start(sin_t[:, :, :], rope_sin.rearrange("(t p) d -> p t d", p=P)).then_inc(small_loaded, 16)
            sp.dma_start(nat_o, wo.rearrange("(c p) i -> p c i", p=P)).then_inc(w_loaded, 16)
            for b in range(2):
                sp.dma_start(xs[:, b, :, :], x_v[b]).then_inc(xs_loaded[b], 16)
                sp.dma_start(xr[:, b, :, :], x_v[b]).then_inc(xr_loaded[b], 16)
            sp.wait_ge(setup_dve, 5)
            for n in range(3):
                sp.dma_start(bias3[n:n + 1, :], bias_parts[:, n * 4 * D:(n + 1) * 4 * D]).then_inc(bias_spread, 16)

            def load_xs(b, half):
                sp.wait_ge(xhat_done, QT * (b - 1))
                sp.dma_start(xs[:, half, :, :], x_v[b]).then_inc(xs_loaded[half], 16)

            def swap_xr(b, half, k):
                sp.wait_ge(x1_done, QT * (b - 1))
                sp.dma_start(x1_v[b - 2], xr[:, half, :, :]).then_inc(x1_stored[half], 16)
                sp.wait_ge(x1_stored[half], 16 * k)
                sp.dma_start(xr[:, half, :, :], x_v[b]).then_inc(xr_loaded[half], 16)

            load_xs(2, 0)
            with sp.Fori(1, B // 2 - 1) as k:
                for half in range(2):
                    load_xs(2 * k + half + 1, 1 - half)
                    swap_xr(2 * k + half, half, k)
            load_xs(B - 1, 1)
            for half in range(2):
                swap_xr(B - 2 + half, half, B // 2 - 1)
            for half in range(2):
                b = B - 2 + half
                sp.wait_ge(x1_done, QT * (b + 1))
                sp.dma_start(x1_v[b], xr[:, half, :, :]).then_inc(x1_stored[half], 16)
            for half in range(2):
                sp.wait_ge(x1_stored[half], 16 * (B // 2))

        @block.gpsimd
        def _(pool):
            nc.gpsimd.memset(ident[:, :], 0.0).then_inc(masks_done, 1)
            nc.gpsimd.memset(ident16[:, :], 0.0).then_inc(masks_done, 1)
            nc.gpsimd.memset(ident_b[:, :], 0.0).then_inc(masks_done, 1)
            nc.gpsimd.memset(causal[:, :, :], 0.0).then_inc(masks_done, 1)
            nc.gpsimd.memset(ones3[:, :], 1.0).then_inc(masks_done, 1)
            nc.gpsimd.memset(neg_half[:, :], -0.5).then_inc(masks_done, 1)
            nc.gpsimd.memset(q_aug[:, :, :, :], 0.0).then_inc(masks_done, 1)
            nc.gpsimd.memset(k_aug[:, :], 0.0).then_inc(masks_done, 1)
            nc.gpsimd.memset(v_sb[:, :, :, :, :], 0.0).then_inc(masks_done, 1)
            pool.wait_ge(masks_done, 9)
            for m in (ident, ident16, ident_b):
                nc.gpsimd.affine_select(out=m[:, :], in_=m[:, :], compare_op=ALU.not_equal, fill=1.0, base=0,
                                        pattern=[[-1, P]], channel_multiplier=1).then_inc(masks_done, 1)
            nc.gpsimd.affine_select(out=causal[:, :, :], in_=causal[:, :, :], compare_op=ALU.is_ge, fill=NEG, base=0,
                                    pattern=[[0, 2], [-1, P]], channel_multiplier=1).then_inc(masks_done, 1)
            nc.gpsimd.memset(k_aug[:, :].rearrange("p (h w) -> p h w", w=HW)[:, :, 3 * DK:3 * DK + 1], 1.0).then_inc(masks_done, 1)
            nc.gpsimd.memset(v_sb[:, :, :, :, DK:DK + 1].rearrange("p a t h o -> p (a t) h o"), 1.0).then_inc(masks_done, 1)

            def rstd_of(T):
                pool.wait_ge(var_done, T + 1)
                nc.gpsimd.tensor_tensor(rstd[:, 0, :], var_eps[:, :], neg_half[:, :], ALU.pow).then_inc(rstd_done, 1)

            def rotate(T, par, t):
                pool.wait_ge(rope_done, 3 * T + 3)
                ge(pool, hi_done, 2 * T)
                ge(pool, lo_done, 2 * T)
                nc.gpsimd.tensor_tensor(rot[:, :], rot_a[:, :], rot_b[:, :], ALU.add).then_inc(rot_done, 1)
                q_v = q_aug[:, par, t, :].rearrange("p (h w) -> p h w", w=HW)
                nc.gpsimd.memset(q_v[:, :, 3 * DK:3 * DK + 1], 0.0).then_inc(row_cleared, 1)

            rstd_of(0)
            for T in range(LEAD):
                rstd_of(T + 1)
                rotate(T, *place(T))

            def unit(i, n):
                U = PAIR * i + n
                for kb in range(QT):
                    if kb == 1:
                        if has(i, n + LEAD):
                            with when(pool, i, n + LEAD):
                                rotate(U + LEAD, *place(n + LEAD))
                        if has(i, n + LEAD + 1):
                            with when(pool, i, n + LEAD + 1):
                                rstd_of(U + LEAD + 1)
                    pool.wait_ge(exp_done, NSHOT * U + EXP_UPTO[kb])
                    pool.sem_inc(pool_turns, 1)
                    diag = prob[:, n % 2, P_AT[kb]:P_AT[kb + 1]].rearrange("p (h q) -> p h q", h=HG)[:, :, 0:P]
                    nc.gpsimd.affine_select(out=diag, in_=diag, compare_op=ALU.is_ge, fill=0.0, base=0,
                                            pattern=[[0, HG], [1, P]], channel_multiplier=-1).then_inc(masked, 1)

            all_units(pool, unit)

        @block.tensor
        def _(pe):
            mm = nc.tensor.matmul
            pe.wait_ge(masks_done, 15)
            pe.wait_ge(w_loaded, 16 * 4)
            step = [0]

            def evacuated():
                step[0] += 1
                ge(pe, setup_ev, step[0] - 1)

            for w in (*(nat[:, n, :, :] for n in range(3)), nat_o):
                evacuated()
                for ic in range(KC):
                    for oc in range(KC):
                        last = nc.tensor.transpose(ps_a[:, (ic * KC + oc) * P:(ic * KC + oc + 1) * P],
                                                   w[:, oc, ic * P:(ic + 1) * P], ident[:, :])
                last.then_inc(setup_ps, 1)
            pe.wait_ge(setup_dve, 2)
            evacuated()
            for k in range(KC):
                last = nc.tensor.transpose(ps_a[:, k * B:(k + 1) * B], c_silu[:, k * P:(k + 1) * P], ident[0:B, 0:B])
            last.then_inc(setup_ps, 1)
            evacuated()
            for n in range(6 * KC):
                for k in range(KC):
                    last = mm(ps_a[:, n * B:(n + 1) * B], wmod_sb[:, k, n * P:(n + 1) * P], c_t[:, k, :],
                              start=(n == 0 and k == 0), stop=(k == KC - 1), skip_group_check=True)
            last.then_inc(setup_ps, 1)
            evacuated()
            for n, part in enumerate((2, 5)):
                for k in range(KC):
                    last = mm(ps_a[0:B, n * D:(n + 1) * D], c_t[:, k, :], wmod_sb[:, k, part * D:(part + 1) * D],
                              start=(n == 0 and k == 0), stop=(k == KC - 1), skip_group_check=True)
            last.then_inc(setup_ps, 1)
            pe.wait_ge(setup_dve, 9)
            for b in range(B):
                evacuated()
                last = mm(ps_a[:, :], row_sel[:, b, :], mod_r.rearrange("p g d -> p (g d)"), start=True, stop=True)
                last.then_inc(setup_ps, 1)
            pe.wait_ge(setup_ev, step[0])
            pe.wait_ge(bias_spread, 48)

            def x_transposes(T):
                pe.wait_ge(xhat_done, T + 1)
                ge(pe, kt_kept, T)
                ge(pe, kt2_kept, T)
                for k in range(KC):
                    last = nc.tensor.transpose(ps_a[:, k * P:(k + 1) * P], xhat[:, k * P:(k + 1) * P], ident[:, :])
                last.then_inc(xt_ps, 1)

            def project_qk(T, k):
                if k == 0:
                    pe.wait_ge(ht_done, KC * T + KC)
                    ge(pe, qt_kept, T)
                    mm(ps_b[:, :], ones3[:, :], bias3[:, 0:2 * D], start=True, stop=False)
                last = mm(ps_b[:, :], h_t[:, k, :], w_qkv[:, k, 0:2 * D], start=False, stop=(k == KC - 1))
                if k == KC - 1:
                    last.then_inc(qk_ps, 1)

            def project_v(T):
                mm(ps_a[:, 0:D], ones3[:, :], bias3[:, 2 * D:3 * D], start=True, stop=False)
                for k in range(KC):
                    last = mm(ps_a[:, 0:D], h_t[:, k, :], w_qkv[:, k, 2 * D:3 * D], start=False, stop=(k == KC - 1))
                last.then_inc(v_ps, 1)

            def q_transposes(T, par, t):
                pe.wait_ge(hi_done, 2 * T + 2)
                pe.wait_ge(lo_done, 2 * T + 2)
                pe.wait_ge(row_cleared, T + 1)
                for m in range(H // 2):
                    last = nc.tensor.transpose(ps_b[:, :].bitcast(F16)[:, m * P:(m + 1) * P],
                                               q_aug[:, par, t, m * P:(m + 1) * P], ident16[:, :])
                last.then_inc(aug_ps, 1)

            def k_transposes(T):
                pe.wait_ge(v_kept, T + 1)
                for m in range(H // 2):
                    last = nc.tensor.transpose(ps_a[:, :].bitcast(F16)[:, m * P:(m + 1) * P],
                                               k_aug[:, m * P:(m + 1) * P], ident16[:, :])
                last.then_inc(aug_ps, 1)

            def max_scores(V, par, g, s):
                qt, first, n, j = MAX_SHOTS[s]
                L = P * (qt + 1)
                if s == 0:
                    if g == 0:
                        pe.wait_ge(qt_kept, V + 4)
                        pe.wait_ge(kt_kept, V + 4)
                        pe.wait_ge(kt2_kept, V + 4)
                ge(pe, max_done, NSHOT * V + s - 1)
                for m in range(n):
                    mm(ps_max[j][:, m * L:(m + 1) * L], q_t[:, par, 2 * g + first + m, qt * P:(qt + 1) * P],
                       k_t[:, par, j, 2 * g + first + m, 0:L], start=(m == 0), stop=False,
                       skip_group_check=True)
                o = ps_max[j][:, 0:n * L].rearrange("p (m l) -> p m l", m=n)[:, :, L - P:L]
                mm(o, ident_b[:, :], causal[:, 0:n, :], start=False, stop=True,
                   skip_group_check=True).then_inc(max_ps, 1)

            def shift_rows(V, par, g):
                pe.wait_ge(negmax_done, V + 1)
                ge(pe, exp_done, NSHOT * V - 1)
                for m in range(2):
                    for qt in range(QT):
                        at = (m * QT + qt) * P
                        last = nc.tensor.transpose(ps_sc[0][:, :].bitcast(F16)[:, at:at + P],
                                                   q_aug[:, par, qt, (2 * g + m) * P:(2 * g + m + 1) * P],
                                                   ident16[:, :])
                last.then_inc(shift_ps, 1)

            def scores(U, par, g, s):
                kb, first, n, j = EXP_SHOTS[s]
                L = S - P * kb
                if s == 0:
                    pe.wait_ge(shift_kept, U + 1)
                if s >= 2:
                    pe.wait_ge(exp_done, NSHOT * U + s - 1)
                for m in range(n):
                    last = mm(ps_sc[j][:, m * L:(m + 1) * L], k_t[:, par, j, 2 * g + first + m, kb * P:(kb + 1) * P],
                              q_t[:, par, 2 * g + first + m, kb * P:S], start=(m == 0), stop=(m == n - 1),
                              skip_group_check=True)
                last.then_inc(sc_ps, 1)

            def weigh(U, half, par, g, kb):
                pe.wait_ge(masked, QT * U + kb + 1)
                L = S - P * kb
                p_kb = prob[:, half, P_AT[kb]:P_AT[kb + 1]].rearrange("p (j m q) -> p j m q", j=2, m=2)
                for m in range(2):
                    for j in range(2):
                        col = 2 * m + j
                        last = mm(ps_pv[32 * col:32 * col + 32, kb * P:S], v_sb[:, par, kb, HG * g + col, :],
                                  p_kb[:, j, m, :], start=(kb == 0), stop=(kb == QT - 1), skip_group_check=True)
                if kb == 0:
                    last.then_inc(pv0_ps, 1)
                if kb == QT - 1:
                    last.then_inc(pv_ps, 1)

            def tokens_first(W, half, x1_before):
                pe.wait_ge(u_kept, W + 1)
                ge(pe, att_done, W)
                if x1_before is not None:
                    ge(pe, x1_done, x1_before)
                for qt in range(QT):
                    last = nc.tensor.transpose(ps_nd[:, qt * P:(qt + 1) * P], u_sb[:, half, qt * P:(qt + 1) * P], ident[:, :])
                last.then_inc(den_ps, 1)

            def att_transposes(X, par, t, units):
                pe.wait_ge(att_done, units)
                if isinstance(X, int):
                    ge(pe, x1_done, X)
                for k in range(KC):
                    last = nc.tensor.transpose(ps_nd[:, k * P:(k + 1) * P], att[:, par, t, k * P:(k + 1) * P], ident[:, :])
                last.then_inc(att_tp, 1)

            def project_out(X):
                pe.wait_ge(att_kept, X + 1)
                o = ps_nd[:, KC * P:KC * P + D]
                mm(o, ones3[:, :], bias3[:, 3 * D:4 * D], start=True, stop=False, skip_group_check=True)
                for k in range(KC):
                    last = mm(o, att_t[:, k, :], w_o[:, k, :], start=False, stop=(k == KC - 1), skip_group_check=True)
                last.then_inc(o_ps, 1)

            for T in range(LEAD):
                x_transposes(T)
                for k in range(KC):
                    project_qk(T, k)
                project_v(T)
                q_transposes(T, *place(T))
                k_transposes(T)
            for s in range(NSHOT):
                max_scores(0, 0, 0, s)
            shift_rows(0, 0, 0)

            def unit(i, n):
                U = PAIR * i + n
                par, g = place(n)
                T, V, X = U + LEAD, U + 1, U - 4
                has_t, has_v, has_x = has(i, n + LEAD), has(i, n + 1), not isinstance(i, int) or U >= QT
                if has_t:
                    with when(pe, i, n + LEAD):
                        x_transposes(T)
                for s in range(NSHOT):
                    if has_v:
                        max_scores(V, *place(n + 1), s)
                    scores(U, par, g, s)
                    if s < KC and has_t:
                        with when(pe, i, n + LEAD):
                            project_qk(T, s)
                    if s == 2 and (n or not isinstance(i, int) or i):
                        tokens_first(U - 1, (n - 1) % 2, None if n == G and not isinstance(i, int) else U - 4 if has_x else 0)
                    if s == 3 and has_t:
                        with when(pe, i, n + LEAD):
                            project_v(T)
                    if s == 4 and has_x:
                        att_transposes(X, *place(n + 4), U)
                    if s == 5:
                        weigh(U, n % 2, par, g, 0)
                    if s == 6 and has_x:
                        project_out(X)
                    if s == 9:
                        weigh(U, n % 2, par, g, 1)
                    if s == 10 and has_t:
                        with when(pe, i, n + LEAD):
                            q_transposes(T, *place(n + LEAD))
                            k_transposes(T)
                weigh(U, n % 2, par, g, 2)
                if has_v:
                    shift_rows(V, *place(n + 1))
                weigh(U, n % 2, par, g, 3)

            all_units(pe, unit)
            tokens_first(NU - 1, (NU - 1) % 2, NU - 4)
            for X in range(NT - QT, NT):
                att_transposes(X, *place(X), NU)
                project_out(X)

        @block.scalar
        def _(act):
            act.wait_ge(mod_loaded, 32)
            nc.scalar.activation(c_exp, c_sb, ACT.Exp, scale=-1.0).then_inc(setup_act, 1)

            def keep_v(T, par, t, after_unit):
                act.wait_ge(v_ps, T + 1)
                if after_unit is not None:
                    act.wait_ge(pv0_ps, after_unit + 1)
                nc.scalar.activation(v_sb[:, par, t, :, 0:DK], ps_a[:, 0:D].rearrange("p (h d) -> p h d", h=H),
                                     ACT.Copy).then_inc(v_kept, 1)

            def hi_parts(T, par, t):
                act.wait_ge(rot_done, T + 1)
                r = rot[:, :].rearrange("p (w h d) -> p w h d", w=2, h=H)
                q_v = q_aug[:, par, t, :].rearrange("p (h w) -> p h w", w=HW)[:, :, 0:4 * DK]
                q_v = q_v.rearrange("p h (a d) -> p h a d", d=2 * DK)[:, :, :, 0:DK]
                k_v = k_aug[:, :].rearrange("p (h w) -> p h w", w=HW)[:, :, 0:2 * DK].rearrange("p h (a d) -> p h a d", a=2)
                for w, v in ((0, q_v), (1, k_v)):
                    nc.scalar.activation(v, r[:, w, :, None, :].to_broadcast([P, H, 2, DK]), ACT.Copy).then_inc(hi_done, 1)

            def keep_kt(T, par, t):
                act.wait_ge(aug_ps, 2 * T + 2)
                nc.scalar.activation(k_t[0:HW, par, 0, :, t * P:(t + 1) * P],
                                     ps_a[0:HW, :].bitcast(F16).rearrange("p (m q) -> p m q", q=P), ACT.Copy).then_inc(kt_kept, 1)

            def keep_att(X):
                act.wait_ge(att_tp, X + 1)
                nc.scalar.activation(att_t[:, :, :].rearrange("p k m -> p (k m)"), ps_nd[:, 0:KC * P], ACT.Copy).then_inc(att_kept, 1)

            def keep_shift(V, par, g):
                act.wait_ge(shift_ps, V + 1)
                nc.scalar.activation(q_t[:, par, 2 * g:2 * g + 2, :],
                                     ps_sc[0][:, :].bitcast(F16).rearrange("p (m q) -> p m q", m=2), ACT.Copy).then_inc(shift_kept, 1)

            def exps(U, half, s):
                kb, first, n, j = EXP_SHOTS[s]
                L = S - P * kb
                act.wait_ge(sc_ps, NSHOT * U + s + 1)
                a = P_AT[kb] + (2 * j + first) * L
                nc.scalar.activation(prob[:, half, a:a + n * L], ps_sc[j][:, 0:n * L], ACT.Exp,
                                     scale=SCALE).then_inc(exp_done, 1)

            def keep_u(U, half):
                act.wait_ge(pv_ps, U + 1)
                nc.scalar.activation(u_sb[:, half, :], ps_pv[:, :], ACT.Copy).then_inc(u_kept, 1)

            act.wait_ge(kt_zeroed, 4)
            for T in range(LEAD):
                keep_v(T, *place(T), None)
                hi_parts(T, *place(T))
                keep_kt(T, *place(T))
            keep_shift(0, 0, 0)

            def unit(i, n):
                U = PAIR * i + n
                par, g = place(n)
                T, V, X = U + LEAD, U + 1, U - 4
                has_t, has_v, has_x = has(i, n + LEAD), has(i, n + 1), not isinstance(i, int) or U >= QT
                for s in range(NSHOT):
                    exps(U, n % 2, s)
                    if s == 4 and has_x:
                        keep_att(X)
                    if s == 6 and has_t:
                        with when(act, i, n + LEAD):
                            keep_v(T, *place(n + LEAD), U if g == G - 1 else None)
                    if s == 7 and has_t:
                        with when(act, i, n + LEAD):
                            hi_parts(T, *place(n + LEAD))
                if has_t:
                    with when(act, i, n + LEAD):
                        keep_kt(T, *place(n + LEAD))
                if has_v:
                    keep_shift(V, *place(n + 1))
                keep_u(U, n % 2)

            all_units(act, unit)
            for X in range(NT - QT, NT):
                keep_att(X)

        @block.vector
        def _(dve):
            for par in range(2):
                for j in range(2):
                    rows = slice(HW * (1 - j), HW * (2 - j))
                    nc.vector.memset(k_t[rows, par, j, :, :].rearrange("p m s -> p (m s)").bitcast(F32), 0.0).then_inc(kt_zeroed, 1)
            dve.wait_ge(small_loaded, 96)
            bias_hi, bias_mid, bias_lo = (bias_parts[:, n * 4 * D:(n + 1) * 4 * D] for n in range(3))
            rest1, rest2 = bias_rest, bias_f

            done = [0]

            def link(ins):
                done[0] += 1
                ins.then_inc(setup_dve, 1)
                dve.wait_ge(setup_dve, done[0])

            dve.wait_ge(setup_act, 1)
            one_plus = mod_s[:, 0, :]
            link(nc.vector.tensor_scalar(c_exp, c_exp, 1.0, None, ALU.add))
            nc.vector.reciprocal(one_plus, c_exp).then_inc(setup_ev2, 1)
            dve.wait_ge(setup_ev2, 1)
            link(nc.vector.tensor_tensor(c_silu, c_sb, one_plus, ALU.mult))
            link(nc.vector.tensor_copy(bias_hi, bias_f))
            link(nc.vector.tensor_tensor(rest1, bias_f, bias_hi, ALU.subtract))
            nc.vector.tensor_copy(bias_mid, rest1).then_inc(setup_ev2, 1)
            dve.wait_ge(setup_ev2, 2)
            nc.vector.tensor_tensor(rest2, rest1, bias_mid, ALU.subtract).then_inc(setup_ev2, 1)
            dve.wait_ge(setup_ev2, 3)
            link(nc.vector.tensor_copy(bias_lo, rest2))

            kept = [0]

            def keep(dst, src):
                nc.vector.tensor_copy(dst, src).then_inc(setup_ev, 1)

            for w in range(3):
                kept[0] += 1
                dve.wait_ge(setup_ps, kept[0])
                keep(w_qkv[:, :, w * D:(w + 1) * D], ps_a[:, :].rearrange("p (i o) -> p i o", i=KC))
            kept[0] += 1
            dve.wait_ge(setup_ps, kept[0])
            keep(w_o[:, :, :], ps_a[:, :].rearrange("p (i o) -> p i o", i=KC))
            kept[0] += 1
            dve.wait_ge(setup_ps, kept[0])
            keep(c_t, ps_a[:, 0:KC * B].rearrange("p (c b) -> p c b", c=KC))
            kept[0] += 1
            dve.wait_ge(setup_ps, kept[0])
            keep(mod_t[:, :, :], ps_a[:, 0:6 * KC * B].rearrange("p (n b) -> p n b", b=B))
            dve.wait_ge(setup_ev, kept[0])
            for part in (1, 4):
                sl = mod_t[:, part * KC:(part + 1) * KC, :]
                link(nc.vector.tensor_scalar(sl, sl, 1.0, None, ALU.add))
            kept[0] += 1
            dve.wait_ge(setup_ps, kept[0])
            keep(mod_r, ps_a[0:B, :].rearrange("p (g d) -> p g d", g=2))
            dve.wait_ge(setup_ev, kept[0])
            nc.vector.tensor_scalar(mod_s, mod_r, 0.0, 2.0, ALU.is_ge, ALU.mult).then_inc(setup_ev2, 1)
            nc.vector.tensor_scalar(mod_m, mod_r, -1.0, None, ALU.mult).then_inc(setup_ev2, 1)
            dve.wait_ge(setup_ev2, 5)
            nc.vector.tensor_tensor(mod_m, mod_m, mod_r, ALU.max).then_inc(setup_ev2, 1)
            dve.wait_ge(setup_ev2, 6)
            nc.vector.tensor_scalar(mod_m, mod_m, ADA_MIN, None, ALU.max).then_inc(setup_ev2, 1)
            dve.wait_ge(setup_ev2, 7)
            link(nc.vector.scalar_tensor_tensor(out=mod_r, in0=mod_s, scalar=-1.0, in1=mod_m, op0=ALU.add, op1=ALU.mult))
            dve.wait_ge(masks_done, 15)
            link(nc.vector.tensor_copy(row_sel, ident[0:B, 0:B, None].to_broadcast([B, B, P])))
            for b in range(B):
                kept[0] += 1
                dve.wait_ge(setup_ps, kept[0])
                nc.vector.tensor_copy(gate_a[:, b, :], ps_a[:, 0:D]).then_inc(setup_ev2, 1)
                keep(gate_b[:, b, :], ps_a[:, D:2 * D])

            def statistics(T, par, t, load_count):
                if t == 0:
                    dve.wait_ge(xs_loaded[par], load_count)
                nc.vector.bn_stats(bn[:, 0, :], xs[:, par, t, :]).then_inc(stats_done, 1)
                dve.wait_ge(stats_done, T + 1)
                dve.sem_inc(dve_turns, 1)
                nc.vector.bn_aggr(mean_var[:, 0, :], bn[:, 0, :]).then_inc(mv_done, 1)
                dve.wait_ge(mv_done, T + 1)
                nc.vector.tensor_scalar(var_eps[:, :], mean_var[:, 0, 1:2], LN_EPS, None, ALU.add).then_inc(var_done, 1)

            def normalise(T, par, t):
                dve.wait_ge(rstd_done, T + 1)
                nc.vector.tensor_scalar(xhat[:, :], xs[:, par, t, :], mean_var[:, 0, 0:1], rstd[:, 0, :],
                                        ALU.subtract, ALU.mult).then_inc(xhat_done, 1)

            def modulate(T, b):
                dve.wait_ge(xt_ps, T + 1)
                for k in range(KC):
                    nc.vector.tensor_scalar(h_t[:, k, :], ps_a[:, k * P:(k + 1) * P],
                                            mod_t[:, KC + k, b], mod_t[:, k, b],
                                            ALU.mult, ALU.add).then_inc(ht_done, 1)

            def rope(T, t):
                dve.wait_ge(qk_ps, T + 1)
                qk = ps_b[:, :].rearrange("p (h d) -> p h d", d=DK)
                nc.vector.tensor_tensor(rot_a[:, :].rearrange("p (h d) -> p h d", d=DK), qk,
                                        cos_t[:, t, None, :].to_broadcast([P, 2 * H, DK]), ALU.mult).then_inc(rope_done, 1)
                qk2 = ps_b[:, :].rearrange("p (h d two) -> p h d two", two=2, d=DK // 2)
                b2 = rot_b[:, :].rearrange("p (h d two) -> p h d two", two=2, d=DK // 2)
                s2 = sin_t[:, t, :].rearrange("p (d two) -> p d two", two=2)
                for e in range(2):
                    nc.vector.tensor_tensor(b2[:, :, :, e], qk2[:, :, :, 1 - e],
                                            s2[:, None, :, e].to_broadcast([P, 2 * H, DK // 2]), ALU.mult).then_inc(rope_done, 1)

            def lo_parts(T, par, t):
                dve.wait_ge(hi_done, 2 * T + 2)
                r = rot[:, :].rearrange("p (w h d) -> p w h d", w=2, h=H)
                q_v = q_aug[:, par, t, :].rearrange("p (h w) -> p h w", w=HW)
                k_v = k_aug[:, :].rearrange("p (h w) -> p h w", w=HW)
                nc.vector.tensor_tensor(q_v[:, :, DK:2 * DK], r[:, 0], q_v[:, :, 0:DK], ALU.subtract).then_inc(lo_done, 1)
                nc.vector.tensor_tensor(k_v[:, :, 2 * DK:3 * DK], r[:, 1], k_v[:, :, 0:DK], ALU.subtract).then_inc(lo_done, 1)

            def keep_qt(T, par, t):
                dve.wait_ge(aug_ps, 2 * T + 1)
                nc.vector.tensor_copy(q_t[:, par, :, t * P:(t + 1) * P],
                                      ps_b[:, :].bitcast(F16).rearrange("p (m q) -> p m q", q=P)).then_inc(qt_kept, 1)

            def keep_kt(T, par, t):
                dve.wait_ge(aug_ps, 2 * T + 2)
                nc.vector.tensor_copy(k_t[HW:P, par, 1, :, t * P:(t + 1) * P],
                                      ps_a[HW:P, :].bitcast(F16).rearrange("p (m q) -> p m q", q=P)).then_inc(kt2_kept, 1)

            def maxima(V, half, s):
                qt, first, n, j = MAX_SHOTS[s]
                L = P * (qt + 1)
                dve.wait_ge(max_ps, NSHOT * V + s + 1)
                dst = row_max[:, half, qt, :].rearrange("p (m j) -> p m j", j=2)[:, first:first + n, j]
                nc.vector.tensor_reduce(dst, ps_max[j][:, 0:n * L].rearrange("p (m l) -> p m l", m=n),
                                        AX.X, ALU.max).then_inc(max_done, 1)

            def negated(V, half, par, g):
                dve.wait_ge(max_done, NSHOT * V + NSHOT)
                q_v = q_aug[:, par, :, :].rearrange("p t (h w) -> p t h w", w=HW)
                nc.vector.tensor_scalar(q_v[:, :, HG * g:HG * (g + 1), 3 * DK], row_max[:, half, :, :],
                                        -1.0, None, ALU.mult).then_inc(negmax_done, 1)

            def divide(W, par, g):
                dve.wait_ge(den_ps, W + 1)
                sums = ps_nd[:, :].rearrange("p (t c d) -> p t c d", t=QT, c=HG)
                nc.vector.reciprocal(recip[:, :, :], sums[:, :, :, DK]).then_inc(recip_done, 1)
                dve.wait_ge(recip_done, W + 1)
                nc.vector.tensor_tensor(att[:, par, :, HG * DK * g:HG * DK * (g + 1)].rearrange("p t (c d) -> p t c d", c=HG),
                                        sums[:, :, :, 0:DK], recip[:, :, :, None].to_broadcast([P, QT, HG, DK]),
                                        ALU.mult).then_inc(att_done, 1)

            def residual(X, b, par, t, load_count):
                if t == 0:
                    dve.wait_ge(xr_loaded[par], load_count)
                dve.wait_ge(o_ps, X + 1)
                gate = gate_a[:, b, :] if isinstance(b, int) else gate_a[:, bass.ds(b, 1), :].rearrange("p b d -> p (b d)")
                nc.vector.tensor_tensor(gated[:, :], ps_nd[:, KC * P:KC * P + D], gate, ALU.mult).then_inc(gated_done, 1)
                dve.wait_ge(gated_done, X + 1)
                nc.vector.tensor_tensor(xr[:, par, t, :], xr[:, par, t, :], gated[:, :], ALU.add).then_inc(x1_done, 1)

            statistics(0, 0, 0, 16)
            normalise(0, 0, 0)
            for T in range(LEAD):
                modulate(T, slice(T // 4, T // 4 + 1))
                statistics(T + 1, *place(T + 1), 16)
                rope(T, T % 4)
                normalise(T + 1, *place(T + 1))
                lo_parts(T, *place(T))
                keep_qt(T, *place(T))
                keep_kt(T, *place(T))
            for s in range(NSHOT):
                maxima(0, 0, s)
            negated(0, 0, 0, 0)

            def unit(i, n):
                U = PAIR * i + n
                par, g = place(n)
                T, V, X = U + LEAD, U + 1, U - 4
                has_t, has_v, has_x = has(i, n + LEAD), has(i, n + 1), not isinstance(i, int) or U >= QT
                if has_t:
                    with when(dve, i, n + LEAD):
                        b_t = 2 * i + (n + LEAD) // 4
                        if not isinstance(i, int):
                            b_t = nc.s_assert_within(b_t, 0, B - 1, skip_runtime_bounds_check_because="left out behind the end")
                        modulate(T, bass.ds(b_t, 1))
                for s in range(NSHOT):
                    if has_v:
                        maxima(V, (n + 1) % 2, s)
                    if s == 3 and (n or not isinstance(i, int) or i):
                        divide(U - 1, *place(n + 7))
                    if s == 2 and has_t:
                        with when(dve, i, n + LEAD):
                            rope(T, (n + LEAD) % 4)
                    if s == 5 and has(i, n + LEAD + 1):
                        with when(dve, i, n + LEAD + 1):
                            statistics(T + 1, *place(n + LEAD + 1), 16 * (i + (n + LEAD + 1) // PAIR + 1))
                    if s == 7:
                        if has_x:
                            residual(X, 2 * i + n // 4 - 1, *place(n + 4), 16 * (i + (n // 4 - 1) // 2 + 1))
                        if has(i, n + LEAD + 1):
                            with when(dve, i, n + LEAD + 1):
                                normalise(T + 1, *place(n + LEAD + 1))
                    if s == 8 and has_t:
                        with when(dve, i, n + LEAD):
                            lo_parts(T, *place(n + LEAD))
                if has_v:
                    negated(V, (n + 1) % 2, *place(n + 1))
                if has_t:
                    with when(dve, i, n + LEAD):
                        keep_qt(T, *place(n + LEAD))
                        keep_kt(T, *place(n + LEAD))

            all_units(dve, unit)
            divide(NU - 1, *place(NU - 1))
            for X in range(NT - QT, NT):
                residual(X, B - 1, *place(X), 16 * (B // 2))


def route_part(nc, sem, x1_dram, xs_dram, w1, b1, w2, b2, switch_w, switch_b, logits, mod_t, ident,
               w1_hi, w1_lo, w2_hi, w2_lo, b1_t, b2_parts, slot, gate_p, tile_e):
    with ExitStack() as ctx:
        def sb(name, shape, dt=F32):
            return ctx.enter_context(nc.sbuf_tensor(name, shape, dt))

        def bank(name):
            return ctx.enter_context(nc.psum_tensor(name, [P, 512], F32))

        rows = sb("rows", [P, NT, 2 * D], F16)
        x1 = sb("x1", [P, 2, QT, D])
        raw1 = sb("raw1", [P, KC, F])
        raw2 = sb("raw2", [P, F // P, D])
        zero = sb("zero", [P, 2 * D], F16)
        bn = sb("bn2", [P, 6])
        mean_var = sb("mean_var2", [P, 2])
        var_eps = sb("var_eps2", [P, 1])
        neg_half = sb("neg_half2", [P, 1])
        rstd = sb("rstd2", [P, 1])
        xhat = sb("xhat2", [P, D])
        h_t = sb("h_t2", [P, 2, KC, P])
        sw = sb("sw", [P, KC, E])
        sw_b = sb("sw_b", [P, E])
        b1_nat = sb("b1_nat", [E * F // P, P])
        ps_xt, ps_row, ps_logit = bank("ps_xt"), [bank("ps_row0"), bank("ps_row1")], bank("ps_logit")
        ps_rank = bank("ps_rank")
        scr = [raw1[:, k, n * NT * E:(n + 1) * NT * E].rearrange("p (t e) -> p t e", e=E)
               for k in range(KC) for n in range(4)]
        onehot, tmp, cum_a, cum_b, within, iota_e, shifted, _ = scr
        jcmp = raw2[:, 0, 0:E * NT].rearrange("p (e j) -> p e j", e=E)
        iota_j = raw2[:, 1, 0:NT]
        iota_i = raw2[:, 2, 0:NSLOT_T]
        ecmp = raw2[:, 3:5, :].rearrange("p a b -> p (a b)")[:, 0:NSLOT_T * E].rearrange("p (j e) -> p j e", e=E)
        before = raw2[:, 5, 0:P]
        ones = raw2[:, 5, P:2 * P]
        small = raw2[:, 6, :]
        top, denom, prob_max, first = (small[:, n * NT:(n + 1) * NT] for n in range(4))
        tiles_of, tiles_a, tiles_b, start_of = (small[:, 128 + n * E:128 + (n + 1) * E] for n in range(4))
        slot_f = small[:, 160:160 + NT]
        expert_f = small[:, 192:192 + NSLOT_T]

        lead = rows[0:1, :, :].rearrange("p t d -> p (t d)")
        b2_f = lead[:, 0:2 * E * D].bitcast(F32)
        b2_rest = lead[:, 2 * E * D:4 * E * D].bitcast(F32)
        b2_s = lead[:, 4 * E * D:7 * E * D].bitcast(BF16)

        x1_v = x1_dram.rearrange("(b t p) d -> b p t d", t=QT, p=P)
        w1_v = w1.rearrange("e (c p) f -> e p c f", p=P)
        w2_v = w2.rearrange("e (f p) d -> e p f d", p=P)

        x1_loaded = [sem("c_x1_loaded0"), sem("c_x1_loaded1")]
        zero_done, cleared = sem("c_zero_done"), sem("c_cleared")
        raw1_loaded, raw2_loaded = sem("raw1_loaded"), sem("raw2_loaded")
        w_hi_done, w_lo_done = sem("w_hi_done"), sem("w_lo_done")
        small_in, b2_spread = sem("c_small_in"), sem("b2_spread")
        turns = sem("c_turns")
        b1_ps, b1_kept = sem("b1_ps"), sem("b1_kept")
        b2_mid, b2_split, b2_split_in = sem("b2_mid"), sem("b2_split"), sem("b2_split_in")
        stats, mv, var, rs, xh = sem("c_stats"), sem("c_mv"), sem("c_var"), sem("c_rstd"), sem("c_xhat")
        xt_ps, ht_done, row_ps, logit_ps = sem("c_xt_ps"), sem("c_ht_done"), sem("c_row_ps"), sem("c_logit_ps")
        hi_done, lo_done, logit_kept = sem("c_hi_done"), sem("c_lo_done"), sem("c_logit_kept")
        iotas, chain, shifted_done, exp_done, rank_ps = (sem("c_iotas"), sem("c_chain"), sem("c_shifted"),
                                                         sem("c_exp"), sem("c_rank_ps"))
        onehot_done, slots_done, scattered = sem("c_onehot"), sem("c_slots"), sem("c_scattered")

        block = ctx.enter_context(nc.Block())

        @block.sync
        def _(sp):
            sp.dma_start(sw[:, :, :], switch_w.rearrange("(c p) e -> p c e", p=P)).then_inc(small_in, 16)
            sp.dma_start(sw_b[:, :], switch_b.partition_broadcast(P)).then_inc(small_in, 16)
            sp.dma_start(b1_nat[:, :], b1.rearrange("e (f p) -> (e f) p", p=P)).then_inc(small_in, 16)
            sp.dma_start(b2_f, b2.rearrange("(a e) d -> a (e d)", a=1)).then_inc(b2_split_in, 16)
            for b in range(2):
                sp.dma_start(x1[:, b, :, :], x1_v[b]).then_inc(x1_loaded[b], 16)
            sp.dma_start(raw1[:, :, :], w1_v[0]).then_inc(raw1_loaded, 16)
            sp.dma_start(raw2[:, :, :], w2_v[0]).then_inc(raw2_loaded, 16)
            sp.wait_ge(zero_done, 2)
            sp.dma_start(xs_dram.rearrange("(n p) d -> p n d", p=P),
                         zero[:, None, :].to_broadcast([P, NSLOT_T, 2 * D])).then_inc(cleared, 16)
            sp.wait_ge(b2_split, 3)
            for n in range(3):
                sp.dma_start(b2_parts[n:n + 1, :], b2_s[:, n * E * D:(n + 1) * E * D]).then_inc(b2_spread, 16)

            def load_expert(e):
                sp.wait_ge(w_hi_done, 2 * e - 1)
                sp.wait_ge(w_lo_done, 2 * e - 1)
                sp.dma_start(raw1[:, :, :], w1_v[e]).then_inc(raw1_loaded, 16)
                sp.wait_ge(w_hi_done, 2 * e)
                sp.wait_ge(w_lo_done, 2 * e)
                sp.dma_start(raw2[:, :, :], w2_v[e]).then_inc(raw2_loaded, 16)

            load_expert(1)
            with sp.Fori(1, B // 2) as k:
                for half in range(2):
                    b = 2 * k + half
                    sp.wait_ge(xh, QT * (b - 1))
                    sp.dma_start(x1[:, half, :, :], x1_v[b]).then_inc(x1_loaded[half], 16)
                    load_expert(b)
            sp.wait_ge(cleared, 16)

        @block.gpsimd
        def _(pool):
            nc.gpsimd.memset(zero[:, :], 0.0).then_inc(zero_done, 1)
            nc.gpsimd.memset(neg_half[:, :], -0.5).then_inc(zero_done, 1)
            pool.wait_ge(zero_done, 2)
            with pool.Fori(0, B) as b:
                for t in range(QT):
                    pool.wait_ge(var, QT * b + t + 1)
                    nc.gpsimd.tensor_tensor(rstd[:, :], var_eps[:, :], neg_half[:, :], ALU.pow).then_inc(rs, 1)
            pool.wait_ge(w_hi_done, 2 * E)
            pool.wait_ge(w_lo_done, 2 * E)
            nc.gpsimd.iota(iota_e, pattern=[[0, NT], [1, E]], base=-E, channel_multiplier=0,
                           allow_small_or_imprecise_dtypes=True).then_inc(iotas, 1)
            nc.gpsimd.iota(iota_j, pattern=[[P, NT]], base=0, channel_multiplier=0,
                           allow_small_or_imprecise_dtypes=True).then_inc(iotas, 1)
            nc.gpsimd.iota(iota_i, pattern=[[1, NSLOT_T]], base=0, channel_multiplier=0,
                           allow_small_or_imprecise_dtypes=True).then_inc(iotas, 1)
            nc.gpsimd.memset(ones, 1.0).then_inc(iotas, 1)
            nc.gpsimd.memset(before, 1.0).then_inc(iotas, 1)
            pool.wait_ge(iotas, 5)
            nc.gpsimd.affine_select(out=before, in_=before, compare_op=ALU.is_gt, fill=0.0, base=0,
                                    pattern=[[1, P]], channel_multiplier=-1).then_inc(iotas, 1)
            pool.wait_ge(slots_done, 1)
            pool.wait_ge(cleared, 16)
            pool.wait_ge(hi_done, NT)
            pool.wait_ge(lo_done, NT)
            for T in range(NT):
                nc.gpsimd.indirect_dma_start(xs_dram, bass.IndirectOffsetOnAxis(ap=slot[:, T:T + 1], axis=0),
                                             rows[:, T, :], None).then_inc(scattered, 16)
            pool.wait_ge(scattered, 16 * NT)

        @block.tensor
        def _(pe):
            mm = nc.tensor.matmul
            pe.wait_ge(small_in, 48)
            nc.tensor.transpose(ps_rank[:, 0:E * F // P], b1_nat[:, :], ident[0:E * F // P, 0:E * F // P]).then_inc(b1_ps, 1)
            with pe.Fori(0, B) as b:
                for t in range(QT):
                    T = QT * b + t
                    pe.wait_ge(xh, T + 1)
                    for k in range(KC):
                        last = nc.tensor.transpose(ps_xt[:, k * P:(k + 1) * P], xhat[:, k * P:(k + 1) * P], ident[:, :])
                    last.then_inc(xt_ps, 1)
                    pe.wait_ge(ht_done, KC * T + KC)
                    if t >= 2:
                        pe.wait_ge(lo_done, T - 1)
                        pe.wait_ge(hi_done, T - 1)
                    for k in range(KC):
                        last = nc.tensor.transpose(ps_row[t % 2][:, k * P:(k + 1) * P], h_t[:, t % 2, k, :], ident[:, :])
                    last.then_inc(row_ps, 1)
                    if t:
                        pe.wait_ge(logit_kept, T)
                    for k in range(KC):
                        last = mm(ps_logit[:, 0:E], h_t[:, t % 2, k, :], sw[:, k, :], start=(k == 0), stop=(k == KC - 1))
                    last.then_inc(logit_ps, 1)
                pe.wait_ge(logit_kept, QT * b + QT)
                pe.wait_ge(lo_done, QT * b + QT)
            pe.wait_ge(iotas, 6)
            pe.wait_ge(onehot_done, 1)
            pe.wait_ge(b1_kept, 1)
            flat = onehot.rearrange("p t e -> p (t e)")
            mm(ps_rank[:, 0:NT * E], before, flat, start=True, stop=True)
            mm(ps_rank[:, NT * E:2 * NT * E], ones, flat, start=False, stop=True, skip_group_check=True).then_inc(rank_ps, 1)

        @block.scalar
        def _(act):
            act.wait_ge(b1_ps, 1)
            nc.scalar.activation(b1_t[:, :, :].rearrange("p e f -> p (e f)"), ps_rank[:, 0:E * F // P], ACT.Copy).then_inc(b1_kept, 1)
            act.wait_ge(b2_spread, 48)
            with act.Fori(0, B) as b:
                act.wait_ge(raw1_loaded, 16 * b + 16)
                nc.scalar.activation(w1_hi[:, bass.ds(b, 1), :, :].rearrange("p e c f -> p (e c) f"), raw1[:, :, :],
                                     ACT.Copy, scale=W_SCALE).then_inc(w_hi_done, 1)
                act.wait_ge(raw2_loaded, 16 * b + 16)
                nc.scalar.activation(w2_hi[:, bass.ds(b, 1), :, :].rearrange("p e c f -> p (e c) f"), raw2[:, :, :],
                                     ACT.Copy, scale=W_SCALE).then_inc(w_hi_done, 1)
                for t in range(QT):
                    T = QT * b + t
                    act.wait_ge(row_ps, T + 1)
                    nc.scalar.activation(rows[:, bass.ds(T, 1), 0:D].rearrange("p t d -> p (t d)"), ps_row[t % 2][:, 0:D], ACT.Copy).then_inc(hi_done, 1)
                    act.wait_ge(logit_ps, T + 1)
                    nc.scalar.activation(logits[:, bass.ds(T, 1), :].rearrange("p t d -> p (t d)"), ps_logit[:, 0:E], ACT.Copy).then_inc(logit_kept, 1)
            act.wait_ge(shifted_done, 1)
            nc.scalar.activation(tmp, shifted, ACT.Exp).then_inc(exp_done, 1)

        @block.vector
        def _(dve):
            dve.wait_ge(b2_split_in, 16)
            part = [b2_s[:, n * E * D:(n + 1) * E * D] for n in range(3)]
            nc.vector.tensor_copy(part[0], b2_f).then_inc(b2_split, 1)
            dve.wait_ge(b2_split, 1)
            nc.vector.tensor_tensor(b2_rest, b2_f, part[0], ALU.subtract).then_inc(b2_mid, 1)
            dve.wait_ge(b2_mid, 1)
            nc.vector.tensor_copy(part[1], b2_rest).then_inc(b2_split, 1)
            dve.wait_ge(b2_split, 2)
            nc.vector.tensor_tensor(b2_f, b2_rest, part[1], ALU.subtract).then_inc(b2_mid, 1)
            dve.wait_ge(b2_mid, 2)
            nc.vector.tensor_copy(part[2], b2_f).then_inc(b2_split, 1)
            with dve.Fori(0, B // 2) as i:
                for u in range(2 * QT):
                    T = 2 * QT * i + u
                    par, t = u // QT, u % QT
                    if t == 0:
                        dve.wait_ge(x1_loaded[par], 16 * i + 16)
                    if t % 2 == 1:
                        e = 2 * i + par
                        raw, hi, lo, loaded = ((raw1, w1_hi, w1_lo, raw1_loaded) if t == 1 else
                                               (raw2, w2_hi, w2_lo, raw2_loaded))
                        dve.wait_ge(w_hi_done, 2 * e + (1 if t == 1 else 2))
                        nc.vector.scalar_tensor_tensor(out=lo[:, bass.ds(e, 1), :, :].rearrange("p e c f -> p (e c) f"),
                                                       in0=raw[:, :, :], scalar=W_SCALE,
                                                       in1=hi[:, bass.ds(e, 1), :, :].rearrange("p e c f -> p (e c) f"),
                                                       op0=ALU.mult, op1=ALU.subtract).then_inc(w_lo_done, 1)
                    nc.vector.bn_stats(bn[:, :], x1[:, par, t, :]).then_inc(stats, 1)
                    dve.wait_ge(stats, T + 1)
                    dve.sem_inc(turns, 1)
                    nc.vector.bn_aggr(mean_var[:, :], bn[:, :]).then_inc(mv, 1)
                    dve.wait_ge(mv, T + 1)
                    nc.vector.tensor_scalar(var_eps[:, :], mean_var[:, 1:2], LN_EPS, None, ALU.add).then_inc(var, 1)
                    dve.wait_ge(rs, T + 1)
                    nc.vector.tensor_scalar(xhat[:, :], x1[:, par, t, :], mean_var[:, 0:1], rstd[:, :],
                                            ALU.subtract, ALU.mult).then_inc(xh, 1)
                    dve.wait_ge(xt_ps, T + 1)
                    b_ = 2 * i + par
                    for k in range(KC):
                        nc.vector.tensor_scalar(h_t[:, t % 2, k, :], ps_xt[:, k * P:(k + 1) * P],
                                                mod_t[:, 4 * KC + k, bass.ds(b_, 1)], mod_t[:, 3 * KC + k, bass.ds(b_, 1)],
                                                ALU.mult, ALU.add).then_inc(ht_done, 1)
                    dve.wait_ge(hi_done, T + 1)
                    nc.vector.tensor_tensor(rows[:, bass.ds(T, 1), D:2 * D].rearrange("p t d -> p (t d)"), ps_row[t % 2][:, 0:D],
                                            rows[:, bass.ds(T, 1), 0:D].rearrange("p t d -> p (t d)"), ALU.subtract).then_inc(lo_done, 1)

            done = [0]

            def link(ins):
                done[0] += 1
                ins.then_inc(chain, 1)
                dve.wait_ge(chain, done[0])

            tt, ts, red = nc.vector.tensor_tensor, nc.vector.tensor_scalar, nc.vector.tensor_reduce
            dve.wait_ge(logit_kept, NT)
            dve.wait_ge(iotas, 6)
            link(tt(logits[:, :, :], logits[:, :, :], sw_b[:, None, :].to_broadcast([P, NT, E]), ALU.add))
            link(red(top, logits[:, :, :], AX.X, ALU.max))
            top_b = top[:, :, None].to_broadcast([P, NT, E])
            tt(shifted, logits[:, :, :], top_b, ALU.subtract).then_inc(shifted_done, 1)
            link(tt(onehot, logits[:, :, :], top_b, ALU.is_equal))
            link(tt(cum_a, onehot, iota_e, ALU.mult))
            link(red(first, cum_a, AX.X, ALU.min))
            ins = tt(onehot, iota_e, first[:, :, None].to_broadcast([P, NT, E]), ALU.is_equal)
            ins.then_inc(onehot_done, 1)
            dve.wait_ge(exp_done, 1)
            link(red(denom, tmp, AX.X, ALU.add))
            link(nc.vector.reciprocal(prob_max, denom))
            link(ts(gate_p[:, :], prob_max, 1.0 / W_SCALE, None, ALU.mult))
            dve.wait_ge(rank_ps, 1)
            link(nc.vector.tensor_copy(cum_a, ps_rank[:, NT * E:2 * NT * E].rearrange("p (t e) -> p t e", e=E)))
            link(nc.vector.tensor_copy(within, ps_rank[:, 0:NT * E].rearrange("p (t e) -> p t e", e=E)))
            link(tt(within, within, cum_a, ALU.subtract))
            a, b2_ = cum_a, cum_b
            step = 1
            while step < NT:
                nc.vector.tensor_copy(b2_[:, 0:step, :], a[:, 0:step, :]).then_inc(chain, 1)
                done[0] += 1
                link(tt(b2_[:, step:NT, :], a[:, step:NT, :], a[:, 0:NT - step, :], ALU.add))
                a, b2_ = b2_, a
                step *= 2
            link(tt(jcmp, iota_j[:, None, :].to_broadcast([P, E, NT]),
                    a[:, NT - 1, :, None].to_broadcast([P, E, NT]), ALU.is_lt))
            link(red(tiles_of, jcmp, AX.X, ALU.add))
            ta, tb = tiles_of, tiles_a
            step = 1
            while step < E:
                nc.vector.tensor_copy(tb[:, 0:step], ta[:, 0:step]).then_inc(chain, 1)
                done[0] += 1
                link(tt(tb[:, step:E], ta[:, step:E], ta[:, 0:E - step], ALU.add))
                ta, tb = tb, (tiles_b if ta is tiles_of else ta)
                step *= 2
            link(tt(start_of, ta, tiles_of, ALU.subtract))
            link(ts(start_of, start_of, float(P), None, ALU.mult))
            link(tt(ecmp, iota_i[:, :, None].to_broadcast([P, NSLOT_T, E]), ta[:, None, :].to_broadcast([P, NSLOT_T, E]), ALU.is_ge))
            link(red(expert_f, ecmp, AX.X, ALU.add))
            link(ts(tile_e[:, :], expert_f, float(E - 1), None, ALU.min))
            link(tt(within, within, a, ALU.add))
            link(tt(within, within, start_of[:, None, :].to_broadcast([P, NT, E]), ALU.add))
            link(tt(within, within, onehot, ALU.mult))
            link(red(slot_f, within, AX.X, ALU.add))
            nc.vector.tensor_copy(slot[:, :], slot_f).then_inc(slots_done, 1)


def expert_part(nc, sem, x1_dram, xs_dram, ys_dram, gate_b, ident16, w1_hi, w1_lo, w2_hi, w2_lo, b1_t,
                b2_parts, slot, gate_p, tile_e, out):
    with ExitStack() as ctx:
        def sb(name, shape, dt=F32):
            return ctx.enter_context(nc.sbuf_tensor(name, shape, dt))

        def bank(name):
            return ctx.enter_context(nc.psum_tensor(name, [P, 512], F32))

        FC = F // P
        rows = sb("x_rows", [P, 2, 2 * D], F16)
        tok_t = sb("tok_t", [P, 2, 2, KC, P], F16)
        hid = sb("hid", [P, 2, FC, P])
        hid_hi = sb("hid_hi", [P, 2, FC, P], F16)
        hid_lo = sb("hid_lo", [P, 2, FC, P], F16)
        y = sb("y", [P, 2, D])
        scale3 = sb("scale3", [3, P], BF16)
        x1 = sb("x1_last", [P, 2, QT, D])
        back = sb("back", [P, 2, QT, D])
        ps_x = bank("ps_x")
        ps_h = [[bank(f"ps_h{a}{b}") for b in range(2)] for a in range(2)]
        ps_y = [bank("ps_y0"), bank("ps_y1")]

        rows_loaded = [sem("rows_loaded0"), sem("rows_loaded1")]
        scale_done = sem("scale_done")
        x_ps, x_kept, h_ps, gelu_done = sem("f_x_ps"), sem("f_x_kept"), sem("f_h_ps"), sem("f_gelu")
        hi_done, lo_done, y_ps, y_kept = sem("f_hi"), sem("f_lo"), sem("f_y_ps"), sem("f_y_kept")
        y_stored = [sem("y_stored0"), sem("y_stored1")]
        x1_loaded = [sem("l_x1_loaded0"), sem("l_x1_loaded1")]
        gathered = [sem("gathered0"), sem("gathered1")]
        gated, summed = sem("l_gated"), sem("l_summed")
        out_stored = [sem("out_stored0"), sem("out_stored1")]

        xs_v = xs_dram.rearrange("(n p) d -> n p d", p=P)
        ys_v = ys_dram.rearrange("(n p) d -> n p d", p=P)
        x1_v = x1_dram.rearrange("(b t p) d -> b p t d", t=QT, p=P)
        out_v = out.rearrange("b (t p) d -> b p t d", p=P)
        NJ = NSLOT_T - 1

        block = ctx.enter_context(nc.Block())

        def steps(eng, step):
            step(0, 0, first=True)
            with eng.Fori(0, (NJ - 1) // 2) as i:
                for u in range(2):
                    step(2 * i + u + 1, (u + 1) % 2)

        @block.sync
        def _(sp):
            for j in range(2):
                sp.dma_start(rows[:, j, :], xs_v[j]).then_inc(rows_loaded[j], 16)
            for b in range(2):
                sp.dma_start(x1[:, b, :, :], x1_v[b]).then_inc(x1_loaded[b], 16)

            def load_rows(j, half):
                sp.wait_ge(x_ps, j - 1)
                sp.dma_start(rows[:, half, :], xs_v[j]).then_inc(rows_loaded[half], 16)

            def store_y(j, half):
                sp.wait_ge(y_kept, j + 1)
                sp.dma_start(ys_v[j], y[:, half, :]).then_inc(y_stored[half], 16)

            load_rows(2, 0)
            with sp.Fori(1, (NJ - 1) // 2) as k:
                for half in range(2):
                    load_rows(2 * k + half + 1, 1 - half)
                    store_y(2 * k + half - 2, half)
            load_rows(NJ, 1)
            for j in range(NJ - 3, NJ):
                store_y(j, j % 2)
            for b in range(2):
                sp.wait_ge(summed, QT * (b + 1))
                sp.dma_start(out_v[b], x1[:, b, :, :]).then_inc(out_stored[b], 16)
            with sp.Fori(1, B // 2) as k:
                for half in range(2):
                    b = 2 * k + half
                    sp.wait_ge(out_stored[half], 16 * k)
                    sp.dma_start(x1[:, half, :, :], x1_v[b]).then_inc(x1_loaded[half], 16)
                    sp.wait_ge(summed, QT * (b + 1))
                    sp.dma_start(out_v[b], x1[:, half, :, :]).then_inc(out_stored[half], 16)
            for half in range(2):
                sp.wait_ge(out_stored[half], 16 * (B // 2))

        @block.gpsimd
        def _(pool):
            nc.gpsimd.memset(scale3[:, :], W_SCALE).then_inc(scale_done, 1)
            pool.wait_ge(y_stored[0], 16 * ((NJ + 1) // 2))
            pool.wait_ge(y_stored[1], 16 * (NJ // 2))
            for b in range(B):
                if b >= 2:
                    pool.wait_ge(summed, QT * (b - 1))
                for t in range(QT):
                    T = QT * b + t
                    nc.gpsimd.indirect_dma_start(back[:, b % 2, t, :], None, ys_dram,
                                                 bass.IndirectOffsetOnAxis(ap=slot[:, T:T + 1], axis=0)).then_inc(gathered[b % 2], 16)

        @block.tensor
        def _(pe):
            mm = nc.tensor.matmul

            def transposes(j, half, load_count):
                pe.wait_ge(rows_loaded[half], load_count)
                ge(pe, x_kept, j)
                for n in range(2 * KC):
                    last = nc.tensor.transpose(ps_x[:, :].bitcast(F16)[:, n * P:(n + 1) * P],
                                               rows[:, half, n * P:(n + 1) * P], ident16[:, :])
                last.then_inc(x_ps, 1)

            def product1(j, half, e, q):
                if q == 0:
                    pe.wait_ge(x_kept, j + 1)
                for q in (q,):
                    for f in range(q * FC // 2, (q + 1) * FC // 2):
                        o = ps_h[half][q][:, (f % (FC // 2)) * P:(f % (FC // 2) + 1) * P]
                        n = 0
                        for k in range(KC):
                            for w, parts in ((w1_hi, (0, 1)), (w1_lo, (0,))):
                                for part in parts:
                                    last = mm(o, w[:, bass.ds(e, 1), k, f * P:(f + 1) * P].rearrange("p e f -> p (e f)"), tok_t[:, half, part, k, :],
                                              start=(n == 0 and f % (FC // 2) == 0), stop=(n == 3 * KC - 1),
                                              skip_group_check=True)
                                    n += 1
                    last.then_inc(h_ps, 1)

            def product2(j, half, e):
                pe.wait_ge(hi_done, 2 * j + 2)
                pe.wait_ge(lo_done, 2 * j + 2)
                mm(ps_y[half][:, 0:D], scale3[:, :], b2_parts[:, bass.ds(e * D, D)], start=True, stop=False)
                for f in range(FC):
                    for a, w in ((hid_hi, w2_hi), (hid_lo, w2_hi), (hid_hi, w2_lo)):
                        last = mm(ps_y[half][:, 0:D], a[:, half, f, :], w[:, bass.ds(e, 1), f, :].rearrange("p e d -> p (e d)"),
                                  start=False, stop=(f == FC - 1 and w is w2_lo))
                last.then_inc(y_ps, 1)

            pe.wait_ge(scale_done, 1)
            transposes(0, 0, 16)
            e0 = pe.value_load(tile_e[0:1, 0:1], min_val=0, max_val=E - 1)
            product1(0, 0, e0, 0)
            transposes(1, 1, 16)
            product1(0, 0, e0, 1)
            with pe.Fori(0, (NJ - 1) // 2) as i:
                _, e = nc.values_load_multi_w_load_instructions(tile_e[0:1, bass.ds(2 * i, 3)], engines=[mybir.EngineType.PE], min_val=0, max_val=E - 1)
                for u in range(2):
                    j = 2 * i + u + 1
                    product1(j, (u + 1) % 2, e[u + 1], 0)
                    transposes(j + 1, u, 16 * (i + 2))
                    product1(j, (u + 1) % 2, e[u + 1], 1)
                    product2(j - 1, u, e[u])
            e = pe.value_load(tile_e[0:1, NJ - 1:NJ], min_val=0, max_val=E - 1)
            product2(NJ - 1, 0, e)

        @block.scalar
        def _(act):
            def keep_x(j, half):
                act.wait_ge(x_ps, j + 1)
                nc.scalar.activation(tok_t[:, half, :, :, :].rearrange("p a k m -> p (a k m)"),
                                     ps_x[:, :].bitcast(F16)[:, 0:2 * KC * P], ACT.Copy).then_inc(x_kept, 1)

            def gelu(j, half, e):
                for f in range(FC):
                    q = f // (FC // 2)
                    if f % (FC // 2) == 0:
                        act.wait_ge(h_ps, 2 * j + q + 1)
                    ins = nc.scalar.activation(hid[:, half, f, :], ps_h[half][q][:, (f % (FC // 2)) * P:(f % (FC // 2) + 1) * P],
                                               ACT.Gelu_apprx_tanh, bias=b1_t[:, bass.ds(e, 1), f], scale=1.0 / W_SCALE)
                    if f % (FC // 2) == FC // 2 - 1:
                        ins.then_inc(gelu_done, 1)

            keep_x(0, 0)
            e0 = act.value_load(tile_e[0:1, 0:1], min_val=0, max_val=E - 1)
            keep_x(1, 1)
            gelu(0, 0, e0)
            with act.Fori(0, (NJ - 1) // 2) as i:
                for u in range(2):
                    j = 2 * i + u + 1
                    e = act.value_load(tile_e[0:1, bass.ds(j, 1)], min_val=0, max_val=E - 1)
                    keep_x(j + 1, u)
                    gelu(j, (u + 1) % 2, e)

        @block.vector
        def _(dve):
            def halves(j, half):
                for q in range(2):
                    dve.wait_ge(gelu_done, 2 * j + q + 1)
                    sl = slice(q * FC // 2, (q + 1) * FC // 2)
                    nc.vector.tensor_copy(hid_hi[:, half, sl, :], hid[:, half, sl, :]).then_inc(hi_done, 1)
                    dve.wait_ge(hi_done, 2 * j + q + 1)
                    nc.vector.tensor_tensor(hid_lo[:, half, sl, :], hid[:, half, sl, :], hid_hi[:, half, sl, :],
                                            ALU.subtract).then_inc(lo_done, 1)

            def keep_y(j, half):
                dve.wait_ge(y_ps, j + 1)
                nc.vector.tensor_copy(y[:, half, :], ps_y[half][:, 0:D]).then_inc(y_kept, 1)

            halves(0, 0)
            halves(1, 1)
            keep_y(0, 0)
            halves(2, 0)
            keep_y(1, 1)
            with dve.Fori(1, (NJ - 1) // 2) as i:
                for u in range(2):
                    j = 2 * i + u + 1
                    halves(j, (u + 1) % 2)
                    dve.wait_ge(y_stored[u], 16 * i)
                    keep_y(j - 1, u)
            dve.wait_ge(y_stored[0], 16 * ((NJ - 1) // 2))
            keep_y(NJ - 1, 0)
            with dve.Fori(0, B // 2) as i:
                for u in range(2 * QT):
                    par, t = u // QT, u % QT
                    b, T = 2 * i + par, 2 * QT * i + u
                    if t == 0:
                        dve.wait_ge(x1_loaded[par], 16 * i + 16)
                        dve.wait_ge(gathered[par], 16 * QT * (i + 1))
                    nc.vector.scalar_tensor_tensor(out=back[:, par, t, :], in0=back[:, par, t, :],
                                                   scalar=gate_p[:, bass.ds(T, 1)],
                                                   in1=gate_b[:, bass.ds(b, 1), :].rearrange("p b d -> p (b d)"),
                                                   op0=ALU.mult, op1=ALU.mult).then_inc(gated, 1)
                    dve.wait_ge(gated, T + 1)
                    nc.vector.tensor_tensor(x1[:, par, t, :], x1[:, par, t, :], back[:, par, t, :], ALU.add).then_inc(summed, 1)


_INS = {"x": "L0_attn_x", "wq": "L0_attn_Wq", "bq": "L0_attn_bq", "wk": "L0_attn_Wk", "bk": "L0_attn_bk",
        "wv": "L0_attn_Wv", "bv": "L0_attn_bv", "wo": "L0_attn_Wo", "bo": "L0_attn_bo",
        "switch_w": "L0_ffn_switch_w", "switch_b": "L0_ffn_switch_b", "w1": "L0_ffn_w1", "b1": "L0_ffn_b1",
        "w2": "L0_ffn_w2", "b2": "L0_ffn_b2", "c": "L0_c", "wmod": "L0_wmod"}


def rope_tables():
    import numpy as np

    inv_freq = np.float32(1.0) / np.float32(10000.0) ** (np.arange(0, DK, 2, dtype=np.float32) / np.float32(DK))
    angles = (np.arange(S, dtype=np.float32)[:, None] * inv_freq.astype(np.float32)).astype(np.float64)
    sign = np.where(np.arange(DK) % 2 == 0, -1.0, 1.0)
    return (np.repeat(np.cos(angles), 2, axis=1).astype(np.float32),
            (np.repeat(np.sin(angles), 2, axis=1) * sign).astype(np.float32))


def kernel(**inputs):
    import numpy as np
    import concourse.bacc as bacc
    from concourse.bass_utils import run_bass_kernel_spmd

    nc = bacc.Bacc("TRN2", target_bir_lowering=False, num_devices=1)
    arrays = {name: np.ascontiguousarray(inputs[given]) for name, given in _INS.items()}
    arrays["rope_cos"], arrays["rope_sin"] = rope_tables()
    args = [nc.dram_tensor(name, a.shape, mybir.dt.from_np(a.dtype), kind="ExternalInput").ap()
            for name, a in arrays.items()]
    out = nc.dram_tensor("out", (B, S, D), F32, kind="ExternalOutput").ap()
    build(nc, *args, out)
    r = run_bass_kernel_spmd(nc, [arrays], core_ids=[0])
    return r.results[0]["out"]
```

```python
import concourse.bass as bass
from concourse import mybir
from contextlib import ExitStack, nullcontext
from math import prod

F32 = mybir.dt.float32
F16 = mybir.dt.float16
BF16 = mybir.dt.bfloat16
I32 = mybir.dt.int32
ALU = mybir.AluOpType
ACT = mybir.ActivationFunctionType
AX = mybir.AxisListType

B, S, D = 8, 512, 256
H = 16
DK = D // H
P = 128
QT = S // P
NT = B * QT
KC = D // P
E, F = 8, 1024
NSLOT_T = NT + E
W_SCALE = 64.0
HG = 4
G = H // HG
NU = B * G
HW = 64
NEG = -1.0e30
ROUND = 1.5 * 2.0 ** 23
SCALE = 1.0 / DK ** 0.5
LN_EPS = 1e-5
ADA_MIN = 0.25
LEAD = 5

def shots(length):
    out = []
    for blk in range(QT):
        n = min(2, S // length(blk)) if length(blk) * 2 <= S else 1
        for first in range(0, 2, n):
            for j in range(2):
                out.append((blk, first, n, j))
    return out


MAX_SHOTS = shots(lambda qt: P * (qt + 1))
EXP_SHOTS = shots(lambda kb: S - P * kb)
NSHOT = len(MAX_SHOTS)
EXP_UPTO = [1 + max(i for i, s in enumerate(EXP_SHOTS) if s[0] == kb) for kb in range(QT)]
P_AT = [HG * sum(S - P * k for k in range(kb)) for kb in range(QT + 1)]


def ge(eng, sem, count):
    if isinstance(count, int) and count <= 0:
        return
    eng.wait_ge(sem, count)


def build(nc, x, wq, bq, wk, bk, wv, bv, wo, bo, switch_w, switch_b, w1, b1, w2, b2, c, wmod,
          rope_cos, rope_sin, out):
    with ExitStack() as whole:
        sems = {}

        def sem(name):
            if name not in sems:
                sems[name] = whole.enter_context(nc.semaphore(name))
            return sems[name]

        x1_dram = nc.dram_tensor("x1_dram", [B * S, D + 1], F32, kind="Internal").ap()
        h_dram = nc.dram_tensor("h_dram", [B * S, 2 * D], F16, kind="Internal").ap()
        gates_dram = nc.dram_tensor("gates_dram", [2, B * D], F32, kind="Internal").ap()

        def sb(name, shape, dt=F32):
            return whole.enter_context(nc.sbuf_tensor(name, shape, dt))

        logits = sb("logits", [P, NT, E])
        mod_t = sb("mod_t", [P, 6 * KC, B])
        ident = sb("ident", [P, P])
        ident16 = sb("ident16", [P, P], F16)
        attention_part(nc, sem, x, wq, bq, wk, bk, wv, bv, wo, bo, c, wmod, rope_cos, rope_sin,
                       x1_dram, gates_dram, mod_t, ident, ident16)
        w1_hi, w1_lo = (sb(n, [P, E, KC, F], F16) for n in ("w1_hi", "w1_lo"))
        w2_hi, w2_lo = (sb(n, [P, E, F // P, D], F16) for n in ("w2_hi", "w2_lo"))
        b1_t = sb("b1_t", [P, E, F // P])
        b2_parts = sb("b2_parts", [3, E * D], BF16)
        token = sb("token", [P, NSLOT_T], I32)
        gate_row = sb("gate_row", [P, NSLOT_T], I32)
        tile_e = sb("tile_e", [P, NSLOT_T], I32)
        rows = sb("slot_rows", [P, 2, 2 * D], F16)
        slot_x1 = sb("slot_x1", [P, 2, D + 1])
        slot_gate = sb("slot_gate", [P, 2, D])

        def of_slots(table, j):
            return bass.IndirectOffsetOnAxis(ap=table[:, j:j + 1], axis=0)

        def fetch_rows(j):
            nc.gpsimd.indirect_dma_start(rows[:, j % 2, :], None, h_dram, of_slots(token, j), bounds_check=NT * P - 1,
                                         oob_is_err=False).then_inc(sem(f"rows_loaded{j % 2}"), 16)

        def fetch_x1(j):
            nc.gpsimd.indirect_dma_start(slot_x1[:, j % 2, :], None, x1_dram, of_slots(token, j), bounds_check=NT * P - 1,
                                         oob_is_err=False).then_inc(sem(f"x1_fetched{j % 2}"), 16)
            nc.gpsimd.indirect_dma_start(slot_gate[:, j % 2, :], None, gates_dram.rearrange("g (b d) -> (g b) d", d=D),
                                         of_slots(gate_row, j)).then_inc(sem(f"gate_fetched{j % 2}"), 16)

        route_part(nc, sem, x1_dram, h_dram, w1, b1, w2, b2, switch_w, switch_b, logits, mod_t, ident,
                   w1_hi, w1_lo, w2_hi, w2_lo, b1_t, b2_parts, token, gate_row, tile_e, rows, slot_x1, fetch_rows)
        expert_part(nc, sem, ident16, w1_hi, w1_lo, w2_hi, w2_lo, b1_t, b2_parts, token, tile_e,
                    rows, slot_x1, slot_gate, of_slots, fetch_rows, fetch_x1, out)


def attention_part(nc, sem, x, wq, bq, wk, bk, wv, bv, wo, bo, c, wmod, rope_cos, rope_sin,
                   x1_dram, gates_dram, mod_t, ident, ident16):
    with ExitStack() as ctx:
        def sb(name, shape, dt=F32):
            return ctx.enter_context(nc.sbuf_tensor(name, shape, dt))

        def bank(name):
            return ctx.enter_context(nc.psum_tensor(name, [P, 512], F32))

        xs = sb("xs", [P, 2, QT, D])
        xr = sb("xr", [P, 2, QT, D])
        bn = sb("bn", [P, 2, 6])
        mean_var = sb("mean_var", [P, 2, 2])
        rstd = sb("rstd", [P, 2, 1])
        var_eps = sb("var_eps", [P, 1])
        neg_half = sb("neg_half", [P, 1])
        xhat = sb("xhat", [P, D])
        h_t = sb("h_t", [P, KC, P])
        rot_a = sb("rot_a", [P, 2 * D])
        rot_b = sb("rot_b", [P, 2 * D])
        rot = sb("rot", [P, 2 * D])
        q_aug = sb("q_aug", [P, 2, QT, H * HW], F16)
        k_aug = sb("k_aug", [P, H * HW], F16)
        q_t = sb("q_t", [P, 2, H // 2, S], F16)
        k_t = sb("k_t", [P, 2, 2, H // 2, S], F16)
        v_sb = sb("v_sb", [P, 2, QT, H, 32])
        prob = sb("prob", [P, 2, P_AT[QT]])
        row_max = sb("row_max", [P, 2, QT, HG])
        u_sb = sb("u_sb", [P, 2, S])
        recip = sb("recip", [P, QT, HG])
        att = sb("att", [P, 2, QT, D])
        att_t = sb("att_t", [P, KC, P])
        gated = sb("gated", [P, D])
        w_qkv = sb("w_qkv", [P, KC, 3 * D])
        w_o = sb("w_o", [P, KC, D])
        gate_a = sb("gate_a", [P, B, D])
        cos_t = sb("cos_t", [P, QT, DK])
        sin_t = sb("sin_t", [P, QT, DK])
        bias3 = sb("bias3", [3, 4 * D], BF16)
        ones3 = sb("ones3", [3, P], BF16)
        ident_b = sb("ident_b", [P, P], BF16)
        causal = sb("causal", [P, 2, P], BF16)
        ps_a, ps_b = bank("ps_a"), bank("ps_b")
        ps_max = [bank("ps_max0"), bank("ps_max1")]
        ps_sc = [bank("ps_sc0"), bank("ps_sc1")]
        ps_pv, ps_nd = bank("ps_pv"), bank("ps_nd")

        nat = prob[:, 0, 0:3 * KC * D].rearrange("p (w c i) -> p w c i", w=3, c=KC)
        nat_o = prob[:, 1, 0:KC * D].rearrange("p (c i) -> p c i", c=KC)
        wmod_sb = prob[:, 0, 1536:1536 + KC * 6 * D].rearrange("p (c n) -> p c n", c=KC)
        c_sb = prob[0:B, 1, 512:512 + D]
        c_exp = prob[0:B, 1, 768:768 + D]
        c_silu = prob[0:B, 1, 1024:1024 + D]
        c_t = prob[:, 1, 1280:1280 + KC * B].rearrange("p (c b) -> p c b", c=KC)
        mod_r = prob[0:B, 1, 1536:1536 + 2 * D].rearrange("p (g d) -> p g d", g=2)
        mod_s = prob[0:B, 1, 2048:2048 + 2 * D].rearrange("p (g d) -> p g d", g=2)
        mod_m = prob[0:B, 1, 2560:2560 + 2 * D].rearrange("p (g d) -> p g d", g=2)
        BR = 4 * D // 64
        bias_f, bias_rest = sb("bias_f", [BR, 64]), sb("bias_rest", [BR, 64])
        bias_parts = sb("bias_parts", [BR, 3, 64], BF16)

        x_v = x.rearrange("b (t p) d -> b p t d", p=P)
        x1_v = x1_dram[:, 0:D].rearrange("(b t p) d -> b p t d", t=QT, p=P)

        xs_loaded = [sem("xs_loaded0"), sem("xs_loaded1")]
        xr_loaded = [sem("xr_loaded0"), sem("xr_loaded1")]
        x1_stored = [sem("x1_stored0"), sem("x1_stored1")]
        w_loaded, wo_loaded, mod_loaded, c_loaded = sem("w_loaded"), sem("wo_loaded"), sem("mod_loaded"), sem("c_loaded")
        bias_loaded, rope_loaded = sem("bias_loaded"), sem("rope_loaded")
        bias_spread = sem("bias_spread")
        masks_done = sem("masks_done")
        wt_ps, wt_kept, c_exp_done, silu_done = sem("wt_ps"), sem("wt_kept"), sem("c_exp_done"), sem("silu_done")
        ct_ps, ct_kept, mod_ps, mod_kept = sem("ct_ps"), sem("ct_kept"), sem("mod_ps"), sem("mod_kept")
        gates_ps, gates_done, gates_saved = sem("gates_ps"), sem("gates_done"), sem("gates_saved")
        gates_loaded, bias_split, setup_chain = sem("gates_loaded"), sem("bias_split"), sem("setup_chain")
        stats_done, rstd_done, xhat_done = sem("stats_done"), sem("rstd_done"), sem("xhat_done")
        mv_done, var_done = sem("mv_done"), sem("var_done")
        xt_ps, ht_done, qk_ps, v_ps = sem("xt_ps"), sem("ht_done"), sem("qk_ps"), sem("v_ps")
        rope_done, rot_done, hi_done, lo_done = (sem("rope_done"), sem("rot_done"), sem("hi_done"),
                                                 sem("lo_done"))
        row_cleared, kt_zeroed, pv0_ps = sem("row_cleared"), sem("kt_zeroed"), sem("pv0_ps")
        kt2_kept = sem("kt2_kept")
        att_tp, att_kept = sem("att_tp"), sem("att_kept")
        v_kept, aug_ps, qt_kept, kt_kept = sem("v_kept"), sem("aug_ps"), sem("qt_kept"), sem("kt_kept")
        max_ps, max_done, negmax_done = sem("max_ps"), sem("max_done"), sem("negmax_done")
        shift_ps, shift_kept = sem("shift_ps"), sem("shift_kept")
        sc_ps, exp_done, masked = sem("sc_ps"), sem("exp_done"), sem("masked")
        pv_ps, u_kept, den_ps = sem("pv_ps"), sem("u_kept"), sem("den_ps")
        recip_done, att_done = sem("recip_done"), sem("att_done")
        dve_turns, pool_turns = sem("dve_turns"), sem("pool_turns")
        o_ps, gated_done, x1_done = sem("o_ps"), sem("gated_done"), sem("x1_done")

        block = ctx.enter_context(nc.Block())

        PAIR = 2 * G
        LOOPS = B // 2 - 1

        def all_units(eng, unit):
            for n in range(G):
                unit(0, n)
            with eng.Fori(0, LOOPS) as i:
                for n in range(G, G + PAIR):
                    unit(i, n)
            for n in range(G, PAIR):
                unit(LOOPS, n)

        def place(n):
            return (n // 4) % 2, n % 4

        def has(i, n):
            return not isinstance(i, int) or PAIR * i + n < NU

        def when(eng, i, n):
            if not isinstance(i, int) and PAIR * (LOOPS - 1) + n >= NU:
                return eng.If(i < LOOPS - 1)
            return nullcontext()

        def lead_banks(T):
            return (ps_b, ps_a) if T % 2 == (LEAD - 1) % 2 else (ps_sc[1], ps_sc[0])

        @block.sync
        def _(sp):
            sp.dma_start(c_sb, c).then_inc(c_loaded, 16)
            sp.dma_start(xs[:, 0, :, :], x_v[0]).then_inc(xs_loaded[0], 16)
            for n, b_ in enumerate((bq, bk, bv, bo)):
                sp.dma_start(bias_f[n * BR // 4:(n + 1) * BR // 4, :], b_.rearrange("(a n) -> a n", n=64)).then_inc(bias_loaded, 16)
            for n, w in enumerate((wq, wk, wv)):
                sp.dma_start(nat[:, n, :, :], w.rearrange("(c p) i -> p c i", p=P)).then_inc(w_loaded, 16)
            sp.dma_start(wmod_sb, wmod.rearrange("(c p) n -> p c n", p=P)).then_inc(mod_loaded, 16)
            sp.dma_start(cos_t[:, :, :], rope_cos.rearrange("(t p) d -> p t d", p=P)).then_inc(rope_loaded, 16)
            sp.dma_start(sin_t[:, :, :], rope_sin.rearrange("(t p) d -> p t d", p=P)).then_inc(rope_loaded, 16)
            sp.dma_start(nat_o, wo.rearrange("(c p) i -> p c i", p=P)).then_inc(wo_loaded, 16)
            sp.wait_ge(bias_split, 3)
            for n in range(3):
                sp.dma_start(bias3[n:n + 1, :].rearrange("a (r e) -> a r e", e=64), bias_parts[:, n, :]).then_inc(bias_spread, 16)
            sp.dma_start(xs[:, 1, :, :], x_v[1]).then_inc(xs_loaded[1], 16)
            for b in range(2):
                sp.dma_start(xr[:, b, :, :], x_v[b]).then_inc(xr_loaded[b], 16)
            sp.wait_ge(gates_done, 1)
            sp.dma_start(gates_dram.rearrange("g (b d) -> b g d", b=B), mod_r).then_inc(gates_saved, 16)
            sp.wait_ge(gates_saved, 16)
            sp.dma_start(gate_a[:, :, :].rearrange("p b d -> p (b d)"), gates_dram[0].partition_broadcast(P)).then_inc(gates_loaded, 16)

            def load_xs(b, half):
                sp.wait_ge(xhat_done, QT * (b - 1))
                sp.dma_start(xs[:, half, :, :], x_v[b]).then_inc(xs_loaded[half], 16)

            def swap_xr(b, half, k):
                sp.wait_ge(x1_done, QT * (b - 1))
                sp.dma_start(x1_v[b - 2], xr[:, half, :, :]).then_inc(x1_stored[half], 16)
                sp.wait_ge(x1_stored[half], 16 * k)
                sp.dma_start(xr[:, half, :, :], x_v[b]).then_inc(xr_loaded[half], 16)

            load_xs(2, 0)
            with sp.Fori(1, B // 2 - 1) as k:
                for half in range(2):
                    load_xs(2 * k + half + 1, 1 - half)
                    swap_xr(2 * k + half, half, k)
            load_xs(B - 1, 1)
            for half in range(2):
                swap_xr(B - 2 + half, half, B // 2 - 1)
            for half in range(2):
                b = B - 2 + half
                sp.wait_ge(x1_done, QT * (b + 1))
                sp.dma_start(x1_v[b], xr[:, half, :, :]).then_inc(x1_stored[half], 16)
            for half in range(2):
                sp.wait_ge(x1_stored[half], 16 * (B // 2))

        @block.gpsimd
        def _(pool):
            nc.gpsimd.memset(ident[:, :], 0.0).then_inc(masks_done, 1)
            nc.gpsimd.memset(ident16[:, :], 0.0).then_inc(masks_done, 1)
            nc.gpsimd.memset(ident_b[:, :], 0.0).then_inc(masks_done, 1)
            nc.gpsimd.memset(causal[:, :, :], 0.0).then_inc(masks_done, 1)
            pool.wait_ge(masks_done, 4)
            for m in (ident, ident16, ident_b):
                nc.gpsimd.affine_select(out=m[:, :], in_=m[:, :], compare_op=ALU.not_equal, fill=1.0, base=0,
                                        pattern=[[-1, P]], channel_multiplier=1).then_inc(masks_done, 1)
            nc.gpsimd.affine_select(out=causal[:, :, :], in_=causal[:, :, :], compare_op=ALU.is_ge, fill=NEG, base=0,
                                    pattern=[[0, 2], [-1, P]], channel_multiplier=1).then_inc(masks_done, 1)
            nc.gpsimd.memset(ones3[:, :], 1.0).then_inc(masks_done, 1)
            nc.gpsimd.memset(neg_half[:, :], -0.5).then_inc(masks_done, 1)
            for half in range(2):
                nc.gpsimd.memset(q_aug[:, half, :, :].rearrange("p t (h w) -> p (t h) w", w=HW)[:, :, 3 * DK:HW], 0.0).then_inc(masks_done, 1)
            nc.gpsimd.memset(k_aug[:, :].rearrange("p (h w) -> p h w", w=HW)[:, :, 3 * DK:3 * DK + 1], 1.0).then_inc(masks_done, 1)
            nc.gpsimd.memset(k_aug[:, :].rearrange("p (h w) -> p h w", w=HW)[:, :, 3 * DK + 1:HW], 0.0).then_inc(masks_done, 1)
            v_rows = v_sb[:, :, :, :, :].rearrange("p a t h o -> p (a t h) o")
            nc.gpsimd.memset(v_rows[:, :, DK:DK + 1], 1.0).then_inc(masks_done, 1)
            nc.gpsimd.memset(v_rows[:, :, DK + 1:32], 0.0).then_inc(masks_done, 1)
            pool.wait_ge(masks_done, 16)

            def rstd_of(T):
                pool.wait_ge(var_done, T + 1)
                nc.gpsimd.tensor_tensor(rstd[:, 0, :], var_eps[:, :], neg_half[:, :], ALU.pow).then_inc(rstd_done, 1)

            def rotate(T, par, t):
                pool.wait_ge(rope_done, 3 * T + 3)
                ge(pool, hi_done, 2 * T)
                ge(pool, lo_done, 2 * T)
                nc.gpsimd.tensor_tensor(rot[:, :], rot_a[:, :], rot_b[:, :], ALU.add).then_inc(rot_done, 1)
                q_v = q_aug[:, par, t, :].rearrange("p (h w) -> p h w", w=HW)
                nc.gpsimd.memset(q_v[:, :, 3 * DK:3 * DK + 1], 0.0).then_inc(row_cleared, 1)

            rstd_of(0)
            rstd_of(1)
            for T in range(LEAD):
                rotate(T, *place(T))
                if T + 2 <= LEAD:
                    rstd_of(T + 2)

            def unit(i, n):
                U = PAIR * i + n
                for kb in range(QT):
                    if kb == 1:
                        if has(i, n + LEAD):
                            with when(pool, i, n + LEAD):
                                rotate(U + LEAD, *place(n + LEAD))
                        if has(i, n + LEAD + 1):
                            with when(pool, i, n + LEAD + 1):
                                rstd_of(U + LEAD + 1)
                    pool.wait_ge(exp_done, NSHOT * U + EXP_UPTO[kb])
                    pool.sem_inc(pool_turns, 1)
                    diag = prob[:, n % 2, P_AT[kb]:P_AT[kb + 1]].rearrange("p (h q) -> p h q", h=HG)[:, :, 0:P]
                    nc.gpsimd.affine_select(out=diag, in_=diag, compare_op=ALU.is_ge, fill=0.0, base=0,
                                            pattern=[[0, HG], [1, P]], channel_multiplier=-1).then_inc(masked, 1)

            all_units(pool, unit)

        @block.tensor
        def _(pe):
            mm = nc.tensor.matmul
            pe.wait_ge(masks_done, 8)

            def weight_transposes(w, ps):
                for ic in range(KC):
                    for oc in range(KC):
                        last = nc.tensor.transpose(ps[:, (ic * KC + oc) * P:(ic * KC + oc + 1) * P],
                                                   w[:, oc, ic * P:(ic + 1) * P], ident[:, :])
                last.then_inc(wt_ps, 1)

            def modulation(first_part, ps):
                for n in range(2 * KC):
                    at = first_part * D + n * P
                    for k in range(KC):
                        last = mm(ps[:, n * B:(n + 1) * B], wmod_sb[:, k, at:at + P], c_t[:, k, :],
                                  start=(n == 0 and k == 0), stop=(k == KC - 1), skip_group_check=True)
                last.then_inc(mod_ps, 1)

            def raw_gates(ps):
                for n, part in enumerate((2, 5)):
                    for k in range(KC):
                        last = mm(ps[0:B, n * D:(n + 1) * D], c_t[:, k, :], wmod_sb[:, k, part * D:(part + 1) * D],
                                  start=(n == 0 and k == 0), stop=(k == KC - 1), skip_group_check=True)
                last.then_inc(gates_ps, 1)

            pe.wait_ge(silu_done, 1)
            for k in range(KC):
                last = nc.tensor.transpose(ps_b[:, k * B:(k + 1) * B], c_silu[:, k * P:(k + 1) * P], ident[0:B, 0:B])
            last.then_inc(ct_ps, 1)
            pe.wait_ge(w_loaded, 48)
            for n, ps in enumerate((ps_sc[0], ps_sc[1], ps_max[0])):
                weight_transposes(nat[:, n, :, :], ps)
            pe.wait_ge(ct_kept, 1)
            pe.wait_ge(mod_loaded, 16)
            modulation(0, ps_nd)

            def x_transposes(T, ps):
                pe.wait_ge(xhat_done, T + 1)
                for k in range(KC):
                    last = nc.tensor.transpose(ps[:, k * P:(k + 1) * P], xhat[:, k * P:(k + 1) * P], ident[:, :])
                last.then_inc(xt_ps, 1)

            def project_qk(T, k, ps, kept_before):
                if k == 0:
                    pe.wait_ge(ht_done, KC * T + KC)
                    ge(pe, qt_kept, kept_before)
                    mm(ps[:, :], ones3[:, :], bias3[:, 0:2 * D], start=True, stop=False)
                last = mm(ps[:, :], h_t[:, k, :], w_qkv[:, k, 0:2 * D], start=False, stop=(k == KC - 1))
                if k == KC - 1:
                    last.then_inc(qk_ps, 1)

            def project_v(T, ps, kept_before):
                ge(pe, kt_kept, kept_before)
                ge(pe, kt2_kept, kept_before)
                mm(ps[:, 0:D], ones3[:, :], bias3[:, 2 * D:3 * D], start=True, stop=False)
                for k in range(KC):
                    last = mm(ps[:, 0:D], h_t[:, k, :], w_qkv[:, k, 2 * D:3 * D], start=False, stop=(k == KC - 1))
                last.then_inc(v_ps, 1)

            def q_transposes(T, par, t, ps):
                pe.wait_ge(hi_done, 2 * T + 2)
                pe.wait_ge(lo_done, 2 * T + 2)
                pe.wait_ge(row_cleared, T + 1)
                for m in range(H // 2):
                    last = nc.tensor.transpose(ps[:, :].bitcast(F16)[:, m * P:(m + 1) * P],
                                               q_aug[:, par, t, m * P:(m + 1) * P], ident16[:, :])
                last.then_inc(aug_ps, 1)

            def k_transposes(T, ps):
                pe.wait_ge(v_kept, T + 1)
                for m in range(H // 2):
                    last = nc.tensor.transpose(ps[:, :].bitcast(F16)[:, m * P:(m + 1) * P],
                                               k_aug[:, m * P:(m + 1) * P], ident16[:, :])
                last.then_inc(aug_ps, 1)

            def max_scores(V, par, g, s):
                qt, first, n, j = MAX_SHOTS[s]
                L = P * (qt + 1)
                if s == 0:
                    if g == 0:
                        pe.wait_ge(qt_kept, V + 4)
                        pe.wait_ge(kt_kept, V + 4)
                        pe.wait_ge(kt2_kept, V + 4)
                ge(pe, max_done, NSHOT * V + s - 1)
                for m in range(n):
                    mm(ps_max[j][:, m * L:(m + 1) * L], q_t[:, par, 2 * g + first + m, qt * P:(qt + 1) * P],
                       k_t[:, par, j, 2 * g + first + m, 0:L], start=(m == 0), stop=False,
                       skip_group_check=True)
                o = ps_max[j][:, 0:n * L].rearrange("p (m l) -> p m l", m=n)[:, :, L - P:L]
                mm(o, ident_b[:, :], causal[:, 0:n, :], start=False, stop=True,
                   skip_group_check=True).then_inc(max_ps, 1)

            def shift_rows(V, par, g):
                pe.wait_ge(negmax_done, V + 1)
                for m in range(2):
                    ge(pe, exp_done, NSHOT * V - 1 + m)
                    for qt in range(QT):
                        last = nc.tensor.transpose(ps_sc[m][:, :].bitcast(F16)[:, qt * P:(qt + 1) * P],
                                                   q_aug[:, par, qt, (2 * g + m) * P:(2 * g + m + 1) * P],
                                                   ident16[:, :])
                    last.then_inc(shift_ps, 1)

            def scores(U, par, g, s):
                kb, first, n, j = EXP_SHOTS[s]
                L = S - P * kb
                if s < 2:
                    pe.wait_ge(shift_kept, 2 * U + 1 + s)
                if s >= 2:
                    pe.wait_ge(exp_done, NSHOT * U + s - 1)
                for m in range(n):
                    last = mm(ps_sc[j][:, m * L:(m + 1) * L], k_t[:, par, j, 2 * g + first + m, kb * P:(kb + 1) * P],
                              q_t[:, par, 2 * g + first + m, kb * P:S], start=(m == 0), stop=(m == n - 1),
                              skip_group_check=True)
                last.then_inc(sc_ps, 1)

            def weigh(U, half, par, g, kb):
                pe.wait_ge(masked, QT * U + kb + 1)
                L = S - P * kb
                p_kb = prob[:, half, P_AT[kb]:P_AT[kb + 1]].rearrange("p (j m q) -> p j m q", j=2, m=2)
                for m in range(2):
                    for j in range(2):
                        col = 2 * m + j
                        last = mm(ps_pv[32 * col:32 * col + 32, kb * P:S], v_sb[:, par, kb, HG * g + col, :],
                                  p_kb[:, j, m, :], start=(kb == 0), stop=(kb == QT - 1), skip_group_check=True)
                if kb == 0:
                    last.then_inc(pv0_ps, 1)
                if kb == QT - 1:
                    last.then_inc(pv_ps, 1)

            def tokens_first(W, half, x1_before):
                pe.wait_ge(u_kept, W + 1)
                ge(pe, att_done, W)
                if x1_before is not None:
                    ge(pe, x1_done, x1_before)
                for qt in range(QT):
                    last = nc.tensor.transpose(ps_nd[:, qt * P:(qt + 1) * P], u_sb[:, half, qt * P:(qt + 1) * P], ident[:, :])
                last.then_inc(den_ps, 1)

            def att_transposes(X, par, t, units):
                pe.wait_ge(att_done, units)
                if isinstance(X, int):
                    ge(pe, x1_done, X)
                for k in range(KC):
                    last = nc.tensor.transpose(ps_nd[:, k * P:(k + 1) * P], att[:, par, t, k * P:(k + 1) * P], ident[:, :])
                last.then_inc(att_tp, 1)

            def project_out(X):
                pe.wait_ge(att_kept, X + 1)
                o = ps_nd[:, KC * P:KC * P + D]
                mm(o, ones3[:, :], bias3[:, 3 * D:4 * D], start=True, stop=False, skip_group_check=True)
                for k in range(KC):
                    last = mm(o, att_t[:, k, :], w_o[:, k, :], start=False, stop=(k == KC - 1), skip_group_check=True)
                last.then_inc(o_ps, 1)

            x_transposes(0, ps_pv)
            pe.wait_ge(masks_done, 16)
            pe.wait_ge(bias_spread, 48)
            pe.wait_ge(wt_kept, 3)
            for T in range(LEAD):
                ps_q, ps_v = lead_banks(T)
                for k in range(KC):
                    project_qk(T, k, ps_q, T - 1)
                project_v(T, ps_v, T - 1)
                if T + 1 < LEAD:
                    x_transposes(T + 1, ps_pv)
                if T == 0:
                    pe.wait_ge(wo_loaded, 16)
                    weight_transposes(nat_o, ps_max[1])
                if T == 1:
                    modulation(3, ps_max[0])
                if T == 2:
                    raw_gates(ps_nd)
                if T:
                    ps_q, ps_v = lead_banks(T - 1)
                    q_transposes(T - 1, *place(T - 1), ps_q)
                    k_transposes(T - 1, ps_v)
            q_transposes(LEAD - 1, *place(LEAD - 1), ps_b)
            k_transposes(LEAD - 1, ps_a)
            x_transposes(LEAD, ps_nd)
            for s in range(NSHOT):
                max_scores(0, 0, 0, s)
            shift_rows(0, 0, 0)

            def unit(i, n):
                U = PAIR * i + n
                par, g = place(n)
                T, V, X = U + LEAD, U + 1, U - 4
                has_t, has_v, has_x = has(i, n + LEAD), has(i, n + 1), not isinstance(i, int) or U >= QT
                for s in range(NSHOT):
                    if has_v and s != 1:
                        max_scores(V, *place(n + 1), s)
                    if has_v and s == 0:
                        max_scores(V, *place(n + 1), 1)
                    scores(U, par, g, s)
                    if s < KC and has_t:
                        with when(pe, i, n + LEAD):
                            project_qk(T, s, ps_b, T)
                    if s == 2 and (n or not isinstance(i, int) or i):
                        tokens_first(U - 1, (n - 1) % 2, None if n == G and not isinstance(i, int) else U - 4 if has_x else 0)
                    if s == 3 and has_t:
                        with when(pe, i, n + LEAD):
                            project_v(T, ps_a, T)
                    if s == 5 and has_x:
                        att_transposes(X, *place(n + 4), U)
                    if s == 5:
                        weigh(U, n % 2, par, g, 0)
                    if s == 7 and has_x:
                        project_out(X)
                    if s == 10:
                        weigh(U, n % 2, par, g, 1)
                if has_t:
                    with when(pe, i, n + LEAD):
                        q_transposes(T, *place(n + LEAD), ps_b)
                        k_transposes(T, ps_a)
                weigh(U, n % 2, par, g, 2)
                if has(i, n + LEAD + 1):
                    with when(pe, i, n + LEAD + 1):
                        x_transposes(T + 1, ps_nd)
                if has_v:
                    shift_rows(V, *place(n + 1))
                weigh(U, n % 2, par, g, 3)

            all_units(pe, unit)
            tokens_first(NU - 1, (NU - 1) % 2, NU - 4)
            for X in range(NT - QT, NT):
                att_transposes(X, *place(X), NU)
                project_out(X)

        @block.scalar
        def _(act):
            act.wait_ge(c_loaded, 16)
            nc.scalar.activation(c_exp, c_sb, ACT.Exp, scale=-1.0).then_inc(c_exp_done, 1)
            for n, ps in enumerate((ps_sc[0], ps_sc[1], ps_max[0])):
                act.wait_ge(wt_ps, n + 1)
                nc.scalar.activation(w_qkv[:, :, n * D:(n + 1) * D], ps[:, :].rearrange("p (i o) -> p i o", i=KC),
                                     ACT.Copy).then_inc(wt_kept, 1)

            def keep_v(T, par, t, after_unit, ps=ps_a):
                act.wait_ge(v_ps, T + 1)
                if after_unit is not None:
                    act.wait_ge(pv0_ps, after_unit + 1)
                nc.scalar.activation(v_sb[:, par, t, :, 0:DK], ps[:, 0:D].rearrange("p (h d) -> p h d", h=H),
                                     ACT.Copy).then_inc(v_kept, 1)

            def hi_parts(T, par, t):
                act.wait_ge(rot_done, T + 1)
                r = rot[:, :].rearrange("p (w h d) -> p w h d", w=2, h=H)
                q_v = q_aug[:, par, t, :].rearrange("p (h w) -> p h w", w=HW)[:, :, 0:4 * DK]
                q_v = q_v.rearrange("p h (a d) -> p h a d", d=2 * DK)[:, :, :, 0:DK]
                k_v = k_aug[:, :].rearrange("p (h w) -> p h w", w=HW)[:, :, 0:2 * DK].rearrange("p h (a d) -> p h a d", a=2)
                for w, v in ((0, q_v), (1, k_v)):
                    nc.scalar.activation(v, r[:, w, :, None, :].to_broadcast([P, H, 2, DK]), ACT.Copy).then_inc(hi_done, 1)

            def keep_kt(T, par, t, ps=ps_a):
                act.wait_ge(aug_ps, 2 * T + 2)
                nc.scalar.activation(k_t[0:HW, par, 0, :, t * P:(t + 1) * P],
                                     ps[0:HW, :].bitcast(F16).rearrange("p (m q) -> p m q", q=P), ACT.Copy).then_inc(kt_kept, 1)

            def keep_att(X):
                act.wait_ge(att_tp, X + 1)
                nc.scalar.activation(att_t[:, :, :].rearrange("p k m -> p (k m)"), ps_nd[:, 0:KC * P], ACT.Copy).then_inc(att_kept, 1)

            def keep_shift(V, par, g):
                for m in range(2):
                    act.wait_ge(shift_ps, 2 * V + 1 + m)
                    nc.scalar.activation(q_t[:, par, 2 * g + m, :], ps_sc[m][:, :].bitcast(F16)[:, 0:S], ACT.Copy).then_inc(shift_kept, 1)

            def exps(U, half, s):
                kb, first, n, j = EXP_SHOTS[s]
                L = S - P * kb
                act.wait_ge(sc_ps, NSHOT * U + s + 1)
                a = P_AT[kb] + (2 * j + first) * L
                nc.scalar.activation(prob[:, half, a:a + n * L], ps_sc[j][:, 0:n * L], ACT.Exp,
                                     scale=SCALE).then_inc(exp_done, 1)

            def keep_u(U, half):
                act.wait_ge(pv_ps, U + 1)
                nc.scalar.activation(u_sb[:, half, :], ps_pv[:, :], ACT.Copy).then_inc(u_kept, 1)

            for T in range(LEAD):
                keep_v(T, *place(T), None, lead_banks(T)[1])
                if T == 0:
                    act.wait_ge(wt_ps, 4)
                    nc.scalar.activation(w_o[:, :, :], ps_max[1][:, :].rearrange("p (i o) -> p i o", i=KC), ACT.Copy).then_inc(wt_kept, 1)
                if T == 1:
                    act.wait_ge(kt_zeroed, 4)
                if T:
                    keep_kt(T - 1, *place(T - 1), lead_banks(T - 1)[1])
                hi_parts(T, *place(T))
            keep_kt(LEAD - 1, *place(LEAD - 1))
            act.wait_ge(gates_saved, 16)
            keep_shift(0, 0, 0)

            def unit(i, n):
                U = PAIR * i + n
                par, g = place(n)
                T, V, X = U + LEAD, U + 1, U - 4
                has_t, has_v, has_x = has(i, n + LEAD), has(i, n + 1), not isinstance(i, int) or U >= QT
                for s in range(NSHOT):
                    exps(U, n % 2, s)
                    if s == 5 and has_x:
                        keep_att(X)
                    if s == 6 and has_t:
                        with when(act, i, n + LEAD):
                            keep_v(T, *place(n + LEAD), U if g == G - 1 else None)
                    if s == 7 and has_t:
                        with when(act, i, n + LEAD):
                            hi_parts(T, *place(n + LEAD))
                if has_t:
                    with when(act, i, n + LEAD):
                        keep_kt(T, *place(n + LEAD))
                if has_v:
                    keep_shift(V, *place(n + 1))
                keep_u(U, n % 2)

            all_units(act, unit)
            for X in range(NT - QT, NT):
                keep_att(X)

        @block.vector
        def _(dve):
            done = [0]

            def link(ins):
                done[0] += 1
                ins.then_inc(setup_chain, 1)
                dve.wait_ge(setup_chain, done[0])

            one_plus = mod_s[:, 0, :]
            dve.wait_ge(c_exp_done, 1)
            link(nc.vector.tensor_scalar(c_exp, c_exp, 1.0, None, ALU.add))
            link(nc.vector.reciprocal(one_plus, c_exp))
            nc.vector.tensor_tensor(c_silu, c_sb, one_plus, ALU.mult).then_inc(silu_done, 1)
            dve.wait_ge(bias_loaded, 64)
            for n in range(3):
                nc.vector.tensor_copy(bias_parts[:, n, :], bias_f[:, :]).then_inc(bias_split, 1)
                if n < 2:
                    dve.wait_ge(bias_split, n + 1)
                    link(nc.vector.tensor_tensor(bias_f[:, :], bias_f[:, :], bias_parts[:, n, :], ALU.subtract))

            def zeros(par):
                for j in range(2):
                    rows = slice(HW * (1 - j), HW * (2 - j))
                    nc.vector.memset(k_t[rows, par, j, :, :].rearrange("p m s -> p (m s)").bitcast(F32), 0.0).then_inc(kt_zeroed, 1)

            def keep_modulation(first_part, ps, count):
                dve.wait_ge(mod_ps, count)
                at = first_part * KC
                nc.vector.tensor_copy(mod_t[:, at:at + KC, :], ps[:, 0:KC * B].rearrange("p (n b) -> p n b", b=B)).then_inc(mod_kept, 1)
                nc.vector.tensor_scalar(mod_t[:, at + KC:at + 2 * KC, :], ps[:, KC * B:2 * KC * B].rearrange("p (n b) -> p n b", b=B),
                                        1.0, None, ALU.add).then_inc(mod_kept, 1)

            def keep_gates():
                dve.wait_ge(gates_ps, 1)
                link(nc.vector.tensor_copy(mod_r, ps_nd[0:B, :].rearrange("p (g d) -> p g d", g=2)))
                link(nc.vector.tensor_scalar(mod_s, mod_r, 0.0, 2.0, ALU.is_ge, ALU.mult))
                link(nc.vector.tensor_scalar(mod_m, mod_r, -1.0, None, ALU.mult))
                link(nc.vector.tensor_tensor(mod_m, mod_m, mod_r, ALU.max))
                link(nc.vector.tensor_scalar(mod_m, mod_m, ADA_MIN, None, ALU.max))
                nc.vector.scalar_tensor_tensor(out=mod_r, in0=mod_s, scalar=-1.0, in1=mod_m, op0=ALU.add,
                                               op1=ALU.mult).then_inc(gates_done, 1)

            def statistics(T, par, t, load_count):
                if t == 0:
                    dve.wait_ge(xs_loaded[par], load_count)
                nc.vector.bn_stats(bn[:, 0, :], xs[:, par, t, :]).then_inc(stats_done, 1)
                dve.wait_ge(stats_done, T + 1)
                dve.sem_inc(dve_turns, 1)
                nc.vector.bn_aggr(mean_var[:, 0, :], bn[:, 0, :]).then_inc(mv_done, 1)
                dve.wait_ge(mv_done, T + 1)
                nc.vector.tensor_scalar(var_eps[:, :], mean_var[:, 0, 1:2], LN_EPS, None, ALU.add).then_inc(var_done, 1)

            def normalise(T, par, t):
                dve.wait_ge(rstd_done, T + 1)
                nc.vector.tensor_scalar(xhat[:, :], xs[:, par, t, :], mean_var[:, 0, 0:1], rstd[:, 0, :],
                                        ALU.subtract, ALU.mult).then_inc(xhat_done, 1)

            def modulate(T, b, ps=ps_nd):
                dve.wait_ge(xt_ps, T + 1)
                for k in range(KC):
                    nc.vector.tensor_scalar(h_t[:, k, :], ps[:, k * P:(k + 1) * P],
                                            mod_t[:, KC + k, b], mod_t[:, k, b],
                                            ALU.mult, ALU.add).then_inc(ht_done, 1)

            def rope(T, t, ps=ps_b):
                dve.wait_ge(qk_ps, T + 1)
                qk = ps[:, :].rearrange("p (h d) -> p h d", d=DK)
                nc.vector.tensor_tensor(rot_a[:, :].rearrange("p (h d) -> p h d", d=DK), qk,
                                        cos_t[:, t, None, :].to_broadcast([P, 2 * H, DK]), ALU.mult).then_inc(rope_done, 1)
                qk2 = ps[:, :].rearrange("p (h d two) -> p h d two", two=2, d=DK // 2)
                b2 = rot_b[:, :].rearrange("p (h d two) -> p h d two", two=2, d=DK // 2)
                s2 = sin_t[:, t, :].rearrange("p (d two) -> p d two", two=2)
                for e in range(2):
                    nc.vector.tensor_tensor(b2[:, :, :, e], qk2[:, :, :, 1 - e],
                                            s2[:, None, :, e].to_broadcast([P, 2 * H, DK // 2]), ALU.mult).then_inc(rope_done, 1)

            def lo_parts(T, par, t):
                dve.wait_ge(hi_done, 2 * T + 2)
                r = rot[:, :].rearrange("p (w h d) -> p w h d", w=2, h=H)
                q_v = q_aug[:, par, t, :].rearrange("p (h w) -> p h w", w=HW)
                k_v = k_aug[:, :].rearrange("p (h w) -> p h w", w=HW)
                nc.vector.tensor_tensor(q_v[:, :, DK:2 * DK], r[:, 0], q_v[:, :, 0:DK], ALU.subtract).then_inc(lo_done, 1)
                nc.vector.tensor_tensor(k_v[:, :, 2 * DK:3 * DK], r[:, 1], k_v[:, :, 0:DK], ALU.subtract).then_inc(lo_done, 1)

            def keep_qt(T, par, t, ps=ps_b):
                dve.wait_ge(aug_ps, 2 * T + 1)
                nc.vector.tensor_copy(q_t[:, par, :, t * P:(t + 1) * P],
                                      ps[:, :].bitcast(F16).rearrange("p (m q) -> p m q", q=P)).then_inc(qt_kept, 1)

            def keep_kt(T, par, t, ps=ps_a):
                dve.wait_ge(aug_ps, 2 * T + 2)
                nc.vector.tensor_copy(k_t[HW:P, par, 1, :, t * P:(t + 1) * P],
                                      ps[HW:P, :].bitcast(F16).rearrange("p (m q) -> p m q", q=P)).then_inc(kt2_kept, 1)

            def maxima(V, half, s):
                qt, first, n, j = MAX_SHOTS[s]
                L = P * (qt + 1)
                dve.wait_ge(max_ps, NSHOT * V + s + 1)
                dst = row_max[:, half, qt, :].rearrange("p (m j) -> p m j", j=2)[:, first:first + n, j]
                nc.vector.tensor_reduce(dst, ps_max[j][:, 0:n * L].rearrange("p (m l) -> p m l", m=n),
                                        AX.X, ALU.max).then_inc(max_done, 1)

            def negated(V, half, par, g):
                dve.wait_ge(max_done, NSHOT * V + NSHOT)
                q_v = q_aug[:, par, :, :].rearrange("p t (h w) -> p t h w", w=HW)
                nc.vector.tensor_scalar(q_v[:, :, HG * g:HG * (g + 1), 3 * DK], row_max[:, half, :, :],
                                        -1.0, None, ALU.mult).then_inc(negmax_done, 1)

            def divide(W, par, g):
                dve.wait_ge(den_ps, W + 1)
                sums = ps_nd[:, :].rearrange("p (t c d) -> p t c d", t=QT, c=HG)
                nc.vector.reciprocal(recip[:, :, :], sums[:, :, :, DK]).then_inc(recip_done, 1)
                dve.wait_ge(recip_done, W + 1)
                nc.vector.tensor_tensor(att[:, par, :, HG * DK * g:HG * DK * (g + 1)].rearrange("p t (c d) -> p t c d", c=HG),
                                        sums[:, :, :, 0:DK], recip[:, :, :, None].to_broadcast([P, QT, HG, DK]),
                                        ALU.mult).then_inc(att_done, 1)

            def residual(X, b, par, t, load_count):
                if t == 0:
                    dve.wait_ge(xr_loaded[par], load_count)
                dve.wait_ge(o_ps, X + 1)
                gate = gate_a[:, b, :] if isinstance(b, int) else gate_a[:, bass.ds(b, 1), :].rearrange("p b d -> p (b d)")
                nc.vector.tensor_tensor(gated[:, :], ps_nd[:, KC * P:KC * P + D], gate, ALU.mult).then_inc(gated_done, 1)
                dve.wait_ge(gated_done, X + 1)
                nc.vector.tensor_tensor(xr[:, par, t, :], xr[:, par, t, :], gated[:, :], ALU.add).then_inc(x1_done, 1)

            statistics(0, 0, 0, 16)
            dve.wait_ge(ct_ps, 1)
            nc.vector.tensor_copy(c_t, ps_b[:, 0:KC * B].rearrange("p (c b) -> p c b", c=KC)).then_inc(ct_kept, 1)
            normalise(0, 0, 0)
            zeros(0)
            keep_modulation(0, ps_nd, 1)
            dve.wait_ge(mod_kept, 2)
            dve.wait_ge(rope_loaded, 32)
            modulate(0, slice(0, 1), ps_pv)
            statistics(1, 0, 1, 16)
            normalise(1, 0, 1)
            for T in range(LEAD):
                rope(T, T % 4, lead_banks(T)[0])
                if T + 1 < LEAD:
                    modulate(T + 1, slice((T + 1) // 4, (T + 1) // 4 + 1), ps_pv)
                if T + 2 <= LEAD:
                    statistics(T + 2, *place(T + 2), 16)
                if T:
                    keep_qt(T - 1, *place(T - 1), lead_banks(T - 1)[0])
                    keep_kt(T - 1, *place(T - 1), lead_banks(T - 1)[1])
                if T + 2 <= LEAD:
                    normalise(T + 2, *place(T + 2))
                if T == 0:
                    zeros(1)
                if T == 1:
                    keep_modulation(3, ps_max[0], 2)
                if T == 2:
                    keep_gates()
                lo_parts(T, *place(T))
            keep_qt(LEAD - 1, *place(LEAD - 1))
            keep_kt(LEAD - 1, *place(LEAD - 1))
            modulate(LEAD, slice(LEAD // 4, LEAD // 4 + 1))
            for s in range(NSHOT):
                maxima(0, 0, s)
            negated(0, 0, 0, 0)

            def unit(i, n):
                U = PAIR * i + n
                par, g = place(n)
                T, V, X = U + LEAD, U + 1, U - 4
                has_t, has_v, has_x = has(i, n + LEAD), has(i, n + 1), not isinstance(i, int) or U >= QT
                for s in range(NSHOT):
                    if has_v:
                        maxima(V, (n + 1) % 2, s)
                    if s == 3 and (n or not isinstance(i, int) or i):
                        divide(U - 1, *place(n + 7))
                    if s == 3 and has_t:
                        with when(dve, i, n + LEAD):
                            rope(T, (n + LEAD) % 4)
                    if s == 5 and has(i, n + LEAD + 1):
                        with when(dve, i, n + LEAD + 1):
                            statistics(T + 1, *place(n + LEAD + 1), 16 * (i + (n + LEAD + 1) // PAIR + 1))
                    if s == 8 and has_t:
                        with when(dve, i, n + LEAD):
                            lo_parts(T, *place(n + LEAD))
                    if s == 9:
                        if has_x:
                            residual(X, 2 * i + n // 4 - 1, *place(n + 4), 16 * (i + (n // 4 - 1) // 2 + 1))
                        if has(i, n + LEAD + 1):
                            with when(dve, i, n + LEAD + 1):
                                normalise(T + 1, *place(n + LEAD + 1))
                if has_v:
                    negated(V, (n + 1) % 2, *place(n + 1))
                if isinstance(i, int) and U == QT - 1:
                    dve.wait_ge(gates_loaded, 16)
                if has_t:
                    with when(dve, i, n + LEAD):
                        keep_qt(T, *place(n + LEAD))
                if has(i, n + LEAD + 1):
                    with when(dve, i, n + LEAD + 1):
                        b_t = 2 * i + (n + LEAD + 1) // 4
                        if not isinstance(i, int):
                            b_t = nc.s_assert_within(b_t, 0, B - 1, skip_runtime_bounds_check_because="left out behind the end")
                        modulate(T + 1, bass.ds(b_t, 1))
                if has_t:
                    with when(dve, i, n + LEAD):
                        keep_kt(T, *place(n + LEAD))

            all_units(dve, unit)
            divide(NU - 1, *place(NU - 1))
            for X in range(NT - QT, NT):
                residual(X, B - 1, *place(X), 16 * (B // 2))


def route_part(nc, sem, x1_dram, h_dram, w1, b1, w2, b2, switch_w, switch_b, logits, mod_t, ident,
               w1_hi, w1_lo, w2_hi, w2_lo, b1_t, b2_parts, token, gate_row, tile_e, rows_0, slot_x1, fetch_rows):
    with ExitStack() as ctx:
        def sb(name, shape, dt=F32):
            return ctx.enter_context(nc.sbuf_tensor(name, shape, dt))

        def bank(name):
            return ctx.enter_context(nc.psum_tensor(name, [P, 512], F32))

        x1 = sb("x1", [P, 2, QT, D])
        rows = sb("rows", [P, 2, QT, 2 * D], F16)
        raw = sb("raw", [P, 4, F])
        bn = sb("bn2", [P, QT, 6])
        mean_var = sb("mean_var2", [P, QT, 2])
        var_eps = sb("var_eps2", [P, QT])
        neg_half = sb("neg_half2", [P, QT])
        rstd = sb("rstd2", [P, QT])
        xhat = sb("xhat2", [P, QT, D])
        h_t = sb("h_t2", [P, 2, KC, S])
        sw = sb("sw", [P, KC, E])
        sw_b = sb("sw_b", [P, E])
        b1_nat = sb("b1_nat", [E * F // P, P])
        ps_xt = [bank("ps_xt0"), bank("ps_xt1")]
        ps_row = [bank("ps_row0"), bank("ps_row1")]
        ps_logit, ps_rank, ps_token = bank("ps_logit"), bank("ps_rank"), bank("ps_token")
        scr = sb("scr", [P, 7, NT, E])
        onehot, tmp, cum_a, cum_b, within, iota_e, shifted = (scr[:, n, :, :] for n in range(7))
        jcmp = sb("jcmp", [P, E, NT])
        iota_j = sb("iota_j", [P, NT])
        iota_i = sb("iota_i", [P, NSLOT_T])
        ecmp = sb("ecmp", [P, NSLOT_T, E])
        ahead = sb("ahead", [P, P])
        ones = sb("ones", [P, P])
        small = sb("small", [P, 512])
        top, denom, prob_max, first = (small[:, n * NT:(n + 1) * NT] for n in range(4))
        tiles_of, tiles_a, tiles_b, start_of = (small[:, 128 + n * E:128 + (n + 1) * E] for n in range(4))
        slot_f = small[:, 160:160 + NT]
        expert_f = small[:, 192:192 + NSLOT_T]
        slot_row, slot_tile = small[:, 256:256 + NT], small[:, 288:288 + NT]
        token_f, empty, batch_f = (small[:, 320 + n * NSLOT_T:320 + (n + 1) * NSLOT_T] for n in range(3))
        gate_p = small[:, 440:440 + NT]
        iota_r, iota_s, tile_no = sb("iota_r", [P, P]), sb("iota_s", [P, NSLOT_T]), sb("tile_no", [P, NT])
        iota_p = sb("iota_p", [P, 1])
        in_row = h_t[:, :, :, :].rearrange("p a c s -> p (a c s)").bitcast(F16)[:, 0:NT * P].rearrange("p (t r) -> p t r", r=P)
        spare = x1[:, :, :, :].rearrange("p a t d -> p (a t d)").bitcast(F16)
        in_tile = spare[:, 0:NT * NSLOT_T].rearrange("p (t j) -> p t j", j=NSLOT_T)
        parts = spare[:, NT * NSLOT_T:3 * NT * NSLOT_T].rearrange("p (t a j) -> p t a j", a=2, j=NSLOT_T)

        BR = E * D // P
        b2_f, b2_rest, b2_s = sb("b2_f", [BR, P]), sb("b2_rest", [BR, P]), sb("b2_s", [BR, 3, P], BF16)

        x1_v = x1_dram[:, 0:D].rearrange("(b t p) d -> b p t d", t=QT, p=P)
        h_v = h_dram.rearrange("(b t p) d -> b p t d", t=QT, p=P)
        w1_v = w1.rearrange("e (c p) f -> e p c f", p=P)
        w2_v = w2.rearrange("e (f p) d -> e p f d", p=P)

        x1_loaded = [sem("c_x1_loaded0"), sem("c_x1_loaded1")]
        rows_stored = [sem("c_rows_stored0"), sem("c_rows_stored1")]
        raw_loaded, raw_scaled, w_hi_done, w_lo_done = ([sem(f"{n}{c}") for c in range(4)] for n in
                                                        ("raw_loaded", "raw_scaled", "w_hi_done", "w_lo_done"))
        half_set, gate_done, gate_saved = sem("c_half_set"), sem("c_gate_done"), sem("c_gate_saved")
        slots_found = sem("c_slots_found")
        small_in, b2_spread = sem("c_small_in"), sem("b2_spread")
        turns = sem("c_turns")
        b1_ps, b1_kept = sem("b1_ps"), sem("b1_kept")
        b2_mid, b2_split, b2_split_in = sem("b2_mid"), sem("b2_split"), sem("b2_split_in")
        stats, mv, var, rs, xh = sem("c_stats"), sem("c_mv"), sem("c_var"), sem("c_rstd"), sem("c_xhat")
        xt_ps, ht_done, row_ps, logit_ps = sem("c_xt_ps"), sem("c_ht_done"), sem("c_row_ps"), sem("c_logit_ps")
        hi_done, lo_done, logit_kept = sem("c_hi_done"), sem("c_lo_done"), sem("c_logit_kept")
        iotas, chain, shifted_done, exp_done, rank_ps = (sem("c_iotas"), sem("c_chain"), sem("c_shifted"),
                                                         sem("c_exp"), sem("c_rank_ps"))
        onehot_done, tables_done, token_ps = sem("c_onehot"), sem("c_tables"), sem("c_token_ps")

        block = ctx.enter_context(nc.Block())

        def batches(eng, step):
            for u in range(2):
                step(0, u)
            with eng.Fori(1, B // 2 - 1) as i:
                for u in range(2):
                    step(i, u)
            for u in range(2):
                step(B // 2 - 1, u)

        def last(i):
            return isinstance(i, int) and i == B // 2 - 1

        W_CHUNKS, W_COLS = 4, F
        HALF_F = F // P // 2

        def chunk(w1_, w2_, e, c):
            if c < 2:
                return w1_[:, bass.ds(e, 1), c, :].rearrange("p e f -> p (e f)")
            return w2_[:, bass.ds(e, 1), HALF_F * (c - 2):HALF_F * (c - 1), :].rearrange("p e c d -> p (e c d)")

        def staged(c):
            return raw[:, c, :]

        def load_chunk(sp, e, c):
            if c < 2:
                sp.dma_start(staged(c), w1_v[e][:, c, :]).then_inc(raw_loaded[c], 16)
            else:
                sp.dma_start(staged(c).rearrange("p (c d) -> p c d", d=D),
                             w2_v[e][:, HALF_F * (c - 2):HALF_F * (c - 1), :]).then_inc(raw_loaded[c], 16)

        def before(i, u):
            return (i, 0) if u else (i - 1, 1)

        @block.sync
        def _(sp):
            for b in range(2):
                sp.dma_start(x1[:, b, :, :], x1_v[b]).then_inc(x1_loaded[b], 16)
            sp.dma_start(b2_f[:, :], b2.rearrange("e (c p) -> (e c) p", p=P)).then_inc(b2_split_in, 16)

            sp.dma_start(sw[:, :, :], switch_w.rearrange("(c p) e -> p c e", p=P)).then_inc(small_in, 16)
            sp.dma_start(sw_b[:, :], switch_b.partition_broadcast(P)).then_inc(small_in, 16)
            sp.dma_start(b1_nat[:, :], b1.rearrange("e (f p) -> (e f) p", p=P)).then_inc(small_in, 16)
            for c in range(W_CHUNKS):
                load_chunk(sp, 0, c)
            sp.wait_ge(b2_split, 3)
            for n in range(3):
                sp.dma_start(b2_parts[n:n + 1, :].rearrange("a (r p) -> a r p", p=P), b2_s[:, n, :]).then_inc(b2_spread, 16)

            def next_chunk(e, c):
                sp.wait_ge(w_lo_done[c], e + 1)
                load_chunk(sp, e + 1, c)

            def store_rows(b, u):
                sp.wait_ge(lo_done, 2 * b + 2)
                sp.dma_start(h_v[b], rows[:, u, :, :]).then_inc(rows_stored[u], 16)

            def step(i, u):
                b = 2 * i + u
                if not last(i):
                    sp.wait_ge(xh, QT * (b + 1))
                    sp.dma_start(x1[:, u, :, :], x1_v[b + 2]).then_inc(x1_loaded[u], 16)
                if not isinstance(b, int) or b:
                    store_rows(b - 1, 1 - u)
                    e, half = before(i, u)
                    for c in (2 * half, 2 * half + 1):
                        next_chunk(e, c)

            batches(sp, step)
            store_rows(B - 1, 1)
            for c in (2, 3):
                next_chunk(B // 2 - 1, c)
            sp.wait_ge(gate_done, 1)
            sp.dma_start(x1_dram[:, D:D + 1].rearrange("(t p) o -> p (t o)", p=P), gate_p,
                         allow_slow_non_contiguous=True).then_inc(gate_saved, 16)
            with sp.Fori(E // 2, E - 1) as e:
                for c in range(W_CHUNKS):
                    next_chunk(e, c)
            sp.wait_ge(gate_saved, 16)
            sp.wait_ge(b2_spread, 48)
            for u in range(2):
                sp.wait_ge(rows_stored[u], 16 * (B // 2))

        @block.gpsimd
        def _(pool):
            nc.gpsimd.memset(neg_half[:, :], -0.5).then_inc(half_set, 1)
            nc.gpsimd.memset(rows_0[:, :, :], 0.0).then_inc(half_set, 1)
            nc.gpsimd.memset(slot_x1[:, :, :], 0.0).then_inc(half_set, 1)
            pool.wait_ge(half_set, 3)

            def rstd_of(b):
                pool.wait_ge(var, b + 1)
                nc.gpsimd.tensor_tensor(rstd[:, :], var_eps[:, :], neg_half[:, :], ALU.pow).then_inc(rs, 1)

            def low_half(e, c, scaled_before):
                pool.wait_ge(raw_scaled[c], scaled_before + 1)
                nc.gpsimd.tensor_tensor(chunk(w1_lo, w2_lo, e, c), staged(c), chunk(w1_hi, w2_hi, e, c),
                                        ALU.subtract).then_inc(w_lo_done[c], 1)

            def step(i, u):
                if not (last(i) and u):
                    rstd_of(2 * i + u + 1)
                low_half(i, 2 * u + 1, i)

            nc.gpsimd.iota(iota_e, pattern=[[0, NT], [1, E]], base=-E, channel_multiplier=0,
                           allow_small_or_imprecise_dtypes=True).then_inc(iotas, 1)
            for table, pattern, base, by_partition in ((iota_j, [[P, NT]], 0, 0), (iota_i, [[1, NSLOT_T]], 0, 0),
                                                       (iota_r, [[1, P]], 0, 0), (iota_s, [[1, NSLOT_T]], 0, 0),
                                                       (tile_no, [[1, NT]], 1, 0), (iota_p, [[0, 1]], 0, 1)):
                nc.gpsimd.iota(table[:, :], pattern=pattern, base=base, channel_multiplier=by_partition,
                               allow_small_or_imprecise_dtypes=True).then_inc(iotas, 1)
            nc.gpsimd.memset(ones[:, :], 1.0).then_inc(iotas, 1)
            nc.gpsimd.memset(ahead[:, :], 1.0).then_inc(iotas, 1)
            pool.wait_ge(iotas, 9)
            nc.gpsimd.affine_select(out=ahead[:, :], in_=ahead[:, :], compare_op=ALU.is_gt, fill=0.0, base=0,
                                    pattern=[[1, P]], channel_multiplier=-1).then_inc(iotas, 1)
            rstd_of(0)
            batches(pool, step)
            with pool.Fori(E // 2, E - 1) as e:
                for c in range(W_CHUNKS):
                    low_half(e, c, e if c % 2 else e - E // 2)
            for u in range(2):
                pool.wait_ge(rows_stored[u], 16 * (B // 2))
            pool.wait_ge(slots_found, 2)
            for j in range(2):
                fetch_rows(j)
            for c in (0, 2):
                low_half(E - 1, c, E // 2 - 1)

        @block.tensor
        def _(pe):
            mm = nc.tensor.matmul
            pe.wait_ge(small_in, 48)
            nc.tensor.transpose(ps_rank[:, 0:E * F // P], b1_nat[:, :], ident[0:E * F // P, 0:E * F // P]).then_inc(b1_ps, 1)

            def normed(b):
                for t in range(QT):
                    pe.wait_ge(xh, QT * b + t + 1)
                    for k in range(KC):
                        done = nc.tensor.transpose(ps_xt[k][:, t * P:(t + 1) * P], xhat[:, t, k * P:(k + 1) * P], ident[:, :])
                done.then_inc(xt_ps, 1)

            def step(i, u):
                b = 2 * i + u
                pe.wait_ge(ht_done, KC * b + KC)
                for t in range(QT):
                    for k in range(KC):
                        at = (t % 2) * D + k * P
                        done = nc.tensor.transpose(ps_row[t // 2][:, at:at + P], h_t[:, u, k, t * P:(t + 1) * P], ident[:, :])
                    if t % 2:
                        done.then_inc(row_ps, 1)
                if not (last(i) and u):
                    normed(b + 1)
                ge(pe, logit_kept, b)
                for t in range(QT):
                    for k in range(KC):
                        done = mm(ps_logit[:, t * E:(t + 1) * E], h_t[:, u, k, t * P:(t + 1) * P], sw[:, k, :],
                                  start=(t == 0 and k == 0), stop=(k == KC - 1), skip_group_check=True)
                done.then_inc(logit_ps, 1)

            normed(0)
            batches(pe, step)
            pe.wait_ge(iotas, 10)
            pe.wait_ge(onehot_done, 1)
            pe.wait_ge(b1_kept, 1)
            flat = onehot.rearrange("p t e -> p (t e)")
            mm(ps_rank[:, 0:NT * E], ahead[:, :], flat, start=True, stop=True)
            mm(ps_rank[:, NT * E:2 * NT * E], ones[:, :], flat, start=False, stop=True, skip_group_check=True).then_inc(rank_ps, 1)
            pe.wait_ge(tables_done, 3)
            for T in range(NT):
                done = mm(ps_token[:, 0:2 * NSLOT_T], in_row[:, T, :], parts[:, T, :, :].rearrange("p a j -> p (a j)"),
                          start=(T == 0), stop=(T == NT - 1))
            done.then_inc(token_ps, 1)

        @block.scalar
        def _(act):
            act.wait_ge(b1_ps, 1)
            nc.scalar.activation(b1_t[:, :, :].rearrange("p e f -> p (e f)"), ps_rank[:, 0:E * F // P], ACT.Copy).then_inc(b1_kept, 1)

            def high_half(e, c, scale_raw):
                act.wait_ge(raw_loaded[c], 16 * e + 16)
                nc.scalar.activation(chunk(w1_hi, w2_hi, e, c), staged(c), ACT.Copy, scale=W_SCALE).then_inc(w_hi_done[c], 1)
                if scale_raw:
                    act.wait_ge(w_hi_done[c], e + 1)
                    nc.scalar.activation(staged(c), staged(c), ACT.Copy, scale=W_SCALE).then_inc(raw_scaled[c], 1)

            def step(i, u):
                b = 2 * i + u
                ge(act, rows_stored[u], 16 * i)
                for q in range(2):
                    act.wait_ge(row_ps, 2 * b + q + 1)
                    nc.scalar.activation(rows[:, u, 2 * q:2 * q + 2, 0:D], ps_row[q][:, :].rearrange("p (t d) -> p t d", t=2),
                                         ACT.Copy).then_inc(hi_done, 1)
                for c in (2 * u, 2 * u + 1):
                    high_half(i, c, c % 2 == 1)
                act.wait_ge(logit_ps, b + 1)
                nc.scalar.activation(logits[:, bass.ds(QT * b, QT), :].rearrange("p t e -> p (t e)"), ps_logit[:, 0:QT * E],
                                     ACT.Copy).then_inc(logit_kept, 1)

            batches(act, step)
            act.wait_ge(shifted_done, 1)
            nc.scalar.activation(tmp, shifted, ACT.Exp).then_inc(exp_done, 1)
            with act.Fori(E // 2, E - 1) as e:
                for c in range(W_CHUNKS):
                    high_half(e, c, True)
            for c in range(W_CHUNKS):
                high_half(E - 1, c, c % 2 == 0)

        @block.vector
        def _(dve):
            def statistics(b, par, load_count):
                dve.wait_ge(x1_loaded[par], load_count)
                for t in range(QT):
                    nc.vector.bn_stats(bn[:, t, :], x1[:, par, t, :]).then_inc(stats, 1)
                dve.wait_ge(stats, QT * b + QT)
                ge(dve, xh, QT * b)
                dve.sem_inc(turns, 1)
                for t in range(QT):
                    nc.vector.bn_aggr(mean_var[:, t, :], bn[:, t, :]).then_inc(mv, 1)
                dve.wait_ge(mv, QT * b + QT)
                nc.vector.tensor_scalar(var_eps[:, :], mean_var[:, :, 1], LN_EPS, None, ALU.add).then_inc(var, 1)

            def low_rows(b, par):
                for q in range(2):
                    dve.wait_ge(hi_done, 2 * b + q + 1)
                    pair = rows[:, par, 2 * q:2 * q + 2, :]
                    nc.vector.tensor_tensor(pair[:, :, D:2 * D], ps_row[q][:, :].rearrange("p (t d) -> p t d", t=2),
                                            pair[:, :, 0:D], ALU.subtract).then_inc(lo_done, 1)

            def low_half(e, c):
                dve.wait_ge(w_hi_done[c], e + 1)
                nc.vector.scalar_tensor_tensor(out=chunk(w1_lo, w2_lo, e, c), in0=staged(c), scalar=W_SCALE,
                                               in1=chunk(w1_hi, w2_hi, e, c), op0=ALU.mult,
                                               op1=ALU.subtract).then_inc(w_lo_done[c], 1)

            def step(i, u):
                b = 2 * i + u
                dve.wait_ge(rs, b + 1)
                for t in range(QT):
                    nc.vector.tensor_scalar(xhat[:, t, :], x1[:, u, t, :], mean_var[:, t, 0:1], rstd[:, t:t + 1],
                                            ALU.subtract, ALU.mult).then_inc(xh, 1)
                if not (last(i) and u):
                    statistics(b + 1, 1 - u, 16 * (i + (u + 1) // 2 + 1))
                if not isinstance(b, int) or b:
                    e, half = before(i, u)
                    low_half(e, 2 * half)
                    low_rows(b - 1, 1 - u)
                dve.wait_ge(xt_ps, b + 1)
                for k in range(KC):
                    nc.vector.tensor_scalar(h_t[:, u, k, :], ps_xt[k][:, :],
                                            mod_t[:, 4 * KC + k, bass.ds(b, 1)], mod_t[:, 3 * KC + k, bass.ds(b, 1)],
                                            ALU.mult, ALU.add).then_inc(ht_done, 1)

            statistics(0, 0, 16)
            dve.wait_ge(b2_split_in, 16)
            nc.vector.tensor_copy(b2_s[:, 0, :], b2_f[:, :]).then_inc(b2_split, 1)
            dve.wait_ge(b2_split, 1)
            nc.vector.tensor_tensor(b2_rest[:, :], b2_f[:, :], b2_s[:, 0, :], ALU.subtract).then_inc(b2_mid, 1)
            dve.wait_ge(b2_mid, 1)
            nc.vector.tensor_copy(b2_s[:, 1, :], b2_rest[:, :]).then_inc(b2_split, 1)
            dve.wait_ge(b2_split, 2)
            nc.vector.tensor_tensor(b2_f[:, :], b2_rest[:, :], b2_s[:, 1, :], ALU.subtract).then_inc(b2_mid, 1)
            dve.wait_ge(b2_mid, 2)
            nc.vector.tensor_copy(b2_s[:, 2, :], b2_f[:, :]).then_inc(b2_split, 1)
            batches(dve, step)
            low_rows(B - 1, 1)
            low_half(B // 2 - 1, 2)

            done = [0]

            def link(ins):
                done[0] += 1
                ins.then_inc(chain, 1)
                dve.wait_ge(chain, done[0])

            tt, ts, red = nc.vector.tensor_tensor, nc.vector.tensor_scalar, nc.vector.tensor_reduce
            dve.wait_ge(logit_kept, B)
            dve.wait_ge(small_in, 48)
            dve.wait_ge(iotas, 10)
            link(tt(logits[:, :, :], logits[:, :, :], sw_b[:, None, :].to_broadcast([P, NT, E]), ALU.add))
            link(red(top, logits[:, :, :], AX.X, ALU.max))
            top_b = top[:, :, None].to_broadcast([P, NT, E])
            tt(shifted, logits[:, :, :], top_b, ALU.subtract).then_inc(shifted_done, 1)
            link(tt(onehot, logits[:, :, :], top_b, ALU.is_equal))
            link(tt(cum_a, onehot, iota_e, ALU.mult))
            link(red(first, cum_a, AX.X, ALU.min))
            ins = tt(onehot, iota_e, first[:, :, None].to_broadcast([P, NT, E]), ALU.is_equal)
            ins.then_inc(onehot_done, 1)
            dve.wait_ge(exp_done, 1)
            link(red(denom, tmp, AX.X, ALU.add))
            link(nc.vector.reciprocal(prob_max, denom))
            ts(gate_p, prob_max, 1.0 / W_SCALE, None, ALU.mult).then_inc(gate_done, 1)
            dve.wait_ge(rank_ps, 1)
            link(nc.vector.tensor_copy(cum_a, ps_rank[:, NT * E:2 * NT * E].rearrange("p (t e) -> p t e", e=E)))
            link(nc.vector.tensor_copy(within, ps_rank[:, 0:NT * E].rearrange("p (t e) -> p t e", e=E)))
            link(tt(within, within, cum_a, ALU.subtract))
            a, b2_ = cum_a, cum_b
            step = 1
            while step < NT:
                nc.vector.tensor_copy(b2_[:, 0:step, :], a[:, 0:step, :]).then_inc(chain, 1)
                done[0] += 1
                link(tt(b2_[:, step:NT, :], a[:, step:NT, :], a[:, 0:NT - step, :], ALU.add))
                a, b2_ = b2_, a
                step *= 2
            link(tt(jcmp[:, :, :], iota_j[:, None, :].to_broadcast([P, E, NT]),
                    a[:, NT - 1, :, None].to_broadcast([P, E, NT]), ALU.is_lt))
            link(red(tiles_of, jcmp[:, :, :], AX.X, ALU.add))
            ta, tb = tiles_of, tiles_a
            step = 1
            while step < E:
                nc.vector.tensor_copy(tb[:, 0:step], ta[:, 0:step]).then_inc(chain, 1)
                done[0] += 1
                link(tt(tb[:, step:E], ta[:, step:E], ta[:, 0:E - step], ALU.add))
                ta, tb = tb, (tiles_b if ta is tiles_of else ta)
                step *= 2
            link(tt(start_of, ta, tiles_of, ALU.subtract))
            link(ts(start_of, start_of, float(P), None, ALU.mult))
            link(tt(ecmp[:, :, :], iota_i[:, :, None].to_broadcast([P, NSLOT_T, E]), ta[:, None, :].to_broadcast([P, NSLOT_T, E]), ALU.is_ge))
            link(red(expert_f, ecmp[:, :, :], AX.X, ALU.add))
            link(ts(tile_e[:, :], expert_f, float(E - 1), None, ALU.min))
            link(tt(within, within, a, ALU.add))
            link(tt(within, within, start_of[:, None, :].to_broadcast([P, NT, E]), ALU.add))
            link(tt(within, within, onehot, ALU.mult))
            link(red(slot_f, within, AX.X, ALU.add))
            link(ts(slot_tile, slot_f, 1.0 / P, 0.5 / P - 0.5, ALU.mult, ALU.add))
            link(ts(slot_tile, slot_tile, ROUND, None, ALU.add))
            link(ts(slot_tile, slot_tile, -ROUND, None, ALU.add))
            link(nc.vector.scalar_tensor_tensor(out=slot_row, in0=slot_tile, scalar=-float(P), in1=slot_f,
                                                op0=ALU.mult, op1=ALU.add))
            tt(in_row, slot_row[:, :, None].to_broadcast([P, NT, P]), iota_r[:, None, :].to_broadcast([P, NT, P]),
               ALU.is_equal).then_inc(tables_done, 1)
            link(tt(in_tile, slot_tile[:, :, None].to_broadcast([P, NT, NSLOT_T]),
                    iota_s[:, None, :].to_broadcast([P, NT, NSLOT_T]), ALU.is_equal))
            tt(parts[:, :, 0, :], in_tile, tile_no[:, :, None].to_broadcast([P, NT, NSLOT_T]), ALU.mult).then_inc(tables_done, 1)
            ts(parts[:, :, 1, :], in_tile, iota_p[:, :], None, ALU.mult).then_inc(tables_done, 1)
            dve.wait_ge(token_ps, 1)
            link(ts(empty, ps_token[:, 0:NSLOT_T], 0.0, float(2 * NT * P), ALU.is_equal, ALU.mult))
            link(nc.vector.scalar_tensor_tensor(out=token_f, in0=ps_token[:, 0:NSLOT_T], scalar=float(P), in1=empty,
                                                op0=ALU.mult, op1=ALU.add))
            link(tt(token_f, token_f, ps_token[:, NSLOT_T:2 * NSLOT_T], ALU.add))
            ts(token[:, :], token_f, -float(P), None, ALU.add).then_inc(slots_found, 1)
            link(ts(batch_f, ps_token[:, 0:NSLOT_T], 1.0 / QT, -1.0 / QT - (QT - 1) / (2 * QT), ALU.mult, ALU.add))
            link(ts(batch_f, batch_f, ROUND, None, ALU.add))
            ts(gate_row[:, :], batch_f, float(B) - ROUND, None, ALU.add).then_inc(slots_found, 1)
            for c in (1, 3):
                low_half(E - 1, c)


def expert_part(nc, sem, ident16, w1_hi, w1_lo, w2_hi, w2_lo, b1_t, b2_parts, token, tile_e,
                rows, slot_x1, slot_gate, of_slots, fetch_rows, fetch_x1, out):
    with ExitStack() as ctx:
        def sb(name, shape, dt=F32):
            return ctx.enter_context(nc.sbuf_tensor(name, shape, dt))

        def bank(name):
            return ctx.enter_context(nc.psum_tensor(name, [P, 512], F32))

        FC = F // P
        tok_t = sb("tok_t", [P, 2, 2, KC, P], F16)
        hid = sb("hid", [P, 2, FC, P])
        hid_hi = sb("hid_hi", [P, 2, FC, P], F16)
        hid_lo = sb("hid_lo", [P, 2, FC, P], F16)
        y = sb("y", [P, 2, D])
        scale3 = sb("scale3", [3, P], BF16)
        ps_x = bank("ps_x")
        ps_h = [[bank(f"ps_h{a}{b}") for b in range(2)] for a in range(2)]
        ps_y = [bank("ps_y0"), bank("ps_y1")]

        rows_loaded = [sem("rows_loaded0"), sem("rows_loaded1")]
        scale_done = sem("scale_done")
        x_ps, x_kept, h_ps, gelu_done = sem("f_x_ps"), sem("f_x_kept"), sem("f_h_ps"), sem("f_gelu")
        hi_done, lo_done, y_ps, y_kept = sem("f_hi"), sem("f_lo"), sem("f_y_ps"), sem("f_y_kept")
        y_stored = [sem("y_stored0"), sem("y_stored1")]
        x1_fetched = [sem("x1_fetched0"), sem("x1_fetched1")]
        gate_fetched = [sem("gate_fetched0"), sem("gate_fetched1")]
        gated = sem("l_gated")

        out_rows = out.rearrange("b s d -> (b s) d")
        NJ = NSLOT_T - 1

        block = ctx.enter_context(nc.Block())

        def steps(eng, step):
            step(0, 0, first=True)
            with eng.Fori(0, (NJ - 1) // 2) as i:
                for u in range(2):
                    step(2 * i + u + 1, (u + 1) % 2)

        @block.gpsimd
        def _(pool):
            nc.gpsimd.memset(scale3[:, :], W_SCALE).then_inc(scale_done, 1)

            def store_y(j):
                pool.wait_ge(y_kept, j + 1)
                nc.gpsimd.indirect_dma_start(out_rows, of_slots(token, j), y[:, j % 2, :], None, bounds_check=NT * P - 1,
                                             oob_is_err=False).then_inc(y_stored[j % 2], 16)

            for j in range(2):
                fetch_x1(j)
            for j in range(2, NSLOT_T):
                pool.wait_ge(x_ps, j - 1)
                fetch_rows(j)
                if j >= 3:
                    store_y(j - 3)
                    fetch_x1(j - 1)
            for j in range(NJ - 2, NJ):
                store_y(j)
            pool.wait_ge(y_stored[0], 16 * ((NJ + 1) // 2))
            pool.wait_ge(y_stored[1], 16 * (NJ // 2))

        @block.tensor
        def _(pe):
            mm = nc.tensor.matmul

            def transposes(j, half, load_count):
                pe.wait_ge(rows_loaded[half], load_count)
                ge(pe, x_kept, j)
                for n in range(2 * KC):
                    last = nc.tensor.transpose(ps_x[:, :].bitcast(F16)[:, n * P:(n + 1) * P],
                                               rows[:, half, n * P:(n + 1) * P], ident16[:, :])
                last.then_inc(x_ps, 1)

            def product1(j, half, e, q):
                if q == 0:
                    pe.wait_ge(x_kept, j + 1)
                for q in (q,):
                    for f in range(q * FC // 2, (q + 1) * FC // 2):
                        o = ps_h[half][q][:, (f % (FC // 2)) * P:(f % (FC // 2) + 1) * P]
                        n = 0
                        for k in range(KC):
                            for w, parts in ((w1_hi, (0, 1)), (w1_lo, (0,))):
                                for part in parts:
                                    last = mm(o, w[:, bass.ds(e, 1), k, f * P:(f + 1) * P].rearrange("p e f -> p (e f)"), tok_t[:, half, part, k, :],
                                              start=(n == 0 and f % (FC // 2) == 0), stop=(n == 3 * KC - 1),
                                              skip_group_check=True)
                                    n += 1
                    last.then_inc(h_ps, 1)

            def product2(j, half, e):
                pe.wait_ge(hi_done, 2 * j + 2)
                pe.wait_ge(lo_done, 2 * j + 2)
                mm(ps_y[half][:, 0:D], scale3[:, :], b2_parts[:, bass.ds(e * D, D)], start=True, stop=False)
                for f in range(FC):
                    for a, w in ((hid_hi, w2_hi), (hid_lo, w2_hi), (hid_hi, w2_lo)):
                        last = mm(ps_y[half][:, 0:D], a[:, half, f, :], w[:, bass.ds(e, 1), f, :].rearrange("p e d -> p (e d)"),
                                  start=False, stop=(f == FC - 1 and w is w2_lo))
                last.then_inc(y_ps, 1)

            pe.wait_ge(scale_done, 1)
            transposes(0, 0, 16)
            e0 = pe.value_load(tile_e[0:1, 0:1], min_val=0, max_val=E - 1)
            product1(0, 0, e0, 0)
            transposes(1, 1, 16)
            product1(0, 0, e0, 1)

            def steps_of(i, count):
                _, e = nc.values_load_multi_w_load_instructions(tile_e[0:1, bass.ds(UNROLL * i, count + 1)],
                                                                engines=[mybir.EngineType.PE], min_val=0, max_val=E - 1)
                for u in range(count):
                    j, half = UNROLL * i + u + 1, (u + 1) % 2
                    product1(j, half, e[u + 1], 0)
                    transposes(j + 1, 1 - half, 16 * (UNROLL // 2 * i + (u + 2) // 2 + 1))
                    product1(j, half, e[u + 1], 1)
                    product2(j - 1, 1 - half, e[u])

            UNROLL = 8
            with pe.Fori(0, (NJ - 1) // UNROLL) as i:
                steps_of(i, UNROLL)
            if (NJ - 1) % UNROLL:
                steps_of((NJ - 1) // UNROLL, (NJ - 1) % UNROLL)
            e = pe.value_load(tile_e[0:1, NJ - 1:NJ], min_val=0, max_val=E - 1)
            product2(NJ - 1, 0, e)

        @block.scalar
        def _(act):
            def keep_x(j, half):
                act.wait_ge(x_ps, j + 1)
                nc.scalar.activation(tok_t[:, half, :, :, :].rearrange("p a k m -> p (a k m)"),
                                     ps_x[:, :].bitcast(F16)[:, 0:2 * KC * P], ACT.Copy).then_inc(x_kept, 1)

            def gelu(j, half, e):
                for f in range(FC):
                    q = f // (FC // 2)
                    if f % (FC // 2) == 0:
                        act.wait_ge(h_ps, 2 * j + q + 1)
                    ins = nc.scalar.activation(hid[:, half, f, :], ps_h[half][q][:, (f % (FC // 2)) * P:(f % (FC // 2) + 1) * P],
                                               ACT.Gelu_apprx_tanh, bias=b1_t[:, bass.ds(e, 1), f], scale=1.0 / W_SCALE)
                    if f % (FC // 2) == FC // 2 - 1:
                        ins.then_inc(gelu_done, 1)

            keep_x(0, 0)
            e0 = act.value_load(tile_e[0:1, 0:1], min_val=0, max_val=E - 1)
            keep_x(1, 1)
            gelu(0, 0, e0)
            with act.Fori(0, (NJ - 1) // 2) as i:
                for u in range(2):
                    j = 2 * i + u + 1
                    e = act.value_load(tile_e[0:1, bass.ds(j, 1)], min_val=0, max_val=E - 1)
                    keep_x(j + 1, u)
                    gelu(j, (u + 1) % 2, e)

        @block.vector
        def _(dve):
            def halves(j, half):
                for q in range(2):
                    dve.wait_ge(gelu_done, 2 * j + q + 1)
                    sl = slice(q * FC // 2, (q + 1) * FC // 2)
                    nc.vector.tensor_copy(hid_hi[:, half, sl, :], hid[:, half, sl, :]).then_inc(hi_done, 1)
                    dve.wait_ge(hi_done, 2 * j + q + 1)
                    nc.vector.tensor_tensor(hid_lo[:, half, sl, :], hid[:, half, sl, :], hid_hi[:, half, sl, :],
                                            ALU.subtract).then_inc(lo_done, 1)

            def keep_y(j, half, fetched):
                dve.wait_ge(y_ps, j + 1)
                dve.wait_ge(x1_fetched[half], fetched)
                dve.wait_ge(gate_fetched[half], fetched)
                nc.vector.scalar_tensor_tensor(out=y[:, half, :], in0=ps_y[half][:, 0:D], scalar=slot_x1[:, half, D:D + 1],
                                               in1=slot_gate[:, half, :], op0=ALU.mult, op1=ALU.mult).then_inc(gated, 1)
                dve.wait_ge(gated, j + 1)
                nc.vector.tensor_tensor(y[:, half, :], y[:, half, :], slot_x1[:, half, 0:D], ALU.add).then_inc(y_kept, 1)

            halves(0, 0)
            halves(1, 1)
            keep_y(0, 0, 16)
            halves(2, 0)
            keep_y(1, 1, 16)
            with dve.Fori(1, (NJ - 1) // 2) as i:
                for u in range(2):
                    j = 2 * i + u + 1
                    halves(j, (u + 1) % 2)
                    dve.wait_ge(y_stored[u], 16 * i)
                    keep_y(j - 1, u, 16 * i + 16)
            dve.wait_ge(y_stored[0], 16 * ((NJ - 1) // 2))
            keep_y(NJ - 1, 0, 16 * ((NJ + 1) // 2))


_INS = {"x": "L0_attn_x", "wq": "L0_attn_Wq", "bq": "L0_attn_bq", "wk": "L0_attn_Wk", "bk": "L0_attn_bk",
        "wv": "L0_attn_Wv", "bv": "L0_attn_bv", "wo": "L0_attn_Wo", "bo": "L0_attn_bo",
        "switch_w": "L0_ffn_switch_w", "switch_b": "L0_ffn_switch_b", "w1": "L0_ffn_w1", "b1": "L0_ffn_b1",
        "w2": "L0_ffn_w2", "b2": "L0_ffn_b2", "c": "L0_c", "wmod": "L0_wmod"}


def rope_tables():
    import numpy as np

    inv_freq = np.float32(1.0) / np.float32(10000.0) ** (np.arange(0, DK, 2, dtype=np.float32) / np.float32(DK))
    angles = (np.arange(S, dtype=np.float32)[:, None] * inv_freq.astype(np.float32)).astype(np.float64)
    sign = np.where(np.arange(DK) % 2 == 0, -1.0, 1.0)
    return (np.repeat(np.cos(angles), 2, axis=1).astype(np.float32),
            (np.repeat(np.sin(angles), 2, axis=1) * sign).astype(np.float32))


def kernel(**inputs):
    import numpy as np
    import concourse.bacc as bacc
    from concourse.bass_utils import run_bass_kernel_spmd

    nc = bacc.Bacc("TRN2", target_bir_lowering=False, num_devices=1)
    arrays = {name: np.ascontiguousarray(inputs[given]) for name, given in _INS.items()}
    arrays["rope_cos"], arrays["rope_sin"] = rope_tables()
    args = [nc.dram_tensor(name, a.shape, mybir.dt.from_np(a.dtype), kind="ExternalInput").ap()
            for name, a in arrays.items()]
    out = nc.dram_tensor("out", (B, S, D), F32, kind="ExternalOutput").ap()
    build(nc, *args, out)
    r = run_bass_kernel_spmd(nc, [arrays], core_ids=[0])
    return r.results[0]["out"]
```
